# Optimizing a Trainium2 kernel written in Bass

```python
import numpy as np
import jax
import jax.numpy as jnp

def _softmax(x, axis=-1):
    return jax.nn.softmax(x, axis=axis)

def _gelu(x):
    return jax.nn.gelu(x, approximate=True)

def _silu(x):
    return jax.nn.silu(x)

def _sigmoid(x):
    return jax.nn.sigmoid(x)

def _layernorm(x, axis=-1, eps=1e-05):
    m = jnp.mean(x, axis=axis, keepdims=True)
    v = jnp.var(x, axis=axis, keepdims=True)
    return (x - m) / jnp.sqrt(v + eps)

def _scatter_add(tgt, idx, src, axis=0):
    return tgt.at[idx].add(src)

def _segment_sum(src, seg, n):
    return jax.ops.segment_sum(src, seg, n)
kernel_name = 'mk_adaln_ffn_d4_seqx_r8_df92a4'

def setup_inputs(seed: int=0):
    np.random.seed(seed)
    _w = jnp.asarray

    def _rec_inputs():
        import jax
        import jax.numpy as jnp
        _rk = jax.random.key(seed)
        x = -0.000125 + 0.9999 * jax.random.normal(jax.random.fold_in(_rk, 1), (128, 32, 128), jnp.float32)
        _lenS = 32 - jax.random.randint(jax.random.fold_in(_rk, 7), (128,), 0, max(1, 32 // 4) + 1, jnp.int32)
        _lenS2 = 32 - jax.random.randint(jax.random.fold_in(_rk, 8), (128,), 0, max(1, 32 // 4) + 1, jnp.int32)
        cond_1024 = 0.00782532 + 1.00527 * jax.random.normal(jax.random.fold_in(_rk, 11), (128, 128), jnp.float32)
        return (x, cond_1024)
    x, cond_1024 = _rec_inputs()

    def _L0_cond_setup():
        import jax, jax.numpy as jnp
        import numpy as np
        INV_SQRT2 = 0.7071067811865476
        key = jax.random.key(seed)
        k1, k2, k3, k4 = jax.random.split(key, 4)
        B, N, d = (8, 512, 128)
        scale = 1.0 / np.sqrt(d)
        return {'v': jax.random.normal(k1, (B, N, d), dtype=jnp.float32), 'q_pool': jax.random.normal(k2, (B, d), dtype=jnp.float32), 'W1': jax.random.normal(k3, (d, d), dtype=jnp.float32) * scale, 'b1': jnp.zeros((d,), dtype=jnp.float32), 'W2': jax.random.normal(k4, (d, d), dtype=jnp.float32) * scale, 'b2': jnp.zeros((d,), dtype=jnp.float32)}
    _L0_cond_all = _L0_cond_setup()
    _L0_cond_in = {k: v for k, v in _L0_cond_all.items() if k in ('W1', 'b1', 'W2', 'b2')}
    del _L0_cond_all

    def _L0_ffn_setup():
        import jax, jax.numpy as jnp
        import numpy as np
        EPS = 1e-06
        TOP_K = 2

        def rms_norm(x, scale, eps=EPS):
            xf = x.astype(jnp.float32)
            mean_sq = jnp.mean(xf * xf, axis=-1, keepdims=True)
            return (xf * (scale.astype(jnp.float32) * jax.lax.rsqrt(mean_sq + eps))).astype(x.dtype)
        key = jax.random.key(seed)
        k0, k1, k2, k3 = jax.random.split(key, 4)
        B, S, D, H, E = (2, 256, 128, 352, 8)
        x = jax.random.normal(k0, (B, S, D), dtype=jnp.float32)
        norm_scale = jnp.ones((D,), dtype=jnp.float32)
        w_router = jax.random.normal(k1, (E, D), dtype=jnp.float32) * 0.02
        w_up = jax.random.normal(k2, (E, 2 * H, D), dtype=jnp.float32) * 0.02
        w_down = jax.random.normal(k3, (E, D, H), dtype=jnp.float32) * 0.02
        return {'x': x, 'norm_scale': norm_scale, 'w_router': w_router, 'w_up': w_up, 'w_down': w_down}
    _L0_ffn_all = _L0_ffn_setup()
    _L0_ffn_in = {k: v for k, v in _L0_ffn_all.items() if k in ('norm_scale', 'w_router', 'w_up', 'w_down')}
    del _L0_ffn_all

    def _L1_cond_setup():
        import jax, jax.numpy as jnp
        import numpy as np
        import math
        N, T, D, H = (64, 64, 128, 128)
        key = jax.random.key(seed)
        k1, k2, k3, k4 = jax.random.split(key, 4)
        x = jax.random.normal(k1, (N, T, D), dtype=jnp.float32)
        h0 = jax.random.normal(k2, (N, H), dtype=jnp.float32)
        Wx = jax.random.normal(k3, (D, 4 * H), dtype=jnp.float32) / math.sqrt(D)
        Wh = jax.random.normal(k4, (H, 4 * H), dtype=jnp.float32) / math.sqrt(H)
        b = jnp.zeros((4 * H,), dtype=jnp.float32)
        return {'x': x, 'h0': h0, 'Wx': Wx, 'Wh': Wh, 'b': b}
    _L1_cond_all = _L1_cond_setup()
    _L1_cond_in = {k: v for k, v in _L1_cond_all.items() if k in ('Wx', 'Wh', 'b')}
    del _L1_cond_all

    def _L1_ffn_setup():
        import jax, jax.numpy as jnp
        import numpy as np
        BLOCK = 32
        W_BITS = 4
        ACT_BITS = 16

        def act_qdq(x):
            qmax = 2.0 ** (ACT_BITS - 1) - 1.0
            scale = jnp.maximum(jnp.max(jnp.abs(x)) / qmax, 1e-12)
            return jnp.clip(jnp.round(x / scale), -qmax - 1.0, qmax) * scale

        def fixed_qdq_u16(x):
            scale = 1.0 / 65536.0
            return jnp.clip(jnp.round(x / scale), 0.0, 65535.0) * scale

        def lpbq_dequant(w):
            O, I = w.shape
            qmax = 2.0 ** (W_BITS - 1) - 1.0
            wb = w.reshape(O, I // BLOCK, BLOCK)
            s = jnp.maximum(jnp.max(jnp.abs(wb), axis=-1, keepdims=True) / qmax, 1e-12)
            wq = jnp.clip(jnp.round(wb / s), -qmax - 1.0, qmax) * s
            return wq.reshape(O, I)
        key = jax.random.key(seed)
        k1, k2, k3, k4 = jax.random.split(key, 4)
        B, S, H, I = (2, 512, 128, 384)
        x = jax.random.normal(k1, (B, S, H), jnp.float32)
        w_gate = jax.random.normal(k2, (I, H), jnp.float32) * 0.02
        w_up = jax.random.normal(k3, (I, H), jnp.float32) * 0.02
        w_down = jax.random.normal(k4, (H, I), jnp.float32) * 0.02
        return {'x': x, 'w_gate': w_gate, 'w_up': w_up, 'w_down': w_down}
    _L1_ffn_all = _L1_ffn_setup()
    _L1_ffn_in = {k: v for k, v in _L1_ffn_all.items() if k in ('w_gate', 'w_up', 'w_down')}
    del _L1_ffn_all

    def _L2_cond_setup():
        import jax, jax.numpy as jnp
        import numpy as np
        IN_FEATURES = 128
        OUT_FEATURES = 128
        BATCH = 32
        SEQ = 128
        EPS = 1e-08
        key = jax.random.key(seed)
        k1, k2, k3 = jax.random.split(key, 3)
        Efou = jax.random.normal(k1, (BATCH, SEQ, IN_FEATURES), dtype=jnp.float32)
        y = jax.random.normal(k2, (BATCH, IN_FEATURES), dtype=jnp.float32)
        weight = jax.random.normal(k3, (IN_FEATURES, OUT_FEATURES), dtype=jnp.float32)
        return {'Efou': Efou, 'y': y, 'weight': weight}
    _L2_cond_all = _L2_cond_setup()
    _L2_cond_in = {k: v for k, v in _L2_cond_all.items() if k in ('weight',)}
    del _L2_cond_all

    def _L2_ffn_setup():
        import jax, jax.numpy as jnp
        import numpy as np
        INT8_MAX = 127.0

        def _absmax_scale(x, axes):
            amax = jnp.max(jnp.abs(x), axis=axes, keepdims=True)
            return jnp.maximum(amax, 1e-12) / INT8_MAX
        key = jax.random.key(seed)
        k1, k2 = jax.random.split(key)
        lhs = jax.random.normal(k1, (4, 1024, 128), dtype=jnp.float32)
        rhs = jax.random.normal(k2, (128, 128), dtype=jnp.float32)
        return {'lhs': lhs, 'rhs': rhs}
    _L2_ffn_all = _L2_ffn_setup()
    _L2_ffn_in = {k: v for k, v in _L2_ffn_all.items() if k in ('rhs',)}
    del _L2_ffn_all

    def _L3_cond_setup():
        import jax, jax.numpy as jnp
        import numpy as np
        LATENT = 128
        key = jax.random.key(seed)
        k1, k2, k3, k4 = jax.random.split(key, 4)
        B, T, D = (64, 64, LATENT)
        h_t = jax.random.normal(k1, (B, D), dtype=jnp.float32)
        z = jax.random.normal(k2, (B, T, D), dtype=jnp.float32)
        bound = 1.0 / np.sqrt(2 * D)
        W = jax.random.uniform(k3, (D, 2 * D), minval=-bound, maxval=bound, dtype=jnp.float32)
        b = jax.random.uniform(k4, (D,), minval=-bound, maxval=bound, dtype=jnp.float32)
        alpha = jnp.full((D,), 0.1, dtype=jnp.float32)
        return {'h_t': h_t, 'z': z, 'W': W, 'b': b, 'alpha': alpha}
    _L3_cond_all = _L3_cond_setup()
    _L3_cond_in = {k: v for k, v in _L3_cond_all.items() if k in ('W', 'b', 'alpha')}
    del _L3_cond_all

    def _L3_ffn_setup():
        import jax, jax.numpy as jnp
        import numpy as np
        B, C, D = (2, 256, 128)
        I = 256
        E, K = (8, 2)
        CF = 1.25
        key = jax.random.key(seed)
        k1, k2, k3, k4 = jax.random.split(key, 4)
        scale = 0.02
        return {'hidden_states': jax.random.normal(k1, (B, C, D), jnp.float32), 'Wg': jax.random.normal(k2, (E, D), jnp.float32) * scale, 'W1': jax.random.normal(k3, (E, D, 2 * I), jnp.float32) * scale, 'W2': jax.random.normal(k4, (E, I, D), jnp.float32) * scale}
    _L3_ffn_all = _L3_ffn_setup()
    _L3_ffn_in = {k: v for k, v in _L3_ffn_all.items() if k in ('Wg', 'W1', 'W2')}
    del _L3_ffn_all
    return {'x': x, 'cond_1024': cond_1024, 'L0_cond_W1': _L0_cond_in['W1'], 'L0_cond_b1': _L0_cond_in['b1'], 'L0_cond_W2': _L0_cond_in['W2'], 'L0_cond_b2': _L0_cond_in['b2'], 'L0_ffn_norm_scale': _L0_ffn_in['norm_scale'], 'L0_ffn_w_router': _L0_ffn_in['w_router'], 'L0_ffn_w_up': _L0_ffn_in['w_up'], 'L0_ffn_w_down': _L0_ffn_in['w_down'], 'L1_cond_Wx': _L1_cond_in['Wx'], 'L1_cond_Wh': _L1_cond_in['Wh'], 'L1_cond_b': _L1_cond_in['b'], 'L1_ffn_w_gate': _L1_ffn_in['w_gate'], 'L1_ffn_w_up': _L1_ffn_in['w_up'], 'L1_ffn_w_down': _L1_ffn_in['w_down'], 'L2_cond_weight': _L2_cond_in['weight'], 'L2_ffn_rhs': _L2_ffn_in['rhs'], 'L3_cond_W': _L3_cond_in['W'], 'L3_cond_b': _L3_cond_in['b'], 'L3_cond_alpha': _L3_cond_in['alpha'], 'L3_ffn_Wg': _L3_ffn_in['Wg'], 'L3_ffn_W1': _L3_ffn_in['W1'], 'L3_ffn_W2': _L3_ffn_in['W2']}

def reference(x, cond_1024, L0_cond_W1, L0_cond_b1, L0_cond_W2, L0_cond_b2, L0_ffn_norm_scale, L0_ffn_w_router, L0_ffn_w_up, L0_ffn_w_down, L1_cond_Wx, L1_cond_Wh, L1_cond_b, L1_ffn_w_gate, L1_ffn_w_up, L1_ffn_w_down, L2_cond_weight, L2_ffn_rhs, L3_cond_W, L3_cond_b, L3_cond_alpha, L3_ffn_Wg, L3_ffn_W1, L3_ffn_W2):
    import jax
    import jax.numpy as jnp

    def _L0_cond_ref(v, q_pool, W1, b1, W2, b2):
        import jax, jax.numpy as jnp
        import numpy as np
        INV_SQRT2 = 0.7071067811865476
        B, N, d = v.shape
        h = jax.nn.silu(q_pool @ W1.T + b1)
        gate = jax.nn.sigmoid(h @ W2.T + b2)[:, None, :]
        levels = int(np.log2(N))
        a = v
        details = []
        for _ in range(levels):
            e, o = (a[:, 0::2], a[:, 1::2])
            details.append((e - o) * INV_SQRT2)
            a = (e + o) * INV_SQRT2
        a = a * gate
        for dc in reversed(details):
            dc = dc * gate
            e = (a + dc) * INV_SQRT2
            o = (a - dc) * INV_SQRT2
            n = e.shape[1]
            a = jnp.stack([e, o], axis=2).reshape(B, 2 * n, d)
        return v + a

    def _L0_ffn_ref(x, norm_scale, w_router, w_up, w_down):
        import jax, jax.numpy as jnp
        import numpy as np
        EPS = 1e-06
        TOP_K = 2

        def rms_norm(x, scale, eps=EPS):
            xf = x.astype(jnp.float32)
            mean_sq = jnp.mean(xf * xf, axis=-1, keepdims=True)
            return (xf * (scale.astype(jnp.float32) * jax.lax.rsqrt(mean_sq + eps))).astype(x.dtype)
        skip = x
        xn = rms_norm(x, norm_scale)
        scores = jnp.einsum('bsd,ed->bse', xn, w_router)
        _, ids = jax.lax.top_k(scores, TOP_K)
        probs = jax.nn.softmax(scores, axis=-1)
        c = jnp.take_along_axis(probs, ids, axis=-1)
        h = jnp.einsum('bsd,ehd->bseh', xn, w_up)
        val, gate = jnp.split(h, 2, axis=-1)
        h = val * jax.nn.silu(gate)
        y = jnp.einsum('bseh,edh->bsed', h, w_down)
        yk = jnp.take_along_axis(y, ids[..., None], axis=2)
        out = jnp.sum(yk * c[..., None], axis=2)
        return out + skip

    def _L1_cond_ref(x, h0, Wx, Wh, b):
        import jax, jax.numpy as jnp
        import numpy as np
        import math
        N, T, D, H = (64, 64, 128, 128)
        Hdim = h0.shape[1]
        c0 = jnp.zeros_like(h0)
        xW = jnp.einsum('ntd,dk->tnk', x, Wx) + b

        def step(carry, xw_t):
            prev_h, prev_c = carry
            a = xw_t + prev_h @ Wh
            i = jax.nn.sigmoid(a[:, :Hdim])
            f = jax.nn.sigmoid(a[:, Hdim:2 * Hdim])
            o = jax.nn.sigmoid(a[:, 2 * Hdim:3 * Hdim])
            g = jnp.tanh(a[:, 3 * Hdim:])
            next_c = f * prev_c + i * g
            next_h = o * jnp.tanh(next_c)
            return ((next_h, next_c), next_h)
        _, hs = jax.lax.scan(step, (h0, c0), xW)
        return jnp.transpose(hs, (1, 0, 2))

    def _L1_ffn_ref(x, w_gate, w_up, w_down):
        import jax, jax.numpy as jnp
        import numpy as np
        BLOCK = 32
        W_BITS = 4
        ACT_BITS = 16

        def act_qdq(x):
            qmax = 2.0 ** (ACT_BITS - 1) - 1.0
            scale = jnp.maximum(jnp.max(jnp.abs(x)) / qmax, 1e-12)
            return jnp.clip(jnp.round(x / scale), -qmax - 1.0, qmax) * scale

        def fixed_qdq_u16(x):
            scale = 1.0 / 65536.0
            return jnp.clip(jnp.round(x / scale), 0.0, 65535.0) * scale

        def lpbq_dequant(w):
            O, I = w.shape
            qmax = 2.0 ** (W_BITS - 1) - 1.0
            wb = w.reshape(O, I // BLOCK, BLOCK)
            s = jnp.maximum(jnp.max(jnp.abs(wb), axis=-1, keepdims=True) / qmax, 1e-12)
            wq = jnp.clip(jnp.round(wb / s), -qmax - 1.0, qmax) * s
            return wq.reshape(O, I)
        x = act_qdq(x)
        up = act_qdq(x @ lpbq_dequant(w_up).T)
        gate = act_qdq(x @ lpbq_dequant(w_gate).T)
        sig = fixed_qdq_u16(jax.nn.sigmoid(gate))
        gate = act_qdq(gate * sig)
        o = act_qdq(gate * up)
        return o @ lpbq_dequant(w_down).T

    def _L2_cond_ref(Efou, y, weight):
        import jax, jax.numpy as jnp
        import numpy as np
        IN_FEATURES = 128
        OUT_FEATURES = 128
        BATCH = 32
        SEQ = 128
        EPS = 1e-08
        scale = 1.0 / np.sqrt(np.float32(weight.shape[0]))
        ys = y * scale
        d = jax.lax.rsqrt(jnp.einsum('bi,io->bo', ys * ys, weight * weight) + EPS)
        out = jnp.einsum('bsi,io->bso', Efou * ys[:, None, :], weight) * d[:, None, :]
        return out

    def _L2_ffn_ref(lhs, rhs):
        import jax, jax.numpy as jnp
        import numpy as np
        INT8_MAX = 127.0

        def _absmax_scale(x, axes):
            amax = jnp.max(jnp.abs(x), axis=axes, keepdims=True)
            return jnp.maximum(amax, 1e-12) / INT8_MAX
        lhs_scale = _absmax_scale(lhs, (2,))
        rhs_scale = _absmax_scale(rhs, (0,))
        q_lhs = jnp.clip(jnp.round(lhs / lhs_scale), -INT8_MAX, INT8_MAX).astype(jnp.int8)
        q_rhs = jnp.clip(jnp.round(rhs / rhs_scale), -INT8_MAX, INT8_MAX).astype(jnp.int8)
        acc = jax.lax.dot_general(q_lhs, q_rhs, (((2,), (0,)), ((), ())), preferred_element_type=jnp.int32)
        return acc.astype(jnp.float32) * lhs_scale * rhs_scale

    def _L3_cond_ref(h_t, z, W, b, alpha):
        import jax, jax.numpy as jnp
        import numpy as np
        LATENT = 128
        D = h_t.shape[-1]
        Wh = W[:, :D]
        Wz = W[:, D:]
        leak = 1.0 - alpha

        def step(h, z_t):
            gate = jax.nn.sigmoid(h @ Wh.T + z_t @ Wz.T + b)
            h_new = jnp.tanh(h * leak + gate * z_t)
            return (h_new, h_new)
        _, hs = jax.lax.scan(step, h_t, jnp.swapaxes(z, 0, 1))
        return jnp.swapaxes(hs, 0, 1)

    def _L3_ffn_ref(hidden_states, Wg, W1, W2):
        import jax, jax.numpy as jnp
        import numpy as np
        B, C, D = (2, 256, 128)
        I = 256
        E, K = (8, 2)
        CF = 1.25
        Bx, Cx, d = hidden_states.shape
        N = Bx * Cx
        cap = int(N * K * CF / E)
        x = hidden_states.reshape(N, d)
        logits = x @ Wg.T
        top_v, top_i = jax.lax.top_k(logits, K)
        gates = jax.nn.softmax(top_v, axis=-1)
        flat_e = top_i.reshape(N * K)
        gates_f = gates.reshape(N * K)
        tok = jnp.repeat(jnp.arange(N), K)
        onehot = jax.nn.one_hot(flat_e, E, dtype=jnp.int32)
        pos = jnp.cumsum(onehot, axis=0) - 1
        pos_f = jnp.take_along_axis(pos, flat_e[:, None], axis=1)[:, 0]
        keep = pos_f < cap
        pos_safe = jnp.where(keep, pos_f, cap)
        exp_batches = jnp.zeros((E, cap, d), x.dtype).at[flat_e, pos_safe].set(x[tok], mode='drop')
        h = jnp.einsum('ecd,edf->ecf', exp_batches, W1)
        inp, gate = jnp.split(h, 2, axis=-1)
        h = jax.nn.gelu(inp, approximate=False) * gate
        exp_out = jnp.einsum('eci,eid->ecd', h, W2)
        gathered = exp_out[flat_e, jnp.minimum(pos_safe, cap - 1)]
        contrib = jnp.where(keep, gates_f, 0.0)[:, None] * gathered
        out = jax.ops.segment_sum(contrib, tok, num_segments=N)
        return out.reshape(Bx, Cx, d)
    x = x + _L0_ffn_ref(_L0_cond_ref(x, cond_1024, L0_cond_W1, L0_cond_b1, L0_cond_W2, L0_cond_b2), L0_ffn_norm_scale, L0_ffn_w_router, L0_ffn_w_up, L0_ffn_w_down)
    x = x + _L1_ffn_ref(_L1_cond_ref(x, cond_1024, L1_cond_Wx, L1_cond_Wh, L1_cond_b), L1_ffn_w_gate, L1_ffn_w_up, L1_ffn_w_down)
    x = x + _L2_ffn_ref(_L2_cond_ref(x, cond_1024, L2_cond_weight), L2_ffn_rhs)
    x = x + _L3_ffn_ref(_L3_cond_ref(cond_1024, x, L3_cond_W, L3_cond_b, L3_cond_alpha), L3_ffn_Wg, L3_ffn_W1, L3_ffn_W2)
    return x

_drawn_inputs = setup_inputs


def setup_inputs(seed=0):
    import zlib

    import numpy as np

    out = dict(_drawn_inputs(seed))
    spreads = {'L0_cond_b1': (0.0, 0.779),
     'L0_cond_b2': (0.0, 0.625),
     'L0_ffn_norm_scale': (1.0, 0.6),
     'L1_cond_b': (0.0, 2.0),
     'L3_cond_alpha': (0.10000000149011612, 0.6)}
    factors = {'L0_ffn_w_router': 8.0,
     'L0_ffn_w_up': 8.0,
     'L0_ffn_w_down': 8.0,
     'L1_cond_Wx': 8.0,
     'L1_cond_Wh': 8.0,
     'L1_ffn_w_gate': 8.0,
     'L1_ffn_w_up': 8.0,
     'L1_ffn_w_down': 8.0,
     'L3_cond_W': 8.0,
     'L3_cond_b': 64.0,
     'L3_ffn_Wg': 8.0,
     'L3_ffn_W1': 8.0,
     'L3_ffn_W2': 8.0}
    for name, (base, spread) in spreads.items():
        noise = np.random.default_rng([zlib.crc32(name.encode()), seed]).standard_normal(out[name].shape)
        drawn = base * np.exp(spread * noise) if base else spread * noise
        out[name] = jnp.asarray(drawn.astype(out[name].dtype))
    for name, factor in factors.items():
        out[name] = (out[name] * factor).astype(out[name].dtype)
    return out
```

```python
from contextlib import ExitStack

import concourse.bass as bass
from concourse import mybir

F32 = mybir.dt.float32
F32R = mybir.dt.float32r
BF16 = mybir.dt.bfloat16
ALU = mybir.AluOpType
ACT = mybir.ActivationFunctionType
X = mybir.AxisListType.X

P = 128
S = 32
E = 8
BS = 4
NB = S // BS
N = BS * P
T = S * P
H0 = 352
H1 = 384
H3 = 256
CH0 = [(0, 128), (128, 128), (256, 96)]
CAP = int(T * 2 * 1.25 / E)
MAGIC = 1.5 * 2.0 ** 23
MAGIC16 = 192.0
Q16 = 32767.0
TINY = 1e-12

PARAMS = [("condT", 128), ("W1T", 128), ("W2T", 128), ("b2", 128), ("l2w", 128), ("rhsT", 128),
          ("WhT", 128), ("WzT", 128), ("Wx", 512), ("Wh", 512), ("wrT", 8), ("WgT", 8),
          ("bl", 4), ("b1", 1), ("nscale", 1), ("b3", 1), ("alpha", 1)]
CONSTS = [("ident", 128), ("before", 128), ("ties", 64), ("rows", 256), ("ones", 128)]


def columns(parts):
    at, out = 0, {}
    for name, n in parts:
        out[name] = slice(at, at + n)
        at += n
    return out, at


PC, NPC = columns(PARAMS)
CC, NCC = columns(CONSTS)


def block_of(i, n=N):
    return slice(i * n, (i + 1) * n) if isinstance(i, int) else bass.ds(i * n, n)


def need(engine, semaphore, value):
    if not isinstance(value, int) or value > 0:
        engine.wait_ge(semaphore, value)


def mixer_kernel(nc, x, params, consts, w_up, w_down, l1w, w1, w2, out):
    ctx = ExitStack()
    with ctx:
        def keep(name, shape, dt=F32):
            return ctx.enter_context(nc.sbuf_tensor(name, shape, dt))

        def sem(name):
            return ctx.enter_context(nc.semaphore(name))

        tok = keep("tok", [P, S, P])
        xh = keep("xh", [P, T + T + P])
        par = keep("par", [P, NPC])
        con = keep("con", [P, NCC])
        gate1 = keep("gate1", [P, P])
        hid = keep("hid", [P, P])
        tiny = keep("tiny", [P, 64])
        wsel = keep("wsel", [P, S, E])
        scores = keep("scores", [P, S, E])
        expo = keep("expo", [P, S, E])
        rowst = keep("rowst", [P, 4, S])
        x1rows = keep("x1rows", [P, BS, P])
        cell = keep("cell", [P, P])
        gact = keep("gact", [P, 4, P])
        uv = keep("uv", [P, 2, P])
        tcell = keep("tcell", [P, P])
        wscale = keep("wscale", [P, 2, 36])
        maxima = keep("maxima", [P, 2 * NB])
        dmod = keep("dmod", [P, P])
        ysT = keep("ysT", [P, P])
        rscale = keep("rscale", [P, P])
        rhs_q = keep("rhs_q", [P, P], BF16)
        lsc = keep("lsc", [P, 2 * BS])
        sel = keep("sel", [P, E, S])
        place = keep("place", [P, E, S])
        cnt = keep("cnt", [P, E])
        counts = cnt[:]
        xT = xh[:, 0:T]
        hT = xh[:, T:]

        def col(n):
            return tiny[:, n:n + 1]

        def prm(name):
            return par[:, PC[name]]

        def cst(name):
            return con[:, CC[name]]

        ident = cst("ident")
        EPS_RMS, MAG, EPS_L2, HB = 0, 1, 2, 4
        B1H, B3H, LEAK2 = 8, 9, 10
        INVX, KU, KG, SG, KGS, SGS, KO, SO, SX, SU, TMP, TMP2, RSC = range(16, 29)

        banks = [ctx.enter_context(nc.psum_tensor(f"bank{i}", [P, 512], F32)) for i in range(8)]
        GV, Y, Z, TP = banks[0:4], banks[4:6], banks[6], banks[7]

        def layer(parts):
            made = ExitStack()
            got = [made.enter_context(nc.sbuf_tensor(n, s, d)) for n, s, d in parts]
            made.close()
            return got

        (xn_hi, xn_lo, wu_hi, wu_lo, wd_hi, wd_lo, work0, h0_hi, h0_lo, wr_hi, wr_lo) = layer([
            ("xn_hi", [P, T], F32R), ("xn_lo", [P, T], F32R),
            ("wu_hi", [P, E, 2 * H0], F32R), ("wu_lo", [P, E, 2 * H0], F32R),
            ("wd_hi", [P, E, 3, P], F32R), ("wd_lo", [P, E, 3, P], F32R),
            ("work0", [P, 6 * N], F32), ("h0_hi", [P, 4, N], F32R), ("h0_lo", [P, 4, N], F32R),
            ("wr_hi", [P, E], F32R), ("wr_lo", [P, E], F32R)])
        silu0, hf0, scaled0 = (work0[:, k * 2 * N:(k + 1) * 2 * N].rearrange("p (b n) -> p b n", b=2)
                               for k in range(3))
        wup_raw = xh[:, 0:E * 2 * H0].rearrange("p (e r) -> p e r", e=E)
        wdown_raw = work0[:].rearrange("p (e c d) -> p e c d", e=E, c=3)
        lines = xh[:, E * 2 * H0:E * 2 * H0 + 5 * N].rearrange("p (k n) -> p k n", k=5)
        hrow, xnrow, square = lines[:, 0:2], lines[:, 2:4], lines[:, 4]
        pairs = xh[:, E * 2 * H0:E * 2 * H0 + S * E * E].rearrange("p (s e f) -> p s e f", s=S, e=E)

        layer1 = ExitStack()
        (gate_s, sig_s, l1_hi, l1_lo, xq_hi, xq_lo) = [
            layer1.enter_context(nc.sbuf_tensor(n, s, d)) for n, s, d in [
                ("gate_s", [P, NB * 3 * N], F32), ("sig_s", [P, 2, 3 * N], F32),
                ("l1_hi", [P, 9, P], F32R), ("l1_lo", [P, 9, P], F32R),
                ("xq_hi", [P, 2, N], F32R), ("xq_lo", [P, 2, N], F32R)]]
        up_s, = layer([("up_s", [P, NB * 3 * N], F32)])
        (oq_hi, oq_lo, modx, norm2, q2, qT, f1, f2, hs_hi, hs_lo) = layer([
            ("oq_hi", [P, 3, N], F32R), ("oq_lo", [P, 3, N], F32R), ("modx", [P, BS, P], F32),
            ("norm2", [P, BS, P], F32), ("q2", [P, BS, P], F32), ("qT", [P, N], BF16),
            ("f1", [P, BS, P], F32), ("f2", [P, BS, P], F32),
            ("hs_hi", [P, T], F32R), ("hs_lo", [P, T], F32R)])
        layer1.close()
        l1_raw = sig_s[:].rearrange("p b n -> p (b n)")[:, 0:9 * P]
        l1_q = sig_s[:].rearrange("p b n -> p (b n)")[:, 9 * P:18 * P]
        (w1_hi, w1_lo, w2_hi, w2_lo, work3, h3_hi, h3_lo, pairs3) = layer([
            ("w1_hi", [P, E, 2 * H3], F32R), ("w1_lo", [P, E, 2 * H3], F32R),
            ("w2_hi", [P, E, 2, P], F32R), ("w2_lo", [P, E, 2, P], F32R),
            ("work3", [P, 6 * N], F32), ("h3_hi", [P, 4, N], F32R), ("h3_lo", [P, 4, N], F32R),
            ("pairs3", [P, S, E, E], F32)])
        gelu3, hf3, scaled3 = (work3[:, k * 2 * N:(k + 1) * 2 * N].rearrange("p (b n) -> p b n", b=2)
                               for k in range(3))
        w1_raw = tok[:].rearrange("p s d -> p (s d)").rearrange("p (e r) -> p e r", e=E)
        w2_raw = work3[:, 0:E * 2 * P].rearrange("p (e c d) -> p e c d", e=E, c=2)

        (params_in, consts_in, x_in, wdown_in, l1w_in, w1_in, w2_in) = map(
            sem, ["params_in", "consts_in", "x_in", "wdown_in", "l1w_in", "w1_in", "w2_in"])
        wup_in = [sem(f"wup_in{e}") for e in range(E)]
        dve_step, eps_set, magic_set = map(sem, ["dve_step", "eps_set", "magic_set"])
        (hidden_mm, hidden_done, gate_mm, gate_pre, gate_tanh, gate_done) = map(
            sem, ["hidden_mm", "hidden_done", "gate_mm", "gate_pre", "gate_tanh", "gate_done"])
        (h_done, square_done, sum_done, sqrt_done, xn_done, xnT_mm, xn_hi_done, xn_lo_done,
         r_done) = map(sem, ["h_done", "square_done", "sum_done", "sqrt_done", "xn_done", "xnT_mm",
                             "xn_hi_done", "xn_lo_done", "r_done"])
        wu_hi_done, wu_lo_done, wd_hi_done, wd_lo_done, wr_hi_done, wr_lo_done = map(
            sem, ["wu_hi_done", "wu_lo_done", "wd_hi_done", "wd_lo_done", "wr_hi_done", "wr_lo_done"])
        score_mm, scores_read, centred, exp_done = map(
            sem, ["score_mm", "scores_read", "centred", "exp_done"])
        (g_mm, v_mm, silu_done, h0_done, h0_hi_done, h0_lo_done, down_mm, scaled_done, added,
         turned, x1T_done) = map(sem, ["g_mm", "v_mm", "silu_done", "h0_done", "h0_hi_done",
                                       "h0_lo_done", "down_mm", "scaled_done", "added", "turned",
                                       "x1T_done"])
        z_mm, gates_done, uv_done, cell_done, tcell_done, state_done, hmax_done = map(
            sem, ["z_mm", "gates_done", "uv_done", "cell_done", "tcell_done", "state_done", "hmax_done"])
        l1q_done, l1T_mm, l1_hi_done, l1_lo_done = map(sem, ["l1q_done", "l1T_mm", "l1_hi_done", "l1_lo_done"])
        prep_in, prep_mm, prep_act, prep_read, bias_done, kept_done, wh_halved = map(
            sem, ["prep_in", "prep_mm", "prep_act", "prep_read", "bias_done", "kept_done", "wh_halved"])
        max_col, max_turned, max_row, max_mm, factor_done = map(
            sem, ["max_col", "max_turned", "max_row", "max_mm", "factor_done"])
        (xt_done, xq_hi_done, xq_lo_done, ug_mm, ug_copied, ug_max) = map(
            sem, ["xt_done", "xq_hi_done", "xq_lo_done", "ug_mm", "ug_copied", "ug_max"])
        (gt_done, g_done, sig_done, sig_rounded, gs_done, gs_max, ut_done) = map(
            sem, ["gt_done", "g_done", "sig_done", "sig_rounded", "gs_done", "gs_max", "ut_done"])
        gst_done, g2_done, o_done, o_max = map(sem, ["gst_done", "g2_done", "o_done", "o_max"])
        (ot_done, oq_hi_done, oq_lo_done, o_mm, x2T_done, modx_done, l2_mm, norm_done, nmax_done,
         lscale_done, linv_done, q1_done, q2_done, q2T_mm, qT_done, acc_mm, f1_done, f2_done,
         fT_mm, x3T_done) = map(sem, [
             "ot_done", "oq_hi_done", "oq_lo_done", "o_mm", "x2T_done", "modx_done", "l2_mm",
             "norm_done", "nmax_done", "lscale_done", "linv_done", "q1_done", "q2_done", "q2T_mm",
             "qT_done", "acc_mm", "f1_done", "f2_done", "fT_mm", "x3T_done"])
        (rz_mm, rgate_done, ru_done, rv_done, rstate_done, hs_hi_done, hs_lo_done) = map(sem, [
            "rz_mm", "rgate_done", "ru_done", "rv_done", "rstate_done", "hs_hi_done", "hs_lo_done"])
        (logit_mm, centred3, exp3_done, counts_done, before_mm) = map(sem, [
            "logit_mm", "centred3", "exp3_done", "counts_done", "before_mm"])
        w1_hi_done, w1_lo_done, w2_hi_done, w2_lo_done = map(
            sem, ["w1_hi_done", "w1_lo_done", "w2_hi_done", "w2_lo_done"])
        x3_turned, x3_done = map(sem, ["x3_turned", "x3_done"])
        (i3_mm, g3_mm, gelu_done, h3_done, h3_hi_done, h3_lo_done, down3_mm, scaled3_done,
         added3, out_done) = map(sem, ["i3_mm", "g3_mm", "gelu_done", "h3_done", "h3_hi_done",
                                       "h3_lo_done", "down3_mm", "scaled3_done", "added3", "out_done"])

        steps = [0]

        def link(dve, ins):
            steps[0] += 1
            ins.then_inc(dve_step, 1)
            dve.wait_ge(dve_step, steps[0])

        LSTM_AT = [7, 11, 15, 19]
        NK0 = 3 * E
        NK3 = 2 * E

        def wide(ap, n):
            return ap.unsqueeze(2).broadcast_to([P, ap.shape[1], n])

        def over(ap, n):
            return ap.unsqueeze(1).broadcast_to([P, n, ap.shape[1]])

        def steps_of(i):
            return block_of(i, BS)

        block = ctx.enter_context(nc.Block())

        @block.sync
        def _(sp):
            sp.dma_start(par[:], params).then_inc(params_in, 16)
            sp.dma_start(tok[:], x).then_inc(x_in, 16)
            sp.dma_start(con[:], consts).then_inc(consts_in, 16)
            for e in range(E):
                sp.dma_start(wup_raw[:, e, :], w_up[:, e, :]).then_inc(wup_in[e], 16)
            for c, (row, rows) in enumerate(CH0):
                sp.dma_start(wdown_raw[0:rows, :, c, :],
                             w_down[:, row:row + rows, :].rearrange("e p d -> p e d")).then_inc(wdown_in, 16)
            sp.wait_ge(added, NB * E)
            sp.dma_start(l1_raw, l1w).then_inc(l1w_in, 16)
            sp.wait_ge(x1T_done, NB)
            sp.dma_start(w1_raw, w1).then_inc(w1_in, 16)
            sp.wait_ge(x3T_done, NB)
            sp.dma_start(w2_raw, w2).then_inc(w2_in, 16)
            for i in range(NB):
                sp.wait_ge(added3, (i + 1) * E)
                sp.dma_start(out[:, i * BS:(i + 1) * BS, :], x1rows[:]).then_inc(out_done, 16)
            sp.wait_ge(out_done, 16 * NB)

        @block.tensor
        def _(pe):
            pe.nop().then_inc(turned, 1)
            pe.wait_ge(params_in, 16)
            pe.matmul(GV[0][:, 0:P], prm("W1T"), prm("condT"), start=True, stop=True).then_inc(hidden_mm, 1)
            pe.wait_ge(hidden_done, 1)
            pe.matmul(GV[1][:, 0:P], hid[:], prm("W2T"), start=True, stop=True).then_inc(gate_mm, 1)
            pe.wait_ge(consts_in, 16)
            pe.wait_ge(wr_lo_done, 1)
            for k in range(NB + 1):
                if k < NB:
                    pe.wait_ge(xn_done, k + 1)
                    need(pe, xn_lo_done, k - 1)
                    for j in range(BS):
                        m = pe.transpose(GV[2 + k % 2][:, j * P:(j + 1) * P],
                                         xnrow[:, k % 2, j * P:(j + 1) * P], ident)
                    m.then_inc(xnT_mm, 1)
                if k >= 1:
                    pe.wait_ge(xn_lo_done, k)
                    for t in range((k - 1) * BS, k * BS):
                        at, to = slice(t * P, (t + 1) * P), Z[:, t * E:(t + 1) * E]
                        pe.matmul(to, xn_hi[:, at], wr_hi[:], start=True, stop=False)
                        pe.matmul(to, xn_hi[:, at], wr_lo[:], start=False, stop=False)
                        m = pe.matmul(to, xn_lo[:, at], wr_hi[:], start=False, stop=True)
            m.then_inc(score_mm, 1)

            def product(to, a_hi, a_lo, b_hi, b_lo, start=True, stop=True):
                pe.matmul(to, a_hi, b_hi, start=start, stop=False)
                pe.matmul(to, a_hi, b_lo, start=False, stop=False)
                return pe.matmul(to, a_lo, b_hi, start=False, stop=stop)

            def up0(i, e, c):
                k = 3 * e + c
                row, rows = CH0[c]
                need(pe, h0_done, i * NK0 + k - 1)
                for bank, first, signal in ((GV[2 * (k % 2)], H0, g_mm), (GV[2 * (k % 2) + 1], 0, v_mm)):
                    at = slice(first + row, first + row + rows)
                    product(bank[0:rows, :], wu_hi[:, e, at], wu_lo[:, e, at], xn_hi[:, block_of(i)],
                            xn_lo[:, block_of(i)]).then_inc(signal, 1)

            def down0(m, e):
                pe.wait_ge(h0_lo_done, 3 * m + 3)
                need(pe, scaled_done, m - 1)
                for j in range(BS):
                    for c, (row, rows) in enumerate(CH0):
                        r, at = (3 * e + c) % 4, slice(j * P, (j + 1) * P)
                        last = product(Y[e % 2][:, at], h0_hi[0:rows, r, at], h0_lo[0:rows, r, at],
                                       wd_hi[0:rows, e, c, :], wd_lo[0:rows, e, c, :],
                                       start=(c == 0), stop=(c == 2))
                last.then_inc(down_mm, 1)

            def turn0(i):
                pe.wait_ge(added, i * E)
                for j in range(BS):
                    last = pe.transpose(TP[:, j * P:(j + 1) * P], x1rows[:, j, :], ident)
                last.then_inc(turned, 1)

            def lstm_step(i, j):
                t = (i - 1) * BS + j
                if j == 0:
                    pe.wait_ge(x1T_done, i)
                pe.wait_ge(state_done, t + 1)
                for w, rhs, first in ((prm("Wx"), xT, True), (prm("Wh"), hT, False)):
                    for g in range(4):
                        last = pe.matmul(Z[:, g * P:(g + 1) * P], w[:, g * P:(g + 1) * P], rhs[:, block_of(t, P)],
                                         start=(first and g == 0), stop=(not first and g == 3),
                                         skip_group_check=True)
                last.then_inc(z_mm, 1)

            def layer0(i, main=True, tail=True):
                for k in range(NK0):
                    e, c = k // 3, k % 3
                    if main:
                        up0(i, e, c)
                    if c == 1 and (main if e else tail):
                        down0(i * E + e - 1, (e - 1) % E)
                    if tail and k == 4:
                        turn0(i)
                    if tail and k in LSTM_AT:
                        lstm_step(i, LSTM_AT.index(k))

            pe.wait_ge(wh_halved, 1)
            pe.wait_ge(wu_lo_done, E)
            pe.wait_ge(wd_lo_done, 2)
            pe.wait_ge(scores_read, 1)
            layer0(0, tail=False)
            with pe.Fori(1, NB) as i:
                layer0(i)
            layer0(NB, main=False)

            pe.wait_ge(l1q_done, 1)
            for n in range(9):
                if n >= 4:
                    pe.wait_ge(l1_lo_done, n - 3)
                pe.transpose(GV[n % 4][:, 0:P], l1_q[:, n * P:(n + 1) * P], ident).then_inc(l1T_mm, 1)
            pe.wait_ge(prep_in, 1)
            pe.matmul(Y[0][:, 0:P], f1[:, 0, :], f1[:, 1, :], start=True, stop=True)
            pe.transpose(Y[0][:, P:2 * P], f1[:, 2, :], ident)
            pe.matmul(Y[0][:, 2 * P:3 * P], col(RSC).broadcast_to([P, P]), ident,
                      start=True, stop=True).then_inc(prep_mm, 1)

            spread = [0]

            def spread_max():
                spread[0] += 1
                n = spread[0]
                pe.wait_ge(max_col, n)
                pe.transpose(TP[0:1, 0:P], col(TMP), ident).then_inc(max_turned, 1)
                pe.wait_ge(max_row, n)
                pe.matmul(TP[:, P:P + 1], cst("ones")[0:1, :], tiny[0:1, TMP2:TMP2 + 1],
                          start=True, stop=True).then_inc(max_mm, 1)

            spread_max()

            def up_gate(i):
                b = 0
                pe.wait_ge(xq_lo_done, i + 1)
                for c in range(6):
                    need(pe, ug_copied, i * 6 + c - 5)
                    product((GV + Y)[c][:, :], l1_hi[:, c, :], l1_lo[:, c, :],
                            xq_hi[:, b, :], xq_lo[:, b, :]).then_inc(ug_mm, 1)

            pe.wait_ge(l1_lo_done, 9)
            pe.wait_ge(prep_read, 1)
            up_gate(0)
            with pe.Fori(1, NB) as i:
                up_gate(i)
            for _ in range(4):
                spread_max()

            def tile(bank, j):
                return bank[:, j * P:(j + 1) * P]

            def recur(i, j):
                t = i * BS + j
                if j == 0:
                    pe.wait_ge(x3T_done, i + 1)
                    pe.wait_ge(rgate_done, i * BS + 1)
                    pe.matmul(Z[:, :], prm("WzT"), xT[:, block_of(i)], start=True, stop=False,
                              skip_group_check=True)
                pe.wait_ge(rstate_done, t + 1)
                pe.matmul(tile(Z, j), prm("WhT"), hT[:, block_of(t, P)], start=False, stop=(j == 3),
                          skip_group_check=True).then_inc(rz_mm, 1)

            def layer2(i, main=True, tail=True):
                if main:
                    pe.wait_ge(oq_lo_done, i + 1)
                    need(pe, x2T_done, i)
                    for c in range(3):
                        last = product(GV[0][:, :], l1_hi[:, 6 + c, :], l1_lo[:, 6 + c, :], oq_hi[:, c, :],
                                       oq_lo[:, c, :], start=(c == 0), stop=(c == 2))
                    last.then_inc(o_mm, 1)
                if tail:
                    recur(i - 1, 0)
                if main:
                    pe.wait_ge(modx_done, i + 1)
                    for j in range(BS):
                        last = pe.matmul(tile(GV[1], j), modx[:, j, :], prm("l2w"), start=True, stop=True)
                    last.then_inc(l2_mm, 1)
                if tail:
                    recur(i - 1, 1)
                if main:
                    pe.wait_ge(q2_done, i + 1)
                    for j in range(BS):
                        last = pe.transpose(tile(GV[2], j), q2[:, j, :], ident)
                    last.then_inc(q2T_mm, 1)
                if tail:
                    recur(i - 1, 2)
                if main:
                    pe.wait_ge(qT_done, i + 1)
                    for j in range(BS):
                        last = pe.matmul(tile(GV[3], j), qT[:, j * P:(j + 1) * P], rhs_q[:], start=True, stop=True)
                    last.then_inc(acc_mm, 1)
                if tail:
                    recur(i - 1, 3)
                if main:
                    pe.wait_ge(f2_done, i + 1)
                    for j in range(BS):
                        last = pe.transpose(tile(Y[0], j), f2[:, j, :], ident)
                    last.then_inc(fT_mm, 1)

            layer2(0, tail=False)
            with pe.Fori(1, NB) as i:
                layer2(i)
            layer2(NB, main=False)

            pe.wait_ge(rstate_done, S + 1)
            pe.wait_ge(rgate_done, S + 1)
            for t in range(S):
                last = pe.matmul(Z[:, t * E:(t + 1) * E], hT[:, (t + 1) * P:(t + 2) * P], prm("WgT"),
                                 start=True, stop=True)
            last.then_inc(logit_mm, 1)
            pe.wait_ge(counts_done, 1)
            pe.matmul(Y[1][:, 0:E], cst("before"), counts, start=True, stop=True).then_inc(before_mm, 1)
            pe.wait_ge(w1_lo_done, E)
            for i in range(NB):
                need(pe, x3_done, i - 1)
                for j in range(BS):
                    last = pe.transpose(tile(GV[i % 2], j), xT[:, (i * BS + j) * P:(i * BS + j + 1) * P], ident)
                last.then_inc(x3_turned, 1)
            pe.wait_ge(x3_done, NB)

            def up3(i, e, c):
                k = 2 * e + c
                need(pe, h3_done, i * NK3 + k - 1)
                for bank, first, signal in ((GV[2 * (k % 2)], 0, i3_mm), (GV[2 * (k % 2) + 1], H3, g3_mm)):
                    at = slice(first + c * P, first + (c + 1) * P)
                    product(bank[:, :], w1_hi[:, e, at], w1_lo[:, e, at], hs_hi[:, block_of(i)],
                            hs_lo[:, block_of(i)]).then_inc(signal, 1)

            def down3(m, e):
                pe.wait_ge(h3_lo_done, 2 * m + 2)
                need(pe, scaled3_done, m - 1)
                for j in range(BS):
                    for c in range(2):
                        r, at = (2 * e + c) % 4, slice(j * P, (j + 1) * P)
                        last = product(Y[e % 2][:, at], h3_hi[:, r, at], h3_lo[:, r, at],
                                       w2_hi[:, e, c, :], w2_lo[:, e, c, :], start=(c == 0), stop=(c == 1))
                last.then_inc(down3_mm, 1)

            def layer3(i, main=True, tail=True):
                for k in range(NK3):
                    e, c = k // 2, k % 2
                    if main:
                        up3(i, e, c)
                    if c == 1 and (main if e else tail):
                        down3(i * E + e - 1, (e - 1) % E)

            pe.wait_ge(w2_lo_done, 1)
            pe.wait_ge(hs_lo_done, NB)
            pe.wait_ge(kept_done, 1)
            layer3(0, tail=False)
            with pe.Fori(1, NB) as i:
                layer3(i)
            layer3(NB, main=False)

        @block.scalar
        def _(act):
            act.wait_ge(params_in, 16)
            nc.scalar.mul(tiny[:, HB:HB + 4], prm("bl"), 0.5)
            nc.scalar.mul(col(B3H), prm("b3"), 0.5).then_inc(bias_done, 1)
            act.wait_ge(hidden_mm, 1)
            nc.scalar.activation(hid[:], GV[0][:, 0:P], ACT.Silu, bias=prm("b1")).then_inc(hidden_done, 1)
            act.wait_ge(gate_pre, 1)
            nc.scalar.activation(gate1[:], gate1[:], ACT.Tanh, scale=0.5).then_inc(gate_tanh, 1)
            nc.scalar.copy(wr_hi[:], prm("wrT")).then_inc(wr_hi_done, 1)
            act.wait_ge(eps_set, 1)
            for k in range(NB + 1):
                if k < NB:
                    act.wait_ge(h_done, k + 1)
                    need(act, sum_done, k)
                    nc.scalar.activation(square, hrow[:, k % 2], ACT.Square).then_inc(square_done, 1)
                    act.wait_ge(sum_done, k + 1)
                    nc.scalar.activation(rowst[:, 3, k * BS:(k + 1) * BS], rowst[:, 3, k * BS:(k + 1) * BS],
                                         ACT.Sqrt, scale=1.0 / P, bias=col(EPS_RMS)).then_inc(sqrt_done, 1)
                if k >= 1:
                    act.wait_ge(xnT_mm, k)
                    nc.scalar.activation(xn_hi[:, block_of(k - 1)], GV[2 + (k - 1) % 2][:, :], ACT.Copy,
                                         scale=prm("nscale")).then_inc(xn_hi_done, 1)
            for e in range(E):
                act.wait_ge(wup_in[e], 16)
                nc.scalar.copy(wu_hi[:, e, :], wup_raw[:, e, :]).then_inc(wu_hi_done, 1)
            act.wait_ge(wdown_in, 48)
            nc.scalar.copy(wd_hi[:, :, 0:2, :], wdown_raw[:, :, 0:2, :]).then_inc(wd_hi_done, 1)
            nc.scalar.copy(wd_hi[0:96, :, 2, :], wdown_raw[0:96, :, 2, :]).then_inc(wd_hi_done, 1)
            act.wait_ge(centred, 1)
            nc.scalar.activation(expo[:], expo[:], ACT.Exp).then_inc(exp_done, 1)
            act.wait_ge(wu_lo_done, E)
            nc.scalar.mul(hT[:, 0:P], prm("condT"), 2.0).then_inc(state_done, 1)
            act.wait_ge(wd_lo_done, 2)

            def high0(n, k):
                rows = CH0[k % 3][1]
                act.wait_ge(h0_done, n + 1)
                return nc.scalar.copy(h0_hi[0:rows, k % 4, :], hf0[0:rows, k % 2, :]).then_inc(h0_hi_done, 1)

            def gates(i, j):
                t = (i - 1) * BS + j
                act.wait_ge(z_mm, t + 1)
                for g in range(4):
                    tanh_g = g == 3
                    last = nc.scalar.activation(gact[:, g, :], Z[:, g * P:(g + 1) * P], ACT.Tanh,
                                                scale=1.0 if tanh_g else 0.5,
                                                bias=prm("bl")[:, 3:4] if tanh_g else tiny[:, HB + g:HB + g + 1])
                last.then_inc(gates_done, 1)

            def cell_tanh(i, j):
                t = (i - 1) * BS + j
                act.wait_ge(cell_done, t + 2)
                nc.scalar.activation(tcell[:], cell[:], ACT.Tanh, scale=0.5).then_inc(tcell_done, 1)

            def layer0(i, main=True, tail=True):
                for k in range(NK0):
                    n = i * NK0 + k
                    rows = CH0[k % 3][1]
                    if main:
                        act.wait_ge(g_mm, n + 1)
                        need(act, h0_done, n - 1)
                        nc.scalar.activation(silu0[0:rows, k % 2, :], GV[2 * (k % 2)][0:rows, :],
                                             ACT.Silu).then_inc(silu_done, 1)
                    if main if k else tail:
                        need(act, down_mm, i * E + (k - 5) // 3 + 1)
                        high0(n - 1, (k - 1) % NK0)
                    if tail and k == 4:
                        act.wait_ge(turned, i + 1)
                        nc.scalar.copy(xT[:, block_of(i - 1)], TP[:, :]).then_inc(x1T_done, 1)
                    if tail and k in LSTM_AT:
                        gates(i, LSTM_AT.index(k))
                    if tail and k - 1 in LSTM_AT:
                        cell_tanh(i, LSTM_AT.index(k - 1))

            layer0(0, tail=False)
            with act.Fori(1, NB) as i:
                layer0(i)
            layer0(NB, main=False)

            for n in range(9):
                act.wait_ge(l1T_mm, n + 1)
                nc.scalar.copy(l1_hi[:, n, :], GV[n % 4][:, 0:P]).then_inc(l1_hi_done, 1)
            act.wait_ge(prep_mm, 1)
            nc.scalar.activation(dmod[:], Y[0][:, 0:P], ACT.Sqrt, bias=col(EPS_L2))
            nc.scalar.copy(rhs_q[:], Y[0][:, P:2 * P])
            nc.scalar.copy(rscale[:], Y[0][:, 2 * P:3 * P]).then_inc(prep_act, 1)

            act.wait_ge(factor_done, 1)

            def states(i):
                at = hT[:, bass.ds(i * N + P, N)] if not isinstance(i, int) else hT[:, P + i * N:P + (i + 1) * N]
                nc.scalar.activation(at, at, ACT.Identity, scale=col(INVX), bias=col(MAG)).then_inc(xt_done, 1)

            def keep_ug(i):
                for c in range(6):
                    act.wait_ge(ug_mm, i * 6 + c + 1)
                    to, r = (up_s, c) if c < 3 else (gate_s, c - 3)
                    at = slice((i * 3 + r) * N, (i * 3 + r + 1) * N) if isinstance(i, int) else \
                        bass.ds((i * 3 + r) * N, N)
                    nc.scalar.copy(to[:, at], (GV + Y)[c][:, :]).then_inc(ug_copied, 1)

            states(0)
            with act.Fori(0, NB - 1) as i:
                states(i + 1)
                keep_ug(i)
            keep_ug(NB - 1)

            def rounded(i, scale, signal):
                at = gate_s[:, block_of(i, 3 * N)]
                nc.scalar.activation(at, at, ACT.Identity, scale=col(scale), bias=col(MAG)).then_inc(signal, 1)

            def sigmoid(i, b):
                act.wait_ge(g_done, i + 1)
                need(act, gs_done, i - 1)
                nc.scalar.activation(sig_s[:, b, :], gate_s[:, block_of(i, 3 * N)],
                                     ACT.Sigmoid).then_inc(sig_done, 1)

            act.wait_ge(factor_done, 2)
            rounded(0, KG, gt_done)
            for i in range(NB):
                if i + 1 < NB:
                    rounded(i + 1, KG, gt_done)
                sigmoid(i, i % 2)
            act.wait_ge(factor_done, 3)
            with act.Fori(0, NB) as i:
                rounded(i, KGS, gst_done)
            act.wait_ge(factor_done, 4)
            nc.scalar.copy(hT[:, 0:P], prm("condT")).then_inc(rstate_done, 1)
            act.nop().then_inc(rgate_done, 1)

            def recur(i, j):
                t = i * BS + j
                act.wait_ge(rz_mm, t + 1)
                nc.scalar.activation(gact[:, 0, :], Z[:, j * P:(j + 1) * P], ACT.Tanh, scale=0.5,
                                     bias=col(B3H)).then_inc(rgate_done, 1)
                act.wait_ge(rv_done, t + 1)
                nc.scalar.activation(hT[:, block_of(t + 1, P)], uv[:, 1, :], ACT.Tanh,
                                     scale=0.5).then_inc(rstate_done, 1)

            def layer2(i, main=True, tail=True):
                if main:
                    rounded(i, KO, ot_done)
                if tail:
                    recur(i - 1, 0)
                    recur(i - 1, 1)
                if main:
                    act.wait_ge(q2T_mm, i + 1)
                    nc.scalar.copy(qT[:], GV[2][:, :]).then_inc(qT_done, 1)
                if tail:
                    recur(i - 1, 2)
                    recur(i - 1, 3)
                    at = slice((i - 1) * N + P, i * N + P) if isinstance(i, int) else bass.ds((i - 1) * N + P, N)
                    act.wait_ge(rstate_done, i * BS + 1)
                    nc.scalar.copy(hs_hi[:, block_of(i - 1)], hT[:, at]).then_inc(hs_hi_done, 1)

            layer2(0, tail=False)
            with act.Fori(1, NB) as i:
                layer2(i)
            layer2(NB, main=False)

            act.wait_ge(centred3, 1)
            nc.scalar.activation(expo[:], expo[:], ACT.Exp).then_inc(exp3_done, 1)
            act.wait_ge(w1_in, 16)
            for e in range(E):
                nc.scalar.copy(w1_hi[:, e, :], w1_raw[:, e, :]).then_inc(w1_hi_done, 1)
            act.wait_ge(w2_in, 16)
            nc.scalar.copy(w2_hi[:], w2_raw).then_inc(w2_hi_done, 1)
            for i in range(NB):
                act.wait_ge(x3_turned, i + 1)
                nc.scalar.copy(tok[:, i * BS:(i + 1) * BS, :].rearrange("p s d -> p (s d)"),
                               GV[i % 2][:, :]).then_inc(x3_done, 1)
            act.wait_ge(w2_lo_done, 1)

            def layer3(i, main=True, tail=True):
                for k in range(NK3):
                    n = i * NK3 + k
                    if main:
                        act.wait_ge(i3_mm, n + 1)
                        need(act, h3_done, n - 1)
                        nc.scalar.activation(gelu3[:, k % 2, :], GV[2 * (k % 2)][:, :],
                                             ACT.Gelu).then_inc(gelu_done, 1)
                    if main if k else tail:
                        need(act, down3_mm, i * E + (k - 5) // 2 + 1)
                        act.wait_ge(h3_done, n)
                        nc.scalar.copy(h3_hi[:, (k - 1) % 4, :], hf3[:, (k - 1) % 2, :]).then_inc(h3_hi_done, 1)

            layer3(0, tail=False)
            with act.Fori(1, NB) as i:
                layer3(i)
            layer3(NB, main=False)

        @block.vector
        def _(dve):
            dve.memset(col(EPS_RMS), 1e-6)
            dve.memset(col(MAG), MAGIC)
            dve.memset(col(EPS_L2), 1e-8)
            dve.memset(cell[:], 0.0).then_inc(cell_done, 1)
            dve.wait_ge(cell_done, 1)
            dve.nop().then_inc(eps_set, 1)
            dve.wait_ge(params_in, 16)
            dve.tensor_scalar(prm("Wh"), prm("Wh"), 0.5, None, ALU.mult).then_inc(wh_halved, 1)
            dve.wait_ge(gate_mm, 1)
            dve.tensor_tensor(gate1[:], GV[1][:, 0:P], prm("b2"), ALU.add).then_inc(gate_pre, 1)
            dve.wait_ge(gate_tanh, 1)
            dve.tensor_scalar(gate1[:], gate1[:], 0.5, 1.5, ALU.mult, ALU.add).then_inc(gate_done, 1)
            dve.wait_ge(gate_done, 1)
            dve.wait_ge(wr_hi_done, 1)
            dve.tensor_tensor(wr_lo[:], prm("wrT"), wr_hi[:].bitcast(F32), ALU.subtract).then_inc(wr_lo_done, 1)
            dve.wait_ge(x_in, 16)

            def gated(k):
                need(dve, r_done, k - 1)
                need(dve, xn_done, k - 1)
                dve.tensor_tensor(hrow[:, k % 2].rearrange("p (s d) -> p s d", s=BS),
                                  tok[:, k * BS:(k + 1) * BS, :], over(gate1[:], BS),
                                  ALU.mult).then_inc(h_done, 1)

            gated(0)
            for k in range(NB + 1):
                if k + 1 < NB:
                    gated(k + 1)
                if k < NB:
                    at = rowst[:, 3, k * BS:(k + 1) * BS]
                    dve.wait_ge(square_done, k + 1)
                    dve.tensor_reduce(at, square.rearrange("p (s d) -> p s d", s=BS), X,
                                      ALU.add).then_inc(sum_done, 1)
                    dve.wait_ge(sqrt_done, k + 1)
                    link(dve, dve.reciprocal(at, at))
                    need(dve, xnT_mm, k - 1)
                    dve.tensor_tensor(xnrow[:, k % 2].rearrange("p (s d) -> p s d", s=BS),
                                      hrow[:, k % 2].rearrange("p (s d) -> p s d", s=BS), wide(at, P),
                                      ALU.mult).then_inc(xn_done, 1)
                if k >= 1:
                    dve.wait_ge(xn_hi_done, k)
                    dve.scalar_tensor_tensor(
                        out=xn_lo[:, block_of(k - 1)], in0=GV[2 + (k - 1) % 2][:, :], scalar=prm("nscale"),
                        in1=xn_hi[:, block_of(k - 1)].bitcast(F32), op0=ALU.mult,
                        op1=ALU.subtract).then_inc(xn_lo_done, 1)

            def ranks(pairs_at, signal):
                link(dve, dve.tensor_reduce(rowst[:, 0, :], scores[:], X, ALU.max))
                dve.tensor_tensor(expo[:], scores[:], wide(rowst[:, 0, :], E), ALU.subtract).then_inc(signal, 1)
                link(dve, dve.tensor_tensor(pairs_at, scores[:].unsqueeze(2).broadcast_to([P, S, E, E]),
                                            scores[:].unsqueeze(3).broadcast_to([P, S, E, E]), ALU.subtract))
                flat = pairs_at.rearrange("p s e f -> p s (e f)")
                link(dve, dve.tensor_tensor(flat, flat, over(cst("ties"), S), ALU.is_gt))
                link(dve, dve.tensor_reduce(wsel[:], pairs_at, X, ALU.add))

            dve.wait_ge(score_mm, 1)
            steps[0] += 1
            dve.tensor_copy(scores[:].rearrange("p s e -> p (s e)"), Z[:, 0:S * E]).then_inc(dve_step, 1)
            dve.wait_ge(dve_step, steps[0])
            dve.nop().then_inc(scores_read, 1)
            dve.wait_ge(r_done, NB)
            ranks(pairs, centred)
            dve.wait_ge(exp_done, 1)
            link(dve, dve.tensor_reduce(rowst[:, 1, :], expo[:], X, ALU.add))
            link(dve, dve.reciprocal(rowst[:, 2, :], rowst[:, 1, :]))
            link(dve, dve.scalar_tensor_tensor(out=wsel[:], in0=wsel[:], scalar=1.5, in1=expo[:],
                                               op0=ALU.is_lt, op1=ALU.mult))
            link(dve, dve.tensor_tensor(wsel[:], wsel[:], wide(rowst[:, 2, :], E), ALU.mult))
            dve.wait_ge(wd_lo_done, 2)
            dve.wait_ge(r_done, NB)

            def state_parts(i, j):
                t = (i - 1) * BS + j
                dve.wait_ge(gates_done, t + 1)
                dve.wait_ge(cell_done, t + 1)
                dve.scalar_tensor_tensor(out=uv[:, 0, :], in0=gact[:, 0, :], scalar=1.0, in1=gact[:, 3, :],
                                         op0=ALU.add, op1=ALU.mult).then_inc(uv_done, 1)
                dve.scalar_tensor_tensor(out=uv[:, 1, :], in0=gact[:, 1, :], scalar=1.0, in1=cell[:],
                                         op0=ALU.add, op1=ALU.mult).then_inc(uv_done, 1)
                dve.wait_ge(uv_done, 2 * t + 2)
                dve.scalar_tensor_tensor(out=cell[:], in0=uv[:, 1, :], scalar=0.5, in1=uv[:, 0, :],
                                         op0=ALU.mult, op1=ALU.add).then_inc(cell_done, 1)

            def state(i, j):
                t = (i - 1) * BS + j
                dve.wait_ge(tcell_done, t + 1)
                dve.scalar_tensor_tensor(out=hT[:, block_of(t + 1, P)], in0=gact[:, 2, :], scalar=1.0,
                                         in1=tcell[:], op0=ALU.add, op1=ALU.mult).then_inc(state_done, 1)

            def layer0(i, main=True, tail=True):
                for k in range(NK0):
                    n = i * NK0 + k
                    e, rows = k // 3, CH0[k % 3][1]
                    if main:
                        dve.wait_ge(v_mm, n + 1)
                        dve.wait_ge(silu_done, n + 1)
                        need(dve, h0_lo_done, n - 1)
                        dve.tensor_tensor(hf0[0:rows, k % 2, :], GV[2 * (k % 2) + 1][0:rows, :],
                                          silu0[0:rows, k % 2, :], ALU.mult).then_inc(h0_done, 1)
                    if k % 3 == 2 and (main if e else tail):
                        m, f = i * E + e - 1, (e - 1) % E
                        at = steps_of(i) if e else steps_of(i - 1)
                        dve.wait_ge(down_mm, m + 1)
                        need(dve, added, m - 1)
                        dve.tensor_tensor(scaled0[:, f % 2].rearrange("p (s d) -> p s d", s=BS),
                                          Y[f % 2][:, :].rearrange("p (s d) -> p s d", s=BS),
                                          wsel[:, at, f:f + 1].broadcast_to([P, BS, P]),
                                          ALU.mult).then_inc(scaled_done, 1)
                        if f == 0:
                            dve.wait_ge(scaled_done, m + 1)
                            dve.wait_ge(turned, i + 1)
                            dve.tensor_tensor(x1rows[:], tok[:, at, :], scaled0[:, 0].rearrange(
                                "p (s d) -> p s d", s=BS), ALU.add).then_inc(added, 1)
                    if tail and k in LSTM_AT:
                        state_parts(i, LSTM_AT.index(k))
                    if tail and k - 1 in LSTM_AT:
                        state(i, LSTM_AT.index(k - 1))
                    if tail and k == 21:
                        at = slice((i - 1) * N + P, i * N + P) if isinstance(i, int) else bass.ds((i - 1) * N + P, N)
                        dve.wait_ge(state_done, i * BS + 1)
                        dve.tensor_reduce(maxima[:, block_of(i - 1, 1)], hT[:, at], X, ALU.max,
                                          apply_absolute_value=True).then_inc(hmax_done, 1)

            layer0(0, tail=False)
            with dve.Fori(1, NB) as i:
                layer0(i)
            layer0(NB, main=False)

            dve.wait_ge(l1w_in, 16)
            raw = l1_raw.rearrange("p (g k) -> p g k", k=32)
            qv = l1_q.rearrange("p (g k) -> p g k", k=32)
            link(dve, dve.tensor_reduce(wscale[:, 0, :], raw, X, ALU.max, apply_absolute_value=True))
            link(dve, dve.tensor_scalar(wscale[:, 0, :], wscale[:, 0, :], 1.0 / 7.0, TINY, ALU.mult, ALU.max))
            link(dve, dve.reciprocal(wscale[:, 1, :], wscale[:, 0, :]))
            link(dve, dve.tensor_tensor(qv, raw, wide(wscale[:, 1, :], 32), ALU.mult))
            link(dve, dve.tensor_scalar(l1_q, l1_q, MAGIC, MAGIC, ALU.add, ALU.subtract))
            dve.tensor_tensor(qv, qv, wide(wscale[:, 0, :], 32), ALU.mult).then_inc(l1q_done, 1)
            link(dve, dve.tensor_scalar(ysT[:], prm("condT"), P ** -0.5, None, ALU.mult))
            link(dve, dve.tensor_tensor(f1[:, 0, :], ysT[:], ysT[:], ALU.mult))
            link(dve, dve.tensor_tensor(f1[:, 1, :], prm("l2w"), prm("l2w"), ALU.mult))
            link(dve, dve.tensor_reduce(col(TMP), prm("rhsT"), X, ALU.max, apply_absolute_value=True))
            link(dve, dve.tensor_scalar(col(RSC), col(TMP), TINY, 1.0 / 127.0, ALU.max, ALU.mult))
            link(dve, dve.reciprocal(col(TMP), col(RSC)))
            link(dve, dve.tensor_scalar(f1[:, 2, :], prm("rhsT"), col(TMP), MAGIC, ALU.mult, ALU.add))
            dve.tensor_scalar(f1[:, 2, :], f1[:, 2, :], MAGIC, None, ALU.subtract).then_inc(prep_in, 1)
            for n in range(9):
                dve.wait_ge(l1_hi_done, n + 1)
                dve.tensor_tensor(l1_lo[:, n, :], GV[n % 4][:, 0:P], l1_hi[:, n, :].bitcast(F32),
                                  ALU.subtract).then_inc(l1_lo_done, 1)
            dve.wait_ge(prep_act, 1)
            link(dve, dve.reciprocal(dmod[:], dmod[:]))
            link(dve, dve.tensor_scalar(col(LEAK2), prm("alpha"), -2.0, 2.0, ALU.mult, ALU.add))
            dve.nop().then_inc(prep_read, 1)

            counted = [0]

            def whole_max(columns_at):
                counted[0] += 1
                n = counted[0]
                dve.tensor_reduce(col(TMP), columns_at, X, ALU.max).then_inc(max_col, 1)
                dve.wait_ge(max_turned, n)
                dve.tensor_reduce(tiny[0:1, TMP2:TMP2 + 1], TP[0:1, 0:P], X, ALU.max).then_inc(max_row, 1)
                dve.wait_ge(max_mm, n)
                return TP[:, P:P + 1]

            dve.wait_ge(hmax_done, NB)
            m = whole_max(maxima[:, 0:NB])
            link(dve, dve.tensor_scalar(col(SX), m, 0.5 / Q16, TINY, ALU.mult, ALU.max))
            link(dve, dve.reciprocal(col(TMP), col(SX)))
            dve.tensor_scalar(col(INVX), col(TMP), 0.5, None, ALU.mult).then_inc(factor_done, 1)
            dve.wait_ge(factor_done, 1)

            def parts_of_x(i):
                at = slice(i * N + P, (i + 1) * N + P) if isinstance(i, int) else bass.ds(i * N + P, N)
                dve.wait_ge(xt_done, i + 1)
                need(dve, ug_mm, i * 6)
                dve.tensor_scalar(xq_hi[:, 0, :], hT[:, at], MAGIC, None, ALU.subtract).then_inc(xq_hi_done, 1)
                dve.wait_ge(xq_hi_done, i + 1)
                dve.scalar_tensor_tensor(out=xq_lo[:, 0, :], in0=hT[:, at], scalar=MAGIC,
                                         in1=xq_hi[:, 0, :].bitcast(F32), op0=ALU.subtract,
                                         op1=ALU.subtract).then_inc(xq_lo_done, 1)

            def maxima_of(i):
                for r, rows in enumerate((up_s, gate_s)):
                    at = slice(r * NB + i, r * NB + i + 1) if isinstance(i, int) else bass.ds(i + r * NB, 1)
                    dve.wait_ge(ug_copied, i * 6 + 3 * r + 3)
                    dve.tensor_reduce(maxima[:, at], rows[:, block_of(i, 3 * N)], X, ALU.max,
                                      apply_absolute_value=True).then_inc(ug_max, 1)

            parts_of_x(0)
            maxima_of(0)
            with dve.Fori(1, NB) as i:
                parts_of_x(i)
                maxima_of(i)
            dve.wait_ge(ug_max, 2 * NB)
            for at, scale, factor in ((slice(0, NB), SU, KU), (slice(NB, 2 * NB), SG, KG)):
                m = whole_max(maxima[:, at])
                link(dve, dve.tensor_scalar(col(TMP), m, col(SX), 1.0 / Q16, ALU.mult, ALU.mult))
                link(dve, dve.tensor_scalar(col(scale), col(TMP), TINY, None, ALU.max))
                link(dve, dve.reciprocal(col(TMP), col(scale)))
                link(dve, dve.tensor_scalar(col(factor), col(TMP), col(SX), None, ALU.mult))
            dve.nop().then_inc(factor_done, 1)

            def gate_value(i):
                at = gate_s[:, block_of(i, 3 * N)]
                dve.wait_ge(gt_done, i + 1)
                dve.tensor_scalar(at, at, MAGIC, col(SG), ALU.subtract, ALU.mult).then_inc(g_done, 1)

            def gated_sig(i, b):
                at = gate_s[:, block_of(i, 3 * N)]
                dve.wait_ge(sig_done, i + 1)
                dve.tensor_scalar(sig_s[:, b, :], sig_s[:, b, :], 65535.0 / 65536.0, MAGIC16, ALU.min,
                                  ALU.add).then_inc(sig_rounded, 1)
                dve.wait_ge(sig_rounded, i + 1)
                dve.scalar_tensor_tensor(out=at, in0=sig_s[:, b, :], scalar=MAGIC16, in1=at,
                                         op0=ALU.subtract, op1=ALU.mult).then_inc(gs_done, 1)
                dve.wait_ge(gs_done, i + 1)
                dve.tensor_reduce(maxima[:, block_of(i, 1)], at, X, ALU.max,
                                  apply_absolute_value=True).then_inc(gs_max, 1)

            gate_value(0)
            gate_value(1)
            gated_sig(0, 0)
            with dve.Fori(1, NB // 2) as i:
                gate_value(2 * i)
                gated_sig(2 * i - 1, 1)
                gate_value(2 * i + 1)
                gated_sig(2 * i, 0)
            gated_sig(NB - 1, 1)
            dve.wait_ge(gs_max, NB)
            m = whole_max(maxima[:, 0:NB])
            link(dve, dve.tensor_scalar(col(SGS), m, 1.0 / Q16, TINY, ALU.mult, ALU.max))
            link(dve, dve.reciprocal(col(KGS), col(SGS)))
            dve.nop().then_inc(factor_done, 1)

            def outer(i):
                at, ups = gate_s[:, block_of(i, 3 * N)], up_s[:, block_of(i, 3 * N)]
                dve.wait_ge(gst_done, i + 1)
                dve.tensor_scalar(at, at, MAGIC, None, ALU.subtract).then_inc(g2_done, 1)
                dve.wait_ge(g2_done, i + 1)
                dve.wait_ge(ut_done, i + 1)
                dve.scalar_tensor_tensor(out=at, in0=ups, scalar=MAGIC, in1=at, op0=ALU.subtract,
                                         op1=ALU.mult).then_inc(o_done, 1)
                dve.wait_ge(o_done, i + 1)
                dve.tensor_reduce(maxima[:, block_of(i, 1)], at, X, ALU.max,
                                  apply_absolute_value=True).then_inc(o_max, 1)

            with dve.Fori(0, NB) as i:
                outer(i)
            dve.wait_ge(o_max, NB)
            m = whole_max(maxima[:, 0:NB])
            link(dve, dve.tensor_scalar(col(SGS), col(SGS), col(SU), None, ALU.mult))
            link(dve, dve.tensor_scalar(col(TMP), m, col(SGS), 1.0 / Q16, ALU.mult, ALU.mult))
            link(dve, dve.tensor_scalar(col(SO), col(TMP), TINY, None, ALU.max))
            link(dve, dve.reciprocal(col(TMP), col(SO)))
            dve.tensor_scalar(col(KO), col(TMP), col(SGS), None, ALU.mult).then_inc(factor_done, 1)
            dve.wait_ge(factor_done, 4)

            def recur(i, j):
                t = i * BS + j
                dve.wait_ge(rgate_done, t + 2)
                dve.scalar_tensor_tensor(out=uv[:, 0, :], in0=gact[:, 0, :], scalar=1.0,
                                         in1=xT[:, block_of(t, P)], op0=ALU.add,
                                         op1=ALU.mult).then_inc(ru_done, 1)
                dve.wait_ge(ru_done, t + 1)
                dve.scalar_tensor_tensor(out=uv[:, 1, :], in0=hT[:, block_of(t, P)], scalar=col(LEAK2),
                                         in1=uv[:, 0, :], op0=ALU.mult, op1=ALU.add).then_inc(rv_done, 1)

            def grid(ap):
                return ap.rearrange("p (s d) -> p s d", s=BS)

            def layer2(i, main=True, tail=True):
                if main:
                    at = gate_s[:, block_of(i, 3 * N)]
                    hi = oq_hi[:].rearrange("p c n -> p (c n)")
                    dve.wait_ge(ot_done, i + 1)
                    need(dve, o_mm, i)
                    dve.tensor_scalar(hi, at, MAGIC, None, ALU.subtract).then_inc(oq_hi_done, 1)
                    dve.wait_ge(oq_hi_done, i + 1)
                    dve.scalar_tensor_tensor(out=oq_lo[:].rearrange("p c n -> p (c n)"), in0=at, scalar=MAGIC,
                                             in1=hi.bitcast(F32), op0=ALU.subtract,
                                             op1=ALU.subtract).then_inc(oq_lo_done, 1)
                if tail:
                    recur(i - 1, 0)
                if main:
                    xb = xT[:, block_of(i)]
                    dve.wait_ge(o_mm, i + 1)
                    dve.scalar_tensor_tensor(out=xb, in0=GV[0][:, :], scalar=col(SO), in1=xb, op0=ALU.mult,
                                             op1=ALU.add).then_inc(x2T_done, 1)
                if tail:
                    recur(i - 1, 1)
                if main:
                    dve.wait_ge(l2_mm, i + 1)
                    need(dve, q1_done, i)
                    dve.tensor_tensor(norm2[:], grid(GV[1][:, :]), over(dmod[:], BS), ALU.mult).then_inc(norm_done, 1)
                    dve.wait_ge(norm_done, i + 1)
                    dve.tensor_reduce(lsc[:, 0:BS], norm2[:], X, ALU.max,
                                      apply_absolute_value=True).then_inc(nmax_done, 1)
                    dve.wait_ge(nmax_done, i + 1)
                    dve.tensor_scalar(lsc[:, 0:BS], lsc[:, 0:BS], TINY, 1.0 / 127.0, ALU.max,
                                      ALU.mult).then_inc(lscale_done, 1)
                    dve.wait_ge(lscale_done, i + 1)
                    dve.reciprocal(lsc[:, BS:2 * BS], lsc[:, 0:BS]).then_inc(linv_done, 1)
                    dve.wait_ge(q1_done, i + 1)
                    need(dve, q2T_mm, i)
                    dve.tensor_scalar(q2[:], norm2[:], MAGIC, MAGIC, ALU.add, ALU.subtract).then_inc(q2_done, 1)
                if tail:
                    recur(i - 1, 2)
                if main:
                    dve.wait_ge(acc_mm, i + 1)
                    need(dve, f2_done, i)
                    dve.tensor_tensor(f1[:], grid(GV[3][:, :]), wide(lsc[:, 0:BS], P), ALU.mult).then_inc(f1_done, 1)
                if tail:
                    recur(i - 1, 3)
                if main:
                    xb = xT[:, block_of(i)]
                    dve.wait_ge(fT_mm, i + 1)
                    dve.wait_ge(modx_done, i + 1)
                    dve.tensor_tensor(xb, Y[0][:, :], xb, ALU.add).then_inc(x3T_done, 1)

            layer2(0, tail=False)
            with dve.Fori(1, NB) as i:
                layer2(i)
            layer2(NB, main=False)

            dve.wait_ge(logit_mm, 1)
            link(dve, dve.tensor_copy(scores[:].rearrange("p s e -> p (s e)"), Z[:, 0:S * E]))
            ranks(pairs3[:], centred3)
            turned_sel = sel[:].rearrange("p e s -> p s e")
            link(dve, dve.tensor_scalar(turned_sel, wsel[:], 1.5, None, ALU.is_lt))
            link(dve, dve.tensor_tensor_scan(place[:].rearrange("p e s -> p (e s)"), cst("rows"),
                                             sel[:].rearrange("p e s -> p (e s)"), 0.0, ALU.mult, ALU.add))
            dve.tensor_copy(counts, place[:, :, S - 1]).then_inc(counts_done, 1)
            dve.wait_ge(exp3_done, 1)
            link(dve, dve.tensor_tensor(wsel[:], turned_sel, expo[:], ALU.mult))
            link(dve, dve.tensor_reduce(rowst[:, 1, :], wsel[:], X, ALU.add))
            link(dve, dve.reciprocal(rowst[:, 2, :], rowst[:, 1, :]))
            link(dve, dve.tensor_tensor(wsel[:], wsel[:], wide(rowst[:, 2, :], E), ALU.mult))
            dve.wait_ge(before_mm, 1)
            link(dve, dve.tensor_tensor(place[:], place[:], wide(Y[1][:, 0:E], S), ALU.add))
            link(dve, dve.scalar_tensor_tensor(out=wsel[:], in0=place[:].rearrange("p e s -> p s e"),
                                               scalar=float(CAP), in1=wsel[:], op0=ALU.is_le, op1=ALU.mult))
            dve.nop().then_inc(kept_done, 1)
            dve.wait_ge(w2_lo_done, 1)
            dve.wait_ge(x3_done, NB)

            def layer3(i, main=True, tail=True):
                for k in range(NK3):
                    n, e = i * NK3 + k, k // 2
                    if main:
                        dve.wait_ge(g3_mm, n + 1)
                        dve.wait_ge(gelu_done, n + 1)
                        need(dve, h3_lo_done, n - 1)
                        dve.tensor_tensor(hf3[:, k % 2, :], GV[2 * (k % 2) + 1][:, :], gelu3[:, k % 2, :],
                                          ALU.mult).then_inc(h3_done, 1)
                    if k % 2 == 1 and (main if e else tail):
                        m, f = i * E + e - 1, (e - 1) % E
                        at = steps_of(i) if e else steps_of(i - 1)
                        dve.wait_ge(down3_mm, m + 1)
                        need(dve, added3, m - 1)
                        dve.tensor_tensor(grid(scaled3[:, f % 2]), grid(Y[f % 2][:, :]),
                                          wsel[:, at, f:f + 1].broadcast_to([P, BS, P]),
                                          ALU.mult).then_inc(scaled3_done, 1)
                        if f == 0:
                            dve.wait_ge(scaled3_done, m + 1)
                            need(dve, out_done, 16 * i)
                            dve.tensor_tensor(x1rows[:], tok[:, at, :], grid(scaled3[:, 0]),
                                              ALU.add).then_inc(added3, 1)

            layer3(0, tail=False)
            with dve.Fori(1, NB) as i:
                layer3(i)
            layer3(NB, main=False)

        @block.gpsimd
        def _(pool):
            for k in range(NB):
                pool.wait_ge(h_done, k + 1)
                rows = tok[:, k * BS:(k + 1) * BS, :]
                nc.gpsimd.tensor_tensor(rows, rows, hrow[:, k % 2].rearrange("p (s d) -> p s d", s=BS),
                                        ALU.add).then_inc(r_done, 1)
            for e in range(E):
                pool.wait_ge(wu_hi_done, e + 1)
                nc.gpsimd.tensor_tensor(wu_lo[:, e, :], wup_raw[:, e, :], wu_hi[:, e, :].bitcast(F32),
                                        ALU.subtract).then_inc(wu_lo_done, 1)
            pool.wait_ge(wd_hi_done, 2)
            nc.gpsimd.tensor_tensor(wd_lo[:, :, 0:2, :], wdown_raw[:, :, 0:2, :],
                                    wd_hi[:, :, 0:2, :].bitcast(F32), ALU.subtract).then_inc(wd_lo_done, 1)
            nc.gpsimd.tensor_tensor(wd_lo[0:96, :, 2, :], wdown_raw[0:96, :, 2, :],
                                    wd_hi[0:96, :, 2, :].bitcast(F32), ALU.subtract).then_inc(wd_lo_done, 1)

            def low0(n, k):
                rows = CH0[k % 3][1]
                pool.wait_ge(h0_hi_done, n + 1)
                nc.gpsimd.tensor_tensor(h0_lo[0:rows, k % 4, :], hf0[0:rows, k % 2, :],
                                        h0_hi[0:rows, k % 4, :].bitcast(F32), ALU.subtract).then_inc(h0_lo_done, 1)

            def add0(m, f):
                pool.wait_ge(scaled_done, m + 1)
                pool.wait_ge(added, m)
                nc.gpsimd.tensor_tensor(x1rows[:], x1rows[:], scaled0[:, f % 2].rearrange(
                    "p (s d) -> p s d", s=BS), ALU.add).then_inc(added, 1)

            def layer0(i, main=True, tail=True):
                for k in range(NK0):
                    e = k // 3
                    if main if k else tail:
                        low0(i * NK0 + k - 1, (k - 1) % NK0)
                    if k % 3 == 2 and e != 1 and (main if e else tail):
                        add0(i * E + e - 1, (e - 1) % E)

            layer0(0, tail=False)
            with pool.Fori(1, NB) as i:
                layer0(i)
            layer0(NB, main=False)

            pool.wait_ge(factor_done, 2)
            for i in range(NB):
                at = up_s[:, block_of(i, 3 * N)]
                nc.gpsimd.tensor_scalar(at, at, col(KU), MAGIC, ALU.mult, ALU.add).then_inc(ut_done, 1)

            def layer2(i):
                pool.wait_ge(x2T_done, i + 1)
                need(pool, l2_mm, i)
                nc.gpsimd.tensor_tensor(modx[:], xT[:, block_of(i)].rearrange("p (s d) -> p s d", s=BS),
                                        over(ysT[:], BS), ALU.mult).then_inc(modx_done, 1)
                pool.wait_ge(linv_done, i + 1)
                nc.gpsimd.tensor_tensor(norm2[:], norm2[:], wide(lsc[:, BS:2 * BS], P), ALU.mult).then_inc(q1_done, 1)
                pool.wait_ge(f1_done, i + 1)
                need(pool, fT_mm, i)
                nc.gpsimd.tensor_tensor(f2[:], f1[:], over(rscale[:], BS), ALU.mult).then_inc(f2_done, 1)

            def low3(i):
                pool.wait_ge(hs_hi_done, i + 1)
                at = slice(i * N + P, (i + 1) * N + P) if isinstance(i, int) else bass.ds(i * N + P, N)
                nc.gpsimd.tensor_tensor(hs_lo[:, block_of(i)], hT[:, at], hs_hi[:, block_of(i)].bitcast(F32),
                                        ALU.subtract).then_inc(hs_lo_done, 1)

            layer2(0)
            with pool.Fori(1, NB) as i:
                layer2(i)
                low3(i - 1)
            low3(NB - 1)
            for e in range(E):
                pool.wait_ge(w1_hi_done, e + 1)
                nc.gpsimd.tensor_tensor(w1_lo[:, e, :], w1_raw[:, e, :], w1_hi[:, e, :].bitcast(F32),
                                        ALU.subtract).then_inc(w1_lo_done, 1)
            pool.wait_ge(w2_hi_done, 1)
            nc.gpsimd.tensor_tensor(w2_lo[:], w2_raw, w2_hi[:].bitcast(F32), ALU.subtract).then_inc(w2_lo_done, 1)

            def layer3(i, main=True, tail=True):
                for k in range(NK3):
                    e, n = k // 2, i * NK3 + k
                    if main if k else tail:
                        pool.wait_ge(h3_hi_done, n)
                        nc.gpsimd.tensor_tensor(h3_lo[:, (k - 1) % 4, :], hf3[:, (k - 1) % 2, :],
                                                h3_hi[:, (k - 1) % 4, :].bitcast(F32),
                                                ALU.subtract).then_inc(h3_lo_done, 1)
                    if k % 2 == 1 and e != 1 and (main if e else tail):
                        m, f = i * E + e - 1, (e - 1) % E
                        pool.wait_ge(scaled3_done, m + 1)
                        pool.wait_ge(added3, m)
                        nc.gpsimd.tensor_tensor(x1rows[:], x1rows[:],
                                                scaled3[:, f % 2].rearrange("p (s d) -> p s d", s=BS),
                                                ALU.add).then_inc(added3, 1)

            layer3(0, tail=False)
            with pool.Fori(1, NB) as i:
                layer3(i)
            layer3(NB, main=False)


def kernel(**inputs):
    import numpy as np
    import concourse.bacc as bacc
    from concourse.bass_utils import run_bass_kernel_spmd

    a = {k: np.asarray(v) for k, v in inputs.items()}
    cond = a["cond_1024"]
    L3W = a["L3_cond_W"]
    parts = {
        "condT": cond.T, "W1T": a["L0_cond_W1"].T, "W2T": a["L0_cond_W2"].T,
        "b2": np.broadcast_to(a["L0_cond_b2"], (P, P)), "l2w": a["L2_cond_weight"], "rhsT": a["L2_ffn_rhs"].T,
        "WhT": L3W[:, :P].T, "WzT": L3W[:, P:].T, "Wx": a["L1_cond_Wx"], "Wh": a["L1_cond_Wh"],
        "wrT": a["L0_ffn_w_router"].T, "WgT": a["L3_ffn_Wg"].T, "bl": a["L1_cond_b"].reshape(4, P).T,
        "b1": a["L0_cond_b1"][:, None], "nscale": a["L0_ffn_norm_scale"][:, None],
        "b3": a["L3_cond_b"][:, None], "alpha": a["L3_cond_alpha"][:, None]}
    ties = np.where(np.arange(E)[None, :] < np.arange(E)[:, None], -1.2e-38, 0.0)
    fixed = {
        "ident": np.eye(P), "before": np.triu(np.ones((P, P)), 1),
        "ties": np.broadcast_to(ties.reshape(1, -1), (P, E * E)),
        "rows": np.broadcast_to((np.arange(S * E) % S > 0)[None, :], (P, S * E)), "ones": np.ones((P, P))}
    arrays = {
        "x": a["x"],
        "params": np.concatenate([parts[n] for n, _ in PARAMS], axis=1),
        "consts": np.concatenate([fixed[n] for n, _ in CONSTS], axis=1).astype(np.float32),
        "w_up": a["L0_ffn_w_up"].transpose(2, 0, 1),
        "w_down": a["L0_ffn_w_down"].transpose(0, 2, 1),
        "l1w": np.concatenate([a["L1_ffn_w_up"].reshape(3, P, P).transpose(1, 0, 2).reshape(P, H1),
                               a["L1_ffn_w_gate"].reshape(3, P, P).transpose(1, 0, 2).reshape(P, H1),
                               a["L1_ffn_w_down"]], axis=1),
        "w1": a["L3_ffn_W1"].transpose(1, 0, 2),
        "w2": a["L3_ffn_W2"].reshape(E, 2, P, P).transpose(2, 0, 1, 3)}
    nc = bacc.Bacc("TRN2", target_bir_lowering=False, num_devices=1)
    args = []
    for name in arrays:
        arrays[name] = np.ascontiguousarray(arrays[name])
        args.append(nc.dram_tensor(f"in_{name}", arrays[name].shape, F32, kind="ExternalInput").ap())
    args.append(nc.dram_tensor("out", (P, S, P), F32, kind="ExternalOutput").ap())
    mixer_kernel(nc, *args)
    r = run_bass_kernel_spmd(nc, [{f"in_{n}": v for n, v in arrays.items()}], core_ids=[0])
    return r.results[0]["out"]
```

```python
from contextlib import ExitStack

import concourse.bass as bass
from concourse import mybir

F32 = mybir.dt.float32
F32R = mybir.dt.float32r
BF16 = mybir.dt.bfloat16
ALU = mybir.AluOpType
ACT = mybir.ActivationFunctionType
X = mybir.AxisListType.X

P = 128
S = 32
E = 8
BS = 4
NB = S // BS
N = BS * P
T = S * P
H0 = 352
H1 = 384
H3 = 256
CH0 = [(0, 128), (128, 128), (256, 96)]
CAP = int(T * 2 * 1.25 / E)
MAGIC = 1.5 * 2.0 ** 23
MAGIC16 = 192.0
Q16 = 32767.0
TINY = 1e-12

PARAMS = [("condT", 128), ("W1T", 128), ("W2T", 128), ("b2", 128), ("l2w", 128), ("rhsT", 128),
          ("WhT", 128), ("WzT", 128), ("Wh", 512), ("wrT", 8), ("WgT", 8), ("b1", 1), ("nscale", 1), ("b3", 1), ("alpha", 1)]
CONSTS = [("ident", 128), ("before", 128), ("ties", 64), ("rows", 256), ("ones", 128),
          ("pick", 8)]


def columns(parts):
    at, out = 0, {}
    for name, n in parts:
        out[name] = slice(at, at + n)
        at += n
    return out, at


PC, NPC = columns(PARAMS)
CC, NCC = columns(CONSTS)


def block_of(i, n=N):
    return slice(i * n, (i + 1) * n) if isinstance(i, int) else bass.ds(i * n, n)


def need(engine, semaphore, value):
    if not isinstance(value, int) or value > 0:
        engine.wait_ge(semaphore, value)


def mixer_kernel(nc, x, params, consts, wx, bl, w_up, w_down, l1w, w1, w2, out):
    ctx = ExitStack()
    with ctx:
        def keep(name, shape, dt=F32):
            return ctx.enter_context(nc.sbuf_tensor(name, shape, dt))

        def sem(name):
            return ctx.enter_context(nc.semaphore(name))

        xh = keep("xh", [P, T + T + P])
        par = keep("par", [P, NPC])
        con = keep("con", [P, NCC])
        gate1 = keep("gate1", [P, P])
        hid = keep("hid", [P, P])
        tiny = keep("tiny", [P, 64])
        wsel = keep("wsel", [P, S, E])
        scores = keep("scores", [P, S, E])
        expo = keep("expo", [P, S, E])
        rowst = keep("rowst", [P, 4, S])
        xacc = keep("xacc", [P, N])
        xs_hi, xs_lo = keep("xs_hi", [P, N], F32R), keep("xs_lo", [P, N], F32R)
        wx_hi, wx_lo = keep("wx_hi", [P, N], F32R), keep("wx_lo", [P, N], F32R)
        bl_hi, bl_lo = keep("bl_hi", [1, N], F32R), keep("bl_lo", [1, N], F32R)
        ones_r = keep("ones_r", [1, P], F32R)
        pick_r = keep("pick_r", [2 * E, E, P], F32R)
        wparts = keep("wparts", [P, S, 2 * E])
        wround = keep("wround", [P, S, E], F32R)
        wcur = keep("wcur", [P, BS, 2 * E])
        wT = keep("wT", [2 * E, N], F32R)
        state2 = keep("state2", [P, P])
        stateT = keep("stateT", [P, P])
        cell = keep("cell", [P, P])
        gact = keep("gact", [P, 4, P])
        uv = keep("uv", [P, 2, P])
        tcell = keep("tcell", [P, P])
        wscale = keep("wscale", [P, 2, 36])
        maxima = keep("maxima", [P, 2 * NB])
        xT = xh[:, 0:T]
        hT = xh[:, T:]

        def col(n):
            return tiny[:, n:n + 1]

        def prm(name):
            return par[:, PC[name]]

        def cst(name):
            return con[:, CC[name]]

        ident = cst("ident")
        EPS_RMS, MAG, EPS_L2 = range(3)
        B1H, B3H, LEAK2 = 8, 9, 10
        INVX, KU, KG, SG, KGS, SGS, KO, SO, SX, SU, TMP, TMP2, RSC = range(16, 29)

        banks = [ctx.enter_context(nc.psum_tensor(f"bank{i}", [P, 512], F32)) for i in range(8)]
        GV, Y, BC, Z, TP = banks[0:4], banks[4], banks[5], banks[6], banks[7]

        def layer(parts):
            made = ExitStack()
            got = [made.enter_context(nc.sbuf_tensor(n, s, d)) for n, s, d in parts]
            made.close()
            return got

        (xn_hi, xn_lo, wu_hi, wu_lo, wd_hi, wd_lo, work0, wr_hi, wr_lo, h0_hi, h0_lo) = layer([
            ("xn_hi", [P, T], F32R), ("xn_lo", [P, T], F32R),
            ("wu_hi", [P, E, 2 * H0], F32R), ("wu_lo", [P, E, 2 * H0], F32R),
            ("wd_hi", [P, E, 3, P], F32R), ("wd_lo", [P, E, 3, P], F32R),
            ("work0", [P, 6 * N], F32), ("wr_hi", [P, E], F32R), ("wr_lo", [P, E], F32R),
            ("h0_hi", [P, 4, N], F32R), ("h0_lo", [P, 4, N], F32R)])
        silu0, hf0 = (work0[:, k * 2 * N:(k + 1) * 2 * N].rearrange("p (b n) -> p b n", b=2)
                      for k in range(2))
        scaled0, bcast0 = work0[:, 4 * N:5 * N], work0[:, 5 * N:6 * N]
        *_, tok = layer([
            ("u1", [P, T], F32R), ("u2", [P, T], F32R), ("u3", [P, E, 2 * H0], F32R),
            ("u4", [P, E, 2 * H0], F32R), ("u5", [P, E, 3, P], F32R), ("u6", [P, E, 3, P], F32R),
            ("u7", [P, 6 * N], F32), ("u8", [P, E], F32R), ("u9", [P, E], F32R), ("tok", [P, S, P], F32)])
        wup_raw = xh[:, 0:E * 2 * H0].rearrange("p (e r) -> p e r", e=E)
        wdown_raw = work0[:].rearrange("p (e c d) -> p e c d", e=E, c=3)
        lines = xh[:, E * 2 * H0:E * 2 * H0 + 5 * N].rearrange("p (k n) -> p k n", k=5)
        hrow, xnrow, square = lines[:, 0:2], lines[:, 2:4], lines[:, 4]
        pairs = xh[:, E * 2 * H0:E * 2 * H0 + S * E * E].rearrange("p (s e f) -> p s e f", s=S, e=E)

        layer1 = ExitStack()
        (gate_s, sig_s, l1_hi, l1_lo, xq_hi, xq_lo) = [
            layer1.enter_context(nc.sbuf_tensor(n, s, d)) for n, s, d in [
                ("gate_s", [P, NB * 3 * N], F32), ("sig_s", [P, 2, 3 * N], F32),
                ("l1_hi", [P, 9, P], F32R), ("l1_lo", [P, 9, P], F32R),
                ("xq_hi", [P, N], F32R), ("xq_lo", [P, N], F32R)]]
        dmod, ysT, rscale, rhs_q, lsc = [
            layer1.enter_context(nc.sbuf_tensor(n, s, d)) for n, s, d in [
                ("dmod", [P, P], F32), ("ysT", [P, P], F32), ("rscale", [P, P], F32),
                ("rhs_q", [P, P], BF16), ("lsc", [P, 2 * BS], F32)]]
        up_s, = layer([("up_s", [P, NB * 3 * N], F32)])
        (oq_hi, oq_lo, modx, norm2, q2, qT, f1, f2, hs_hi, hs_lo) = layer([
            ("oq_hi", [P, 3, N], F32R), ("oq_lo", [P, 3, N], F32R), ("modx", [P, BS, P], F32),
            ("norm2", [P, BS, P], F32), ("q2", [P, BS, P], F32), ("qT", [P, N], BF16),
            ("f1", [P, BS, P], F32), ("f2", [P, BS, P], F32),
            ("hs_hi", [P, T], F32R), ("hs_lo", [P, T], F32R)])
        layer1.close()
        l1_raw = sig_s[:].rearrange("p b n -> p (b n)")[:, 0:9 * P]
        l1_q = sig_s[:].rearrange("p b n -> p (b n)")[:, 9 * P:18 * P]
        _, w1_raw, _, w2_raw = layer([
            ("w1_over", [P, E, 2 * H3], F32R), ("w1_raw", [P, E, 2 * H3], F32),
            ("w2_over", [P, E, 2, P], F32R), ("w2_raw", [P, E, 2, P], F32)])
        (w1_hi, w1_lo, w2_hi, w2_lo, work3, h3_hi, h3_lo, pairs3) = layer([
            ("w1_hi", [P, E, 2 * H3], F32R), ("w1_lo", [P, E, 2 * H3], F32R),
            ("w2_hi", [P, E, 2, P], F32R), ("w2_lo", [P, E, 2, P], F32R),
            ("work3", [P, 6 * N], F32), ("h3_hi", [P, 4, N], F32R), ("h3_lo", [P, 4, N], F32R),
            ("pairs3", [P, S, E, E], F32)])
        gelu3, hf3 = (work3[:, k * 2 * N:(k + 1) * 2 * N].rearrange("p (b n) -> p b n", b=2)
                      for k in range(2))
        scaled3, bcast3 = work3[:, 4 * N:5 * N], work3[:, 5 * N:6 * N]
        pairs_flat = pairs3[:].rearrange("p s e f -> p (s e f)")
        orow = pairs_flat[:, 0:N].rearrange("p (s d) -> p s d", s=BS)
        sel, place = (pairs_flat[:, k * S * E:(k + 1) * S * E].rearrange("p (e s) -> p e s", e=E) for k in (2, 3))
        counts = pairs_flat[:, 4 * S * E:4 * S * E + E]

        (params_in, consts_in, x_in, wdown_in, l1w_in, w1_in, w2_in) = map(
            sem, ["params_in", "consts_in", "x_in", "wdown_in", "l1w_in", "w1_in", "w2_in"])
        wx_in = sem("wx_in")
        (wx_scaled, wx_hi_done, wx_lo_done, picks_done, wcur_done, wturned, wT_done, bc_mm, bc_copied,
         x_turned, xT_done, xs_hi_done, xs_lo_done, h_turned, slot_done, state2_done) = map(sem, [
             "wx_scaled", "wx_hi_done", "wx_lo_done", "picks_done", "wcur_done", "wturned", "wT_done",
             "bc_mm", "bc_copied", "x_turned", "xT_done", "xs_hi_done", "xs_lo_done", "h_turned",
             "slot_done", "state2_done"])
        wcur3_done, wturned3, wT3_done, bc3_mm, bc3_copied, out_turned, orow_done = map(sem, [
            "wcur3_done", "wturned3", "wT3_done", "bc3_mm", "bc3_copied", "out_turned", "orow_done"])
        wup_in = [sem("wup_in_first"), sem("wup_in_last")]
        dve_step, eps_set = map(sem, ["dve_step", "eps_set"])
        (hidden_mm, hidden_done, gate_mm, gate_pre, gate_tanh, gate_done) = map(
            sem, ["hidden_mm", "hidden_done", "gate_mm", "gate_pre", "gate_tanh", "gate_done"])
        (h_done, square_done, sum_done, sqrt_done, xn_done, xnT_mm, xn_hi_done, xn_lo_done,
         r_done) = map(sem, ["h_done", "square_done", "sum_done", "sqrt_done", "xn_done", "xnT_mm",
                             "xn_hi_done", "xn_lo_done", "r_done"])
        wu_hi_done, wu_lo_done, wd_hi_done, wd_lo_done, wr_hi_done, wr_lo_done = map(
            sem, ["wu_hi_done", "wu_lo_done", "wd_hi_done", "wd_lo_done", "wr_hi_done", "wr_lo_done"])
        score_mm, scores_read, centred, exp_done = map(
            sem, ["score_mm", "scores_read", "centred", "exp_done"])
        (g_mm, v_mm, silu_done, h0_done, h0_hi_done, h0_lo_done, down_mm, scaled_done, added,
         turned, x1T_done) = map(sem, ["g_mm", "v_mm", "silu_done", "h0_done", "h0_hi_done",
                                       "h0_lo_done", "down_mm", "scaled_done", "added", "turned",
                                       "x1T_done"])
        z_mm, gates_done, uv_done, cell_done, tcell_done, state_done, hmax_done = map(
            sem, ["z_mm", "gates_done", "uv_done", "cell_done", "tcell_done", "state_done", "hmax_done"])
        l1q_done, l1T_mm, l1_hi_done, l1_lo_done = map(sem, ["l1q_done", "l1T_mm", "l1_hi_done", "l1_lo_done"])
        prep_in, prep_mm, prep_act, prep_read, bias_done, kept_done, wh_halved = map(
            sem, ["prep_in", "prep_mm", "prep_act", "prep_read", "bias_done", "kept_done", "wh_halved"])
        max_col, max_turned, max_row, max_mm, factor_done = map(
            sem, ["max_col", "max_turned", "max_row", "max_mm", "factor_done"])
        (xt_done, xq_hi_done, xq_lo_done, ug_mm, ug_copied, ug_max) = map(
            sem, ["xt_done", "xq_hi_done", "xq_lo_done", "ug_mm", "ug_copied", "ug_max"])
        (gt_done, g_done, sig_done, sig_rounded, gs_done, gs_max, ut_done) = map(
            sem, ["gt_done", "g_done", "sig_done", "sig_rounded", "gs_done", "gs_max", "ut_done"])
        gst_done, g2_done, o_done, o_max = map(sem, ["gst_done", "g2_done", "o_done", "o_max"])
        (ot_done, oq_hi_done, oq_lo_done, o_mm, x2T_done, modx_done, l2_mm, norm_done, nmax_done,
         lscale_done, linv_done, q1_done, q2_done, q2T_mm, qT_done, acc_mm, f1_done, f2_done,
         fT_mm, x3T_done) = map(sem, [
             "ot_done", "oq_hi_done", "oq_lo_done", "o_mm", "x2T_done", "modx_done", "l2_mm",
             "norm_done", "nmax_done", "lscale_done", "linv_done", "q1_done", "q2_done", "q2T_mm",
             "qT_done", "acc_mm", "f1_done", "f2_done", "fT_mm", "x3T_done"])
        (rz_mm, rgate_done, ru_done, rv_done, rstate_done, hs_hi_done, hs_lo_done) = map(sem, [
            "rz_mm", "rgate_done", "ru_done", "rv_done", "rstate_done", "hs_hi_done", "hs_lo_done"])
        (logit_mm, counts_done, before_mm) = map(sem, [
            "logit_mm", "counts_done", "before_mm"])
        w1_hi_done, w1_lo_done, w2_hi_done, w2_lo_done = map(
            sem, ["w1_hi_done", "w1_lo_done", "w2_hi_done", "w2_lo_done"])
        (i3_mm, g3_mm, gelu_done, h3_done, h3_hi_done, h3_lo_done, down3_mm, scaled3_done,
         added3, out_done) = map(sem, ["i3_mm", "g3_mm", "gelu_done", "h3_done", "h3_hi_done",
                                       "h3_lo_done", "down3_mm", "scaled3_done", "added3", "out_done"])

        steps = [0]

        def link(dve, ins):
            steps[0] += 1
            ins.then_inc(dve_step, 1)
            dve.wait_ge(dve_step, steps[0])

        LSTM_AT = [7, 11, 15, 19]
        NK0 = 3 * E
        NK3 = 2 * E

        def wide(ap, n):
            return ap.unsqueeze(2).broadcast_to([P, ap.shape[1], n])

        def over(ap, n):
            return ap.unsqueeze(1).broadcast_to([P, n, ap.shape[1]])

        def steps_of(i):
            return block_of(i, BS)

        block = ctx.enter_context(nc.Block())

        @block.sync
        def _(sp):
            sp.dma_start(par[:], params).then_inc(params_in, 16)
            sp.dma_start(tok[:], x).then_inc(x_in, 16)
            sp.dma_start(con[:], consts).then_inc(consts_in, 16)
            sp.dma_start(xacc[:], wx).then_inc(wx_in, 16)
            sp.dma_start(gact[0:1].rearrange("p g d -> p (g d)"), bl).then_inc(wx_in, 16)
            for e in range(E):
                sp.dma_start(wup_raw[:, e, :], w_up[:, e, :]).then_inc(wup_in[e // 4], 16)
            for c, (row, rows) in enumerate(CH0):
                sp.dma_start(wdown_raw[0:rows, :, c, :],
                             w_down[:, row:row + rows, :].rearrange("e p d -> p e d")).then_inc(wdown_in, 16)
            sp.wait_ge(added, NB * E)
            sp.dma_start(l1_raw, l1w).then_inc(l1w_in, 16)
            sp.wait_ge(oq_lo_done, -(-2 * E * 2 * H3 // (3 * N)))
            sp.dma_start(w1_raw[:], w1).then_inc(w1_in, 16)
            sp.wait_ge(oq_lo_done, NB)
            sp.dma_start(w2_raw[:], w2).then_inc(w2_in, 16)
            for i in range(NB):
                sp.wait_ge(orow_done, i + 1)
                sp.dma_start(out[:, i * BS:(i + 1) * BS, :], orow).then_inc(out_done, 16)
            sp.wait_ge(out_done, 16 * NB + 1)

        @block.tensor
        def _(pe):
            pe.wait_ge(params_in, 16)
            pe.matmul(GV[0][:, 0:P], prm("W1T"), prm("condT"), start=True, stop=True).then_inc(hidden_mm, 1)
            pe.wait_ge(hidden_done, 1)
            pe.matmul(GV[1][:, 0:P], hid[:], prm("W2T"), start=True, stop=True).then_inc(gate_mm, 1)
            pe.wait_ge(consts_in, 16)
            pe.wait_ge(wr_lo_done, 1)
            for k in range(NB + 1):
                if k < NB:
                    pe.wait_ge(xn_done, k + 1)
                    need(pe, xn_lo_done, k - 1)
                    for j in range(BS):
                        m = pe.transpose(GV[2 + k % 2][:, j * P:(j + 1) * P],
                                         xnrow[:, k % 2, j * P:(j + 1) * P], ident)
                    m.then_inc(xnT_mm, 1)
                if k >= 1:
                    pe.wait_ge(xn_lo_done, k)
                    for t in range((k - 1) * BS, k * BS):
                        at, to = slice(t * P, (t + 1) * P), Z[:, t * E:(t + 1) * E]
                        pe.matmul(to, xn_hi[:, at], wr_hi[:], start=True, stop=False)
                        pe.matmul(to, xn_hi[:, at], wr_lo[:], start=False, stop=False)
                        m = pe.matmul(to, xn_lo[:, at], wr_hi[:], start=False, stop=True)
            m.then_inc(score_mm, 1)

            def product(to, a_hi, a_lo, b_hi, b_lo, start=True, stop=True):
                pe.matmul(to, a_hi, b_hi, start=start, stop=False)
                pe.matmul(to, a_hi, b_lo, start=False, stop=False)
                return pe.matmul(to, a_lo, b_hi, start=False, stop=stop)

            def up0(i, e, c):
                k = 3 * e + c
                row, rows = CH0[c]
                need(pe, h0_done, i * NK0 + k - 1)
                for bank, first, signal in ((GV[2 * (k % 2)], H0, g_mm), (GV[2 * (k % 2) + 1], 0, v_mm)):
                    at = slice(first + row, first + row + rows)
                    product(bank[0:rows, :], wu_hi[:, e, at], wu_lo[:, e, at], xn_hi[:, block_of(i)],
                            xn_lo[:, block_of(i)]).then_inc(signal, 1)

            def weigh0(m, e):
                need(pe, bc_copied, m)
                pe.matmul(BC[:, :], pick_r[:, e, :], wT[:], start=True, stop=True).then_inc(bc_mm, 1)

            def down0(m, e):
                pe.wait_ge(h0_lo_done, 3 * m + 3)
                need(pe, scaled_done, m)
                for c, (row, rows) in enumerate(CH0):
                    r = (3 * e + c) % 4
                    last = product(Y[:, :], wd_hi[0:rows, e, c, :], wd_lo[0:rows, e, c, :],
                                   h0_hi[0:rows, r, :], h0_lo[0:rows, r, :], start=(c == 0), stop=(c == 2))
                last.then_inc(down_mm, 1)

            def turn_weights(done, signal, i):
                pe.wait_ge(done, i + 1)
                for j in range(BS):
                    last = pe.transpose(TP[0:2 * E, j * P:(j + 1) * P], wcur[:, j, :], ident)
                last.then_inc(signal, 1)

            def lstm_step(i, j):
                t = (i - 1) * BS + j
                at = slice(j * P, (j + 1) * P)
                if j == 0:
                    pe.wait_ge(xs_lo_done, i)
                pe.wait_ge(gates_done, t + 1)
                pe.matmul(Z[:, :], ones_r[:], bl_hi[:], start=True, stop=False)
                pe.matmul(Z[:, :], ones_r[:], bl_lo[:], start=False, stop=False)
                product(Z[:, :], xs_hi[:, at], xs_lo[:, at], wx_hi[:], wx_lo[:], start=False, stop=False)
                pe.wait_ge(state_done, t + 1)
                pe.matmul(Z[:, :], stateT[:], prm("Wh"), start=False, stop=True).then_inc(z_mm, 1)

            def turn_state(i, j):
                pe.wait_ge(state2_done, (i - 1) * BS + j + 1)
                pe.transpose(TP[:, 0:P], state2[:], ident).then_inc(h_turned, 1)

            def layer0(i, main=True, tail=True):
                for k in range(NK0):
                    e, c = k // 3, k % 3
                    if main:
                        up0(i, e, c)
                    if c == 1 and (main if e else tail):
                        if e == 1:
                            pe.wait_ge(wT_done, i + 1)
                        weigh0(i * E + e - 1, (e - 1) % E)
                        down0(i * E + e - 1, (e - 1) % E)
                    if main and k == 2:
                        need(pe, slot_done, BS * (i - 1) + 1)
                        turn_weights(wcur_done, wturned, i)
                    if tail and k in LSTM_AT:
                        lstm_step(i, LSTM_AT.index(k))
                    if tail and k - 2 in LSTM_AT:
                        turn_state(i, LSTM_AT.index(k - 2))

            for i in range(NB):
                pe.wait_ge(wu_lo_done, E)
                pe.wait_ge(r_done, NB)
                need(pe, xT_done, i - 1)
                for j in range(BS):
                    last = pe.transpose(GV[i % 2][:, j * P:(j + 1) * P], tok[:, i * BS + j, :], ident)
                last.then_inc(x_turned, 1)
            pe.wait_ge(xT_done, NB)
            pe.wait_ge(picks_done, 1)
            pe.wait_ge(wx_lo_done, 2)
            pe.wait_ge(wh_halved, 1)
            pe.wait_ge(wu_lo_done, E)
            pe.wait_ge(wd_lo_done, 2)
            pe.wait_ge(scores_read, 1)
            layer0(0, tail=False)
            with pe.Fori(1, NB) as i:
                layer0(i)
            layer0(NB, main=False)

            pe.wait_ge(l1q_done, 1)
            for n in range(9):
                if n >= 4:
                    pe.wait_ge(l1_lo_done, n - 3)
                pe.transpose(GV[n % 4][:, 0:P], l1_q[:, n * P:(n + 1) * P], ident).then_inc(l1T_mm, 1)
            pe.wait_ge(prep_in, 1)
            pe.matmul(Y[:, 0:P], f1[:, 0, :], f1[:, 1, :], start=True, stop=True)
            pe.transpose(Y[:, P:2 * P], f1[:, 2, :], ident)
            pe.matmul(Y[:, 2 * P:3 * P], col(RSC).broadcast_to([P, P]), ident,
                      start=True, stop=True).then_inc(prep_mm, 1)

            spread = [0]

            def spread_max():
                spread[0] += 1
                n = spread[0]
                pe.wait_ge(max_col, n)
                pe.transpose(TP[0:1, 0:P], col(TMP), ident).then_inc(max_turned, 1)
                pe.wait_ge(max_row, n)
                pe.matmul(TP[:, P:P + 1], cst("ones")[0:1, :], tiny[0:1, TMP2:TMP2 + 1],
                          start=True, stop=True).then_inc(max_mm, 1)

            spread_max()

            def up_gate(i):
                pe.wait_ge(xq_lo_done, i + 1)
                for c in range(6):
                    need(pe, ug_copied, i * 6 + c - 5)
                    product(banks[c][:, :], l1_hi[:, c, :], l1_lo[:, c, :],
                            xq_hi[:], xq_lo[:]).then_inc(ug_mm, 1)

            pe.wait_ge(l1_lo_done, 9)
            pe.wait_ge(prep_read, 1)
            up_gate(0)
            with pe.Fori(1, NB) as i:
                up_gate(i)
            for _ in range(4):
                spread_max()

            def tile(bank, j):
                return bank[:, j * P:(j + 1) * P]

            def recur(i, j):
                t = i * BS + j
                if j == 0:
                    pe.wait_ge(x3T_done, i + 1)
                    pe.wait_ge(rgate_done, i * BS + 1)
                    pe.matmul(Z[:, :], prm("WzT"), xT[:, block_of(i)], start=True, stop=False,
                              skip_group_check=True)
                pe.wait_ge(rstate_done, t + 1)
                pe.matmul(tile(Z, j), prm("WhT"), hT[:, block_of(t, P)], start=False, stop=(j == 3),
                          skip_group_check=True).then_inc(rz_mm, 1)

            def layer2(i, main=True, tail=True):
                if main:
                    pe.wait_ge(oq_lo_done, i + 1)
                    need(pe, x2T_done, i)
                    for c in range(3):
                        last = product(GV[0][:, :], l1_hi[:, 6 + c, :], l1_lo[:, 6 + c, :], oq_hi[:, c, :],
                                       oq_lo[:, c, :], start=(c == 0), stop=(c == 2))
                    last.then_inc(o_mm, 1)
                if tail:
                    recur(i - 1, 0)
                if main:
                    pe.wait_ge(modx_done, i + 1)
                    for j in range(BS):
                        last = pe.matmul(tile(GV[1], j), modx[:, j, :], prm("l2w"), start=True, stop=True)
                    last.then_inc(l2_mm, 1)
                if tail:
                    recur(i - 1, 1)
                if main:
                    pe.wait_ge(q2_done, i + 1)
                    for j in range(BS):
                        last = pe.transpose(tile(GV[2], j), q2[:, j, :], ident)
                    last.then_inc(q2T_mm, 1)
                if tail:
                    recur(i - 1, 2)
                if main:
                    pe.wait_ge(qT_done, i + 1)
                    for j in range(BS):
                        last = pe.matmul(tile(GV[3], j), qT[:, j * P:(j + 1) * P], rhs_q[:], start=True, stop=True)
                    last.then_inc(acc_mm, 1)
                if tail:
                    recur(i - 1, 3)
                if main:
                    pe.wait_ge(f2_done, i + 1)
                    for j in range(BS):
                        last = pe.transpose(tile(Y, j), f2[:, j, :], ident)
                    last.then_inc(fT_mm, 1)

            layer2(0, tail=False)
            with pe.Fori(1, NB) as i:
                layer2(i)
            layer2(NB, main=False)

            pe.wait_ge(rstate_done, S + 1)
            pe.wait_ge(rgate_done, S + 1)
            for t in range(S):
                last = pe.matmul(Z[:, t * E:(t + 1) * E], hT[:, (t + 1) * P:(t + 2) * P], prm("WgT"),
                                 start=True, stop=True)
            last.then_inc(logit_mm, 1)
            pe.wait_ge(counts_done, 1)
            pe.matmul(BC[:, 0:E], cst("before"), counts, start=True, stop=True).then_inc(before_mm, 1)
            def up3(i, e, c):
                k = 2 * e + c
                need(pe, h3_done, i * NK3 + k - 1)
                for bank, first, signal in ((GV[2 * (k % 2)], 0, i3_mm), (GV[2 * (k % 2) + 1], H3, g3_mm)):
                    at = slice(first + c * P, first + (c + 1) * P)
                    product(bank[:, :], w1_hi[:, e, at], w1_lo[:, e, at], hs_hi[:, block_of(i)],
                            hs_lo[:, block_of(i)]).then_inc(signal, 1)

            def weigh3(m, e):
                need(pe, bc3_copied, m)
                pe.matmul(BC[:, :], pick_r[:, e, :], wT[:], start=True, stop=True).then_inc(bc3_mm, 1)

            def down3(m, e):
                pe.wait_ge(h3_lo_done, 2 * m + 2)
                need(pe, scaled3_done, m)
                for c in range(2):
                    r = (2 * e + c) % 4
                    last = product(Y[:, :], w2_hi[:, e, c, :], w2_lo[:, e, c, :], h3_hi[:, r, :], h3_lo[:, r, :],
                                   start=(c == 0), stop=(c == 1))
                last.then_inc(down3_mm, 1)

            def layer3(i, main=True, tail=True):
                for k in range(NK3):
                    e, c = k // 2, k % 2
                    if main:
                        up3(i, e, c)
                    if tail and k == 3:
                        pe.wait_ge(added3, E * i)
                        for j in range(BS):
                            last = pe.transpose(tile(Z, j), xacc[:, j * P:(j + 1) * P], ident)
                        last.then_inc(out_turned, 1)
                    if c == 1 and (main if e else tail):
                        if e == 1:
                            pe.wait_ge(wT3_done, i + 1)
                        weigh3(i * E + e - 1, (e - 1) % E)
                        down3(i * E + e - 1, (e - 1) % E)
                    if main and k == 2:
                        turn_weights(wcur3_done, wturned3, i)

            pe.wait_ge(w2_lo_done, 1)
            pe.wait_ge(w1_lo_done, E)
            pe.wait_ge(hs_lo_done, NB)
            pe.wait_ge(kept_done, 1)
            layer3(0, tail=False)
            with pe.Fori(1, NB) as i:
                layer3(i)
            layer3(NB, main=False)

        @block.scalar
        def _(act):
            act.wait_ge(params_in, 16)
            nc.scalar.mul(col(B3H), prm("b3"), 0.5).then_inc(bias_done, 1)
            act.wait_ge(hidden_mm, 1)
            nc.scalar.activation(hid[:], GV[0][:, 0:P], ACT.Silu, bias=prm("b1")).then_inc(hidden_done, 1)
            act.wait_ge(gate_pre, 1)
            nc.scalar.activation(gate1[:], gate1[:], ACT.Tanh, scale=0.5).then_inc(gate_tanh, 1)
            nc.scalar.copy(wr_hi[:], prm("wrT")).then_inc(wr_hi_done, 1)
            act.wait_ge(consts_in, 16)
            nc.scalar.copy(pick_r[:], cst("pick")[0:2 * E].unsqueeze(2).broadcast_to([2 * E, E, P]))
            nc.scalar.copy(ones_r[:], cst("ones")[0:1, :]).then_inc(picks_done, 1)
            act.wait_ge(wx_scaled, 2)
            nc.scalar.copy(wx_hi[:], xacc[:]).then_inc(wx_hi_done, 1)
            nc.scalar.copy(bl_hi[:], gact[0:1].rearrange("p g d -> p (g d)")).then_inc(wx_hi_done, 1)
            act.wait_ge(eps_set, 1)
            for k in range(NB + 1):
                if k < NB:
                    act.wait_ge(h_done, k + 1)
                    need(act, sum_done, k)
                    nc.scalar.activation(square, hrow[:, k % 2], ACT.Square).then_inc(square_done, 1)
                    act.wait_ge(sum_done, k + 1)
                    nc.scalar.activation(rowst[:, 3, k * BS:(k + 1) * BS], rowst[:, 3, k * BS:(k + 1) * BS],
                                         ACT.Sqrt, scale=1.0 / P, bias=col(EPS_RMS)).then_inc(sqrt_done, 1)
                if k >= 1:
                    act.wait_ge(xnT_mm, k)
                    nc.scalar.activation(xn_hi[:, block_of(k - 1)], GV[2 + (k - 1) % 2][:, :], ACT.Copy,
                                         scale=prm("nscale")).then_inc(xn_hi_done, 1)
            for e in range(E):
                act.wait_ge(wup_in[e // 4], 64)
                nc.scalar.copy(wu_hi[:, e, :], wup_raw[:, e, :]).then_inc(wu_hi_done, 1)
            act.wait_ge(wdown_in, 48)
            nc.scalar.copy(wd_hi[:, :, 0:2, :], wdown_raw[:, :, 0:2, :]).then_inc(wd_hi_done, 1)
            nc.scalar.copy(wd_hi[0:96, :, 2, :], wdown_raw[0:96, :, 2, :]).then_inc(wd_hi_done, 1)
            act.wait_ge(centred, 1)
            nc.scalar.activation(expo[:], expo[:], ACT.Exp).then_inc(exp_done, 1)
            nc.scalar.mul(stateT[:], prm("condT"), 2.0).then_inc(state_done, 1)
            act.nop().then_inc(gates_done, 1)
            act.wait_ge(wu_lo_done, E)
            for i in range(NB):
                act.wait_ge(x_turned, i + 1)
                nc.scalar.copy(xT[:, block_of(i)], GV[i % 2][:, :]).then_inc(xT_done, 1)
            act.wait_ge(wd_lo_done, 2)

            def high0(n, k):
                rows = CH0[k % 3][1]
                act.wait_ge(h0_done, n + 1)
                return nc.scalar.copy(h0_hi[0:rows, k % 4, :], hf0[0:rows, k % 2, :]).then_inc(h0_hi_done, 1)

            def gates(i, j):
                act.wait_ge(z_mm, (i - 1) * BS + j + 1)
                nc.scalar.activation(gact[:].rearrange("p g d -> p (g d)"), Z[:, :], ACT.Tanh,
                                     scale=0.5).then_inc(gates_done, 1)

            def cell_tanh(i, j):
                t = (i - 1) * BS + j
                act.wait_ge(cell_done, t + 2)
                nc.scalar.activation(tcell[:], cell[:], ACT.Tanh, scale=0.5).then_inc(tcell_done, 1)

            def layer0(i, main=True, tail=True):
                for k in range(NK0):
                    n = i * NK0 + k
                    rows = CH0[k % 3][1]
                    if main:
                        act.wait_ge(g_mm, n + 1)
                        need(act, h0_done, n - 1)
                        nc.scalar.activation(silu0[0:rows, k % 2, :], GV[2 * (k % 2)][0:rows, :],
                                             ACT.Silu).then_inc(silu_done, 1)
                    if main if k else tail:
                        need(act, down_mm, i * E + (k - 5) // 3 + 1)
                        high0(n - 1, (k - 1) % NK0)
                    if k % 3 == 1 and (main if k > 1 else tail):
                        m = i * E + k // 3 - 1
                        act.wait_ge(bc_mm, m + 1)
                        need(act, scaled_done, m)
                        nc.scalar.copy(bcast0, BC[:, :]).then_inc(bc_copied, 1)
                    if main and k == 2:
                        act.wait_ge(wturned, i + 1)
                        nc.scalar.copy(wT[:], TP[0:2 * E, :]).then_inc(wT_done, 1)
                    if tail and k == 4:
                        act.wait_ge(added, i * E)
                        nc.scalar.copy(xs_hi[:], xacc[:]).then_inc(xs_hi_done, 1)
                        nc.scalar.copy(xT[:, block_of(i - 1)], xacc[:]).then_inc(x1T_done, 1)
                    if tail and k in LSTM_AT:
                        gates(i, LSTM_AT.index(k))
                    if tail and k - 1 in LSTM_AT:
                        cell_tanh(i, LSTM_AT.index(k - 1))

            layer0(0, tail=False)
            with act.Fori(1, NB) as i:
                layer0(i)
            layer0(NB, main=False)

            for n in range(9):
                act.wait_ge(l1T_mm, n + 1)
                nc.scalar.copy(l1_hi[:, n, :], GV[n % 4][:, 0:P]).then_inc(l1_hi_done, 1)
            act.wait_ge(prep_mm, 1)
            nc.scalar.activation(dmod[:], Y[:, 0:P], ACT.Sqrt, bias=col(EPS_L2))
            nc.scalar.copy(rhs_q[:], Y[:, P:2 * P])
            nc.scalar.copy(rscale[:], Y[:, 2 * P:3 * P]).then_inc(prep_act, 1)

            act.wait_ge(factor_done, 1)

            def states(i):
                at = hT[:, bass.ds(i * N + P, N)] if not isinstance(i, int) else hT[:, P + i * N:P + (i + 1) * N]
                nc.scalar.activation(at, at, ACT.Identity, scale=col(INVX), bias=col(MAG)).then_inc(xt_done, 1)

            def keep_ug(i):
                for c in range(6):
                    act.wait_ge(ug_mm, i * 6 + c + 1)
                    to, r = (up_s, c) if c < 3 else (gate_s, c - 3)
                    at = slice((i * 3 + r) * N, (i * 3 + r + 1) * N) if isinstance(i, int) else \
                        bass.ds((i * 3 + r) * N, N)
                    nc.scalar.copy(to[:, at], banks[c][:, :]).then_inc(ug_copied, 1)

            states(0)
            with act.Fori(0, NB - 1) as i:
                states(i + 1)
                keep_ug(i)
            keep_ug(NB - 1)

            def rounded(i, scale, signal):
                at = gate_s[:, block_of(i, 3 * N)]
                nc.scalar.activation(at, at, ACT.Identity, scale=col(scale), bias=col(MAG)).then_inc(signal, 1)

            def sigmoid(i, b):
                act.wait_ge(g_done, i + 1)
                need(act, gs_done, i - 1)
                nc.scalar.activation(sig_s[:, b, :], gate_s[:, block_of(i, 3 * N)],
                                     ACT.Sigmoid).then_inc(sig_done, 1)

            act.wait_ge(factor_done, 2)
            rounded(0, KG, gt_done)
            for i in range(NB):
                if i + 1 < NB:
                    rounded(i + 1, KG, gt_done)
                sigmoid(i, i % 2)
            act.wait_ge(factor_done, 3)
            with act.Fori(0, NB) as i:
                rounded(i, KGS, gst_done)
            act.wait_ge(factor_done, 4)
            nc.scalar.copy(hT[:, 0:P], prm("condT")).then_inc(rstate_done, 1)
            act.nop().then_inc(rgate_done, 1)

            def recur(i, j):
                t = i * BS + j
                act.wait_ge(rz_mm, t + 1)
                nc.scalar.activation(gact[:, 0, :], Z[:, j * P:(j + 1) * P], ACT.Tanh, scale=0.5,
                                     bias=col(B3H)).then_inc(rgate_done, 1)
                act.wait_ge(rv_done, t + 1)
                nc.scalar.activation(hT[:, block_of(t + 1, P)], uv[:, 1, :], ACT.Tanh,
                                     scale=0.5).then_inc(rstate_done, 1)

            def layer2(i, main=True, tail=True):
                if main:
                    rounded(i, KO, ot_done)
                if tail:
                    recur(i - 1, 0)
                    recur(i - 1, 1)
                if main:
                    act.wait_ge(q2T_mm, i + 1)
                    nc.scalar.copy(qT[:], GV[2][:, :]).then_inc(qT_done, 1)
                if tail:
                    recur(i - 1, 2)
                    recur(i - 1, 3)
                    at = slice((i - 1) * N + P, i * N + P) if isinstance(i, int) else bass.ds((i - 1) * N + P, N)
                    act.wait_ge(rstate_done, i * BS + 1)
                    nc.scalar.copy(hs_hi[:, block_of(i - 1)], hT[:, at]).then_inc(hs_hi_done, 1)

            layer2(0, tail=False)
            with act.Fori(1, NB) as i:
                layer2(i)
            layer2(NB, main=False)

            act.wait_ge(centred, 2)
            nc.scalar.activation(expo[:], expo[:], ACT.Exp).then_inc(exp_done, 1)
            act.wait_ge(w1_in, 16)
            for e in range(E):
                nc.scalar.copy(w1_hi[:, e, :], w1_raw[:, e, :]).then_inc(w1_hi_done, 1)
            act.wait_ge(w2_in, 16)
            nc.scalar.copy(w2_hi[:], w2_raw[:]).then_inc(w2_hi_done, 1)
            act.nop().then_inc(out_done, 1)

            def layer3(i, main=True, tail=True):
                for k in range(NK3):
                    n = i * NK3 + k
                    if main:
                        act.wait_ge(i3_mm, n + 1)
                        need(act, h3_done, n - 1)
                        nc.scalar.activation(gelu3[:, k % 2, :], GV[2 * (k % 2)][:, :],
                                             ACT.Gelu).then_inc(gelu_done, 1)
                    if main if k else tail:
                        need(act, down3_mm, i * E + (k - 5) // 2 + 1)
                        act.wait_ge(h3_done, n)
                        nc.scalar.copy(h3_hi[:, (k - 1) % 4, :], hf3[:, (k - 1) % 2, :]).then_inc(h3_hi_done, 1)
                    if k % 2 == 1 and (main if k > 1 else tail):
                        m = i * E + k // 2 - 1
                        act.wait_ge(bc3_mm, m + 1)
                        need(act, scaled3_done, m)
                        nc.scalar.copy(bcast3, BC[:, :]).then_inc(bc3_copied, 1)
                    if main and k == 2:
                        act.wait_ge(wturned3, i + 1)
                        nc.scalar.copy(wT[:], TP[0:2 * E, :]).then_inc(wT3_done, 1)
                    if tail and k == 4:
                        act.wait_ge(out_turned, i)
                        act.wait_ge(out_done, 16 * (i - 1) + 1)
                        nc.scalar.copy(orow.rearrange("p s d -> p (s d)"), Z[:, :]).then_inc(orow_done, 1)

            layer3(0, tail=False)
            with act.Fori(1, NB) as i:
                layer3(i)
            layer3(NB, main=False)

        @block.vector
        def _(dve):
            dve.memset(col(EPS_RMS), 1e-6)
            dve.memset(col(MAG), MAGIC)
            dve.memset(col(EPS_L2), 1e-8)
            dve.memset(cell[:], 0.0).then_inc(cell_done, 1)
            dve.wait_ge(cell_done, 1)
            dve.nop().then_inc(eps_set, 1)
            dve.nop().then_inc(slot_done, 1)
            dve.wait_ge(params_in, 16)
            dve.wait_ge(gate_mm, 1)
            dve.tensor_tensor(gate1[:], GV[1][:, 0:P], prm("b2"), ALU.add).then_inc(gate_pre, 1)
            dve.wait_ge(gate_tanh, 1)
            dve.tensor_scalar(gate1[:], gate1[:], 0.5, 1.5, ALU.mult, ALU.add).then_inc(gate_done, 1)
            dve.wait_ge(gate_done, 1)
            dve.wait_ge(wr_hi_done, 1)
            dve.tensor_tensor(wr_lo[:], prm("wrT"), wr_hi[:].bitcast(F32), ALU.subtract).then_inc(wr_lo_done, 1)
            dve.tensor_scalar(prm("Wh")[:, 0:3 * P], prm("Wh")[:, 0:3 * P], 0.5, None, ALU.mult).then_inc(wh_halved, 1)
            dve.wait_ge(wx_in, 32)
            dve.tensor_scalar(xacc[:, 3 * P:], xacc[:, 3 * P:], 2.0, None, ALU.mult).then_inc(wx_scaled, 1)
            dve.tensor_scalar(gact[0:1, 3, :], gact[0:1, 3, :], 2.0, None, ALU.mult).then_inc(wx_scaled, 1)
            dve.wait_ge(wx_hi_done, 2)
            dve.tensor_tensor(wx_lo[:], xacc[:], wx_hi[:].bitcast(F32), ALU.subtract).then_inc(wx_lo_done, 1)
            dve.tensor_tensor(bl_lo[:], gact[0:1].rearrange("p g d -> p (g d)"), bl_hi[:].bitcast(F32),
                              ALU.subtract).then_inc(wx_lo_done, 1)
            dve.wait_ge(x_in, 16)

            def gated(k):
                need(dve, r_done, k - 1)
                need(dve, xn_done, k - 1)
                dve.tensor_tensor(hrow[:, k % 2].rearrange("p (s d) -> p s d", s=BS),
                                  tok[:, k * BS:(k + 1) * BS, :], over(gate1[:], BS),
                                  ALU.mult).then_inc(h_done, 1)

            gated(0)
            for k in range(NB + 1):
                if k + 1 < NB:
                    gated(k + 1)
                if k < NB:
                    at = rowst[:, 3, k * BS:(k + 1) * BS]
                    dve.wait_ge(square_done, k + 1)
                    dve.tensor_reduce(at, square.rearrange("p (s d) -> p s d", s=BS), X,
                                      ALU.add).then_inc(sum_done, 1)
                    dve.wait_ge(sqrt_done, k + 1)
                    link(dve, dve.reciprocal(at, at))
                    need(dve, xnT_mm, k - 1)
                    dve.tensor_tensor(xnrow[:, k % 2].rearrange("p (s d) -> p s d", s=BS),
                                      hrow[:, k % 2].rearrange("p (s d) -> p s d", s=BS), wide(at, P),
                                      ALU.mult).then_inc(xn_done, 1)
                if k >= 1:
                    dve.wait_ge(xn_hi_done, k)
                    dve.scalar_tensor_tensor(
                        out=xn_lo[:, block_of(k - 1)], in0=GV[2 + (k - 1) % 2][:, :], scalar=prm("nscale"),
                        in1=xn_hi[:, block_of(k - 1)].bitcast(F32), op0=ALU.mult,
                        op1=ALU.subtract).then_inc(xn_lo_done, 1)

            def ranks(pairs_at, signal):
                link(dve, dve.tensor_reduce(rowst[:, 0, :], scores[:], X, ALU.max))
                dve.tensor_tensor(expo[:], scores[:], wide(rowst[:, 0, :], E), ALU.subtract).then_inc(signal, 1)
                link(dve, dve.tensor_tensor(pairs_at, scores[:].unsqueeze(2).broadcast_to([P, S, E, E]),
                                            scores[:].unsqueeze(3).broadcast_to([P, S, E, E]), ALU.subtract))
                flat = pairs_at.rearrange("p s e f -> p s (e f)")
                link(dve, dve.tensor_tensor(flat, flat, over(cst("ties"), S), ALU.is_gt))
                link(dve, dve.tensor_reduce(wsel[:], pairs_at, X, ALU.add))


            def weight_parts():
                link(dve, dve.tensor_copy(wround[:], wsel[:]))
                link(dve, dve.tensor_copy(wparts[:, :, 0:E], wround[:].bitcast(F32)))
                link(dve, dve.tensor_tensor(wparts[:, :, E:], wsel[:], wround[:].bitcast(F32), ALU.subtract))

            dve.wait_ge(score_mm, 1)
            steps[0] += 1
            dve.tensor_copy(scores[:].rearrange("p s e -> p (s e)"), Z[:, 0:S * E]).then_inc(dve_step, 1)
            dve.wait_ge(dve_step, steps[0])
            dve.nop().then_inc(scores_read, 1)
            dve.wait_ge(r_done, NB)
            ranks(pairs, centred)
            dve.wait_ge(exp_done, 1)
            link(dve, dve.tensor_reduce(rowst[:, 1, :], expo[:], X, ALU.add))
            link(dve, dve.reciprocal(rowst[:, 2, :], rowst[:, 1, :]))
            link(dve, dve.scalar_tensor_tensor(out=wsel[:], in0=wsel[:], scalar=1.5, in1=expo[:],
                                               op0=ALU.is_lt, op1=ALU.mult))
            link(dve, dve.tensor_tensor(wsel[:], wsel[:], wide(rowst[:, 2, :], E), ALU.mult))
            weight_parts()
            dve.wait_ge(wd_lo_done, 2)
            dve.wait_ge(r_done, NB)

            def state_parts(i, j):
                t = (i - 1) * BS + j
                dve.wait_ge(gates_done, t + 2)
                dve.wait_ge(cell_done, t + 1)
                dve.scalar_tensor_tensor(out=uv[:, 0, :], in0=gact[:, 0, :], scalar=1.0, in1=gact[:, 3, :],
                                         op0=ALU.add, op1=ALU.mult).then_inc(uv_done, 1)
                dve.scalar_tensor_tensor(out=uv[:, 1, :], in0=gact[:, 1, :], scalar=1.0, in1=cell[:],
                                         op0=ALU.add, op1=ALU.mult).then_inc(uv_done, 1)
                dve.wait_ge(uv_done, 2 * t + 2)
                dve.scalar_tensor_tensor(out=cell[:], in0=uv[:, 1, :], scalar=0.5, in1=uv[:, 0, :],
                                         op0=ALU.mult, op1=ALU.add).then_inc(cell_done, 1)

            def state(i, j):
                dve.wait_ge(tcell_done, (i - 1) * BS + j + 1)
                dve.scalar_tensor_tensor(out=state2[:], in0=gact[:, 2, :], scalar=1.0, in1=tcell[:],
                                         op0=ALU.add, op1=ALU.mult).then_inc(state2_done, 1)

            def keep_state(i, j):
                t = (i - 1) * BS + j
                dve.wait_ge(h_turned, t + 1)
                dve.tensor_copy(stateT[:], TP[:, 0:P]).then_inc(state_done, 1)
                dve.tensor_copy(hT[:, block_of(t + 1, P)], TP[:, 0:P]).then_inc(slot_done, 1)

            def layer0(i, main=True, tail=True):
                for k in range(NK0):
                    n = i * NK0 + k
                    e, rows = k // 3, CH0[k % 3][1]
                    if main:
                        dve.wait_ge(v_mm, n + 1)
                        dve.wait_ge(silu_done, n + 1)
                        need(dve, h0_lo_done, n - 1)
                        dve.tensor_tensor(hf0[0:rows, k % 2, :], GV[2 * (k % 2) + 1][0:rows, :],
                                          silu0[0:rows, k % 2, :], ALU.mult).then_inc(h0_done, 1)
                    if k % 3 == 2 and (main if e else tail):
                        m, f = i * E + e - 1, (e - 1) % E
                        at = block_of(i)
                        dve.wait_ge(down_mm, m + 1)
                        dve.wait_ge(bc_copied, m + 1)
                        need(dve, added, m)
                        dve.tensor_tensor(scaled0, Y[:, :], bcast0, ALU.mult).then_inc(scaled_done, 1)
                        if f == 0:
                            dve.wait_ge(scaled_done, m + 1)
                            need(dve, x1T_done, i)
                            need(dve, xs_lo_done, i)
                            dve.tensor_tensor(xacc[:], xT[:, at], scaled0, ALU.add).then_inc(added, 1)
                    if main and k == 1:
                        need(dve, wturned, i)
                        dve.tensor_copy(wcur[:], wparts[:, steps_of(i), :]).then_inc(wcur_done, 1)
                    if tail and k in LSTM_AT:
                        state_parts(i, LSTM_AT.index(k))
                    if tail and k - 1 in LSTM_AT:
                        state(i, LSTM_AT.index(k - 1))
                    if tail and k - 2 in LSTM_AT:
                        keep_state(i, LSTM_AT.index(k - 2))
                    if tail and k == 22:
                        at = slice((i - 1) * N + P, i * N + P) if isinstance(i, int) else bass.ds((i - 1) * N + P, N)
                        dve.wait_ge(slot_done, i * BS + 1)
                        dve.tensor_reduce(maxima[:, block_of(i - 1, 1)], hT[:, at], X, ALU.max,
                                          apply_absolute_value=True).then_inc(hmax_done, 1)

            layer0(0, tail=False)
            with dve.Fori(1, NB) as i:
                layer0(i)
            layer0(NB, main=False)

            dve.wait_ge(l1w_in, 16)
            raw = l1_raw.rearrange("p (g k) -> p g k", k=32)
            qv = l1_q.rearrange("p (g k) -> p g k", k=32)
            link(dve, dve.tensor_reduce(wscale[:, 0, :], raw, X, ALU.max, apply_absolute_value=True))
            link(dve, dve.tensor_scalar(wscale[:, 0, :], wscale[:, 0, :], 1.0 / 7.0, TINY, ALU.mult, ALU.max))
            link(dve, dve.reciprocal(wscale[:, 1, :], wscale[:, 0, :]))
            link(dve, dve.tensor_tensor(qv, raw, wide(wscale[:, 1, :], 32), ALU.mult))
            link(dve, dve.tensor_scalar(l1_q, l1_q, MAGIC, MAGIC, ALU.add, ALU.subtract))
            dve.tensor_tensor(qv, qv, wide(wscale[:, 0, :], 32), ALU.mult).then_inc(l1q_done, 1)
            link(dve, dve.tensor_scalar(ysT[:], prm("condT"), P ** -0.5, None, ALU.mult))
            link(dve, dve.tensor_tensor(f1[:, 0, :], ysT[:], ysT[:], ALU.mult))
            link(dve, dve.tensor_tensor(f1[:, 1, :], prm("l2w"), prm("l2w"), ALU.mult))
            link(dve, dve.tensor_reduce(col(TMP), prm("rhsT"), X, ALU.max, apply_absolute_value=True))
            link(dve, dve.tensor_scalar(col(RSC), col(TMP), TINY, 1.0 / 127.0, ALU.max, ALU.mult))
            link(dve, dve.reciprocal(col(TMP), col(RSC)))
            link(dve, dve.tensor_scalar(f1[:, 2, :], prm("rhsT"), col(TMP), MAGIC, ALU.mult, ALU.add))
            dve.tensor_scalar(f1[:, 2, :], f1[:, 2, :], MAGIC, None, ALU.subtract).then_inc(prep_in, 1)
            for n in range(9):
                dve.wait_ge(l1_hi_done, n + 1)
                dve.tensor_tensor(l1_lo[:, n, :], GV[n % 4][:, 0:P], l1_hi[:, n, :].bitcast(F32),
                                  ALU.subtract).then_inc(l1_lo_done, 1)
            dve.wait_ge(prep_act, 1)
            link(dve, dve.reciprocal(dmod[:], dmod[:]))
            link(dve, dve.tensor_scalar(col(LEAK2), prm("alpha"), -2.0, 2.0, ALU.mult, ALU.add))
            dve.nop().then_inc(prep_read, 1)

            counted = [0]

            def whole_max(columns_at):
                counted[0] += 1
                n = counted[0]
                dve.tensor_reduce(col(TMP), columns_at, X, ALU.max).then_inc(max_col, 1)
                dve.wait_ge(max_turned, n)
                dve.tensor_reduce(tiny[0:1, TMP2:TMP2 + 1], TP[0:1, 0:P], X, ALU.max).then_inc(max_row, 1)
                dve.wait_ge(max_mm, n)
                return TP[:, P:P + 1]

            dve.wait_ge(hmax_done, NB)
            m = whole_max(maxima[:, 0:NB])
            link(dve, dve.tensor_scalar(col(SX), m, 0.5 / Q16, TINY, ALU.mult, ALU.max))
            link(dve, dve.reciprocal(col(TMP), col(SX)))
            dve.tensor_scalar(col(INVX), col(TMP), 0.5, None, ALU.mult).then_inc(factor_done, 1)
            dve.wait_ge(factor_done, 1)

            def parts_of_x(i):
                at = slice(i * N + P, (i + 1) * N + P) if isinstance(i, int) else bass.ds(i * N + P, N)
                dve.wait_ge(xt_done, i + 1)
                need(dve, ug_mm, i * 6)
                dve.tensor_scalar(xq_hi[:], hT[:, at], MAGIC, None, ALU.subtract).then_inc(xq_hi_done, 1)
                dve.wait_ge(xq_hi_done, i + 1)
                dve.scalar_tensor_tensor(out=xq_lo[:], in0=hT[:, at], scalar=MAGIC,
                                         in1=xq_hi[:].bitcast(F32), op0=ALU.subtract,
                                         op1=ALU.subtract).then_inc(xq_lo_done, 1)

            def maxima_of(i):
                for r, rows in enumerate((up_s, gate_s)):
                    at = slice(r * NB + i, r * NB + i + 1) if isinstance(i, int) else bass.ds(i + r * NB, 1)
                    dve.wait_ge(ug_copied, i * 6 + 3 * r + 3)
                    dve.tensor_reduce(maxima[:, at], rows[:, block_of(i, 3 * N)], X, ALU.max,
                                      apply_absolute_value=True).then_inc(ug_max, 1)

            parts_of_x(0)
            maxima_of(0)
            with dve.Fori(1, NB) as i:
                parts_of_x(i)
                maxima_of(i)
            dve.wait_ge(ug_max, 2 * NB)
            for at, scale, factor in ((slice(0, NB), SU, KU), (slice(NB, 2 * NB), SG, KG)):
                m = whole_max(maxima[:, at])
                link(dve, dve.tensor_scalar(col(TMP), m, col(SX), 1.0 / Q16, ALU.mult, ALU.mult))
                link(dve, dve.tensor_scalar(col(scale), col(TMP), TINY, None, ALU.max))
                link(dve, dve.reciprocal(col(TMP), col(scale)))
                link(dve, dve.tensor_scalar(col(factor), col(TMP), col(SX), None, ALU.mult))
            dve.nop().then_inc(factor_done, 1)

            def gate_value(i):
                at = gate_s[:, block_of(i, 3 * N)]
                dve.wait_ge(gt_done, i + 1)
                dve.tensor_scalar(at, at, MAGIC, col(SG), ALU.subtract, ALU.mult).then_inc(g_done, 1)

            def gated_sig(i, b):
                at = gate_s[:, block_of(i, 3 * N)]
                dve.wait_ge(sig_done, i + 1)
                dve.tensor_scalar(sig_s[:, b, :], sig_s[:, b, :], 65535.0 / 65536.0, MAGIC16, ALU.min,
                                  ALU.add).then_inc(sig_rounded, 1)
                dve.wait_ge(sig_rounded, i + 1)
                dve.scalar_tensor_tensor(out=at, in0=sig_s[:, b, :], scalar=MAGIC16, in1=at,
                                         op0=ALU.subtract, op1=ALU.mult).then_inc(gs_done, 1)
                dve.wait_ge(gs_done, i + 1)
                dve.tensor_reduce(maxima[:, block_of(i, 1)], at, X, ALU.max,
                                  apply_absolute_value=True).then_inc(gs_max, 1)

            gate_value(0)
            gate_value(1)
            gated_sig(0, 0)
            with dve.Fori(1, NB // 2) as i:
                gate_value(2 * i)
                gated_sig(2 * i - 1, 1)
                gate_value(2 * i + 1)
                gated_sig(2 * i, 0)
            gated_sig(NB - 1, 1)
            dve.wait_ge(gs_max, NB)
            m = whole_max(maxima[:, 0:NB])
            link(dve, dve.tensor_scalar(col(SGS), m, 1.0 / Q16, TINY, ALU.mult, ALU.max))
            link(dve, dve.reciprocal(col(KGS), col(SGS)))
            dve.nop().then_inc(factor_done, 1)

            def outer(i):
                at, ups = gate_s[:, block_of(i, 3 * N)], up_s[:, block_of(i, 3 * N)]
                dve.wait_ge(gst_done, i + 1)
                dve.tensor_scalar(at, at, MAGIC, None, ALU.subtract).then_inc(g2_done, 1)
                dve.wait_ge(g2_done, i + 1)
                dve.wait_ge(ut_done, i + 1)
                dve.scalar_tensor_tensor(out=at, in0=ups, scalar=MAGIC, in1=at, op0=ALU.subtract,
                                         op1=ALU.mult).then_inc(o_done, 1)
                dve.wait_ge(o_done, i + 1)
                dve.tensor_reduce(maxima[:, block_of(i, 1)], at, X, ALU.max,
                                  apply_absolute_value=True).then_inc(o_max, 1)

            with dve.Fori(0, NB) as i:
                outer(i)
            dve.wait_ge(o_max, NB)
            m = whole_max(maxima[:, 0:NB])
            link(dve, dve.tensor_scalar(col(SGS), col(SGS), col(SU), None, ALU.mult))
            link(dve, dve.tensor_scalar(col(TMP), m, col(SGS), 1.0 / Q16, ALU.mult, ALU.mult))
            link(dve, dve.tensor_scalar(col(SO), col(TMP), TINY, None, ALU.max))
            link(dve, dve.reciprocal(col(TMP), col(SO)))
            dve.tensor_scalar(col(KO), col(TMP), col(SGS), None, ALU.mult).then_inc(factor_done, 1)
            dve.wait_ge(factor_done, 4)

            def recur(i, j):
                t = i * BS + j
                dve.wait_ge(rgate_done, t + 2)
                dve.scalar_tensor_tensor(out=uv[:, 0, :], in0=gact[:, 0, :], scalar=1.0,
                                         in1=xT[:, block_of(t, P)], op0=ALU.add,
                                         op1=ALU.mult).then_inc(ru_done, 1)
                dve.wait_ge(ru_done, t + 1)
                dve.scalar_tensor_tensor(out=uv[:, 1, :], in0=hT[:, block_of(t, P)], scalar=col(LEAK2),
                                         in1=uv[:, 0, :], op0=ALU.mult, op1=ALU.add).then_inc(rv_done, 1)

            def grid(ap):
                return ap.rearrange("p (s d) -> p s d", s=BS)

            def layer2(i, main=True, tail=True):
                if main:
                    at = gate_s[:, block_of(i, 3 * N)]
                    hi = oq_hi[:].rearrange("p c n -> p (c n)")
                    dve.wait_ge(ot_done, i + 1)
                    need(dve, o_mm, i)
                    dve.tensor_scalar(hi, at, MAGIC, None, ALU.subtract).then_inc(oq_hi_done, 1)
                    dve.wait_ge(oq_hi_done, i + 1)
                    dve.scalar_tensor_tensor(out=oq_lo[:].rearrange("p c n -> p (c n)"), in0=at, scalar=MAGIC,
                                             in1=hi.bitcast(F32), op0=ALU.subtract,
                                             op1=ALU.subtract).then_inc(oq_lo_done, 1)
                if tail:
                    recur(i - 1, 0)
                if main:
                    xb = xT[:, block_of(i)]
                    dve.wait_ge(o_mm, i + 1)
                    dve.scalar_tensor_tensor(out=xb, in0=GV[0][:, :], scalar=col(SO), in1=xb, op0=ALU.mult,
                                             op1=ALU.add).then_inc(x2T_done, 1)
                if tail:
                    recur(i - 1, 1)
                if main:
                    dve.wait_ge(l2_mm, i + 1)
                    need(dve, q1_done, i)
                    dve.tensor_tensor(norm2[:], grid(GV[1][:, :]), over(dmod[:], BS), ALU.mult).then_inc(norm_done, 1)
                    dve.wait_ge(norm_done, i + 1)
                    dve.tensor_reduce(lsc[:, 0:BS], norm2[:], X, ALU.max,
                                      apply_absolute_value=True).then_inc(nmax_done, 1)
                    dve.wait_ge(nmax_done, i + 1)
                    dve.tensor_scalar(lsc[:, 0:BS], lsc[:, 0:BS], TINY, 1.0 / 127.0, ALU.max,
                                      ALU.mult).then_inc(lscale_done, 1)
                    dve.wait_ge(lscale_done, i + 1)
                    dve.reciprocal(lsc[:, BS:2 * BS], lsc[:, 0:BS]).then_inc(linv_done, 1)
                    dve.wait_ge(q1_done, i + 1)
                    need(dve, q2T_mm, i)
                    dve.tensor_scalar(q2[:], norm2[:], MAGIC, MAGIC, ALU.add, ALU.subtract).then_inc(q2_done, 1)
                if tail:
                    recur(i - 1, 2)
                if main:
                    dve.wait_ge(acc_mm, i + 1)
                    need(dve, f2_done, i)
                    dve.tensor_tensor(f1[:], grid(GV[3][:, :]), wide(lsc[:, 0:BS], P), ALU.mult).then_inc(f1_done, 1)
                if tail:
                    recur(i - 1, 3)
                if main:
                    xb = xT[:, block_of(i)]
                    dve.wait_ge(fT_mm, i + 1)
                    dve.wait_ge(modx_done, i + 1)
                    dve.tensor_tensor(xb, Y[:, :], xb, ALU.add).then_inc(x3T_done, 1)

            layer2(0, tail=False)
            with dve.Fori(1, NB) as i:
                layer2(i)
            layer2(NB, main=False)

            dve.wait_ge(logit_mm, 1)
            link(dve, dve.tensor_copy(scores[:].rearrange("p s e -> p (s e)"), Z[:, 0:S * E]))
            ranks(pairs3[:], centred)
            turned_sel = sel.rearrange("p e s -> p s e")
            link(dve, dve.tensor_scalar(turned_sel, wsel[:], 1.5, None, ALU.is_lt))
            link(dve, dve.tensor_tensor_scan(place.rearrange("p e s -> p (e s)"), cst("rows"),
                                             sel.rearrange("p e s -> p (e s)"), 0.0, ALU.mult, ALU.add))
            dve.tensor_copy(counts, place[:, :, S - 1]).then_inc(counts_done, 1)
            dve.wait_ge(exp_done, 2)
            link(dve, dve.tensor_tensor(wsel[:], turned_sel, expo[:], ALU.mult))
            link(dve, dve.tensor_reduce(rowst[:, 1, :], wsel[:], X, ALU.add))
            link(dve, dve.reciprocal(rowst[:, 2, :], rowst[:, 1, :]))
            link(dve, dve.tensor_tensor(wsel[:], wsel[:], wide(rowst[:, 2, :], E), ALU.mult))
            dve.wait_ge(before_mm, 1)
            link(dve, dve.tensor_tensor(place, place, wide(BC[:, 0:E], S), ALU.add))
            link(dve, dve.scalar_tensor_tensor(out=wsel[:], in0=place.rearrange("p e s -> p s e"),
                                               scalar=float(CAP), in1=wsel[:], op0=ALU.is_le, op1=ALU.mult))
            weight_parts()
            dve.nop().then_inc(kept_done, 1)
            dve.wait_ge(w2_lo_done, 1)

            def layer3(i, main=True, tail=True):
                for k in range(NK3):
                    n, e = i * NK3 + k, k // 2
                    if main:
                        dve.wait_ge(g3_mm, n + 1)
                        dve.wait_ge(gelu_done, n + 1)
                        need(dve, h3_lo_done, n - 1)
                        dve.tensor_tensor(hf3[:, k % 2, :], GV[2 * (k % 2) + 1][:, :], gelu3[:, k % 2, :],
                                          ALU.mult).then_inc(h3_done, 1)
                    if k % 2 == 1 and (main if e else tail):
                        m, f = i * E + e - 1, (e - 1) % E
                        at = block_of(i)
                        dve.wait_ge(down3_mm, m + 1)
                        dve.wait_ge(bc3_copied, m + 1)
                        need(dve, added3, m)
                        dve.tensor_tensor(scaled3, Y[:, :], bcast3, ALU.mult).then_inc(scaled3_done, 1)
                        if f == 0:
                            dve.wait_ge(scaled3_done, m + 1)
                            need(dve, out_turned, i)
                            dve.tensor_tensor(xacc[:], xT[:, at], scaled3, ALU.add).then_inc(added3, 1)
                    if main and k == 1:
                        need(dve, wturned3, i)
                        dve.tensor_copy(wcur[:], wparts[:, steps_of(i), :]).then_inc(wcur3_done, 1)

            layer3(0, tail=False)
            with dve.Fori(1, NB) as i:
                layer3(i)
            layer3(NB, main=False)

        @block.gpsimd
        def _(pool):
            for k in range(NB):
                pool.wait_ge(h_done, k + 1)
                rows = tok[:, k * BS:(k + 1) * BS, :]
                nc.gpsimd.tensor_tensor(rows, rows, hrow[:, k % 2].rearrange("p (s d) -> p s d", s=BS),
                                        ALU.add).then_inc(r_done, 1)
            for e in range(E):
                pool.wait_ge(wu_hi_done, e + 1)
                nc.gpsimd.tensor_tensor(wu_lo[:, e, :], wup_raw[:, e, :], wu_hi[:, e, :].bitcast(F32),
                                        ALU.subtract).then_inc(wu_lo_done, 1)
            pool.wait_ge(wd_hi_done, 2)
            nc.gpsimd.tensor_tensor(wd_lo[:, :, 0:2, :], wdown_raw[:, :, 0:2, :],
                                    wd_hi[:, :, 0:2, :].bitcast(F32), ALU.subtract).then_inc(wd_lo_done, 1)
            nc.gpsimd.tensor_tensor(wd_lo[0:96, :, 2, :], wdown_raw[0:96, :, 2, :],
                                    wd_hi[0:96, :, 2, :].bitcast(F32), ALU.subtract).then_inc(wd_lo_done, 1)

            def low0(n, k):
                rows = CH0[k % 3][1]
                pool.wait_ge(h0_hi_done, n + 1)
                nc.gpsimd.tensor_tensor(h0_lo[0:rows, k % 4, :], hf0[0:rows, k % 2, :],
                                        h0_hi[0:rows, k % 4, :].bitcast(F32), ALU.subtract).then_inc(h0_lo_done, 1)

            def add0(m, f):
                pool.wait_ge(scaled_done, m + 1)
                pool.wait_ge(added, m)
                nc.gpsimd.tensor_tensor(xacc[:], xacc[:], scaled0, ALU.add).then_inc(added, 1)

            def layer0(i, main=True, tail=True):
                for k in range(NK0):
                    e = k // 3
                    if main if k else tail:
                        low0(i * NK0 + k - 1, (k - 1) % NK0)
                    if k % 3 == 2 and e != 1 and (main if e else tail):
                        add0(i * E + e - 1, (e - 1) % E)
                    if tail and k == 4:
                        pool.wait_ge(xs_hi_done, i)
                        nc.gpsimd.tensor_tensor(xs_lo[:], xacc[:], xs_hi[:].bitcast(F32),
                                                ALU.subtract).then_inc(xs_lo_done, 1)

            layer0(0, tail=False)
            with pool.Fori(1, NB) as i:
                layer0(i)
            layer0(NB, main=False)

            pool.wait_ge(factor_done, 2)
            for i in range(NB):
                at = up_s[:, block_of(i, 3 * N)]
                nc.gpsimd.tensor_scalar(at, at, col(KU), MAGIC, ALU.mult, ALU.add).then_inc(ut_done, 1)

            def layer2(i):
                pool.wait_ge(x2T_done, i + 1)
                need(pool, l2_mm, i)
                nc.gpsimd.tensor_tensor(modx[:], xT[:, block_of(i)].rearrange("p (s d) -> p s d", s=BS),
                                        over(ysT[:], BS), ALU.mult).then_inc(modx_done, 1)
                pool.wait_ge(linv_done, i + 1)
                nc.gpsimd.tensor_tensor(norm2[:], norm2[:], wide(lsc[:, BS:2 * BS], P), ALU.mult).then_inc(q1_done, 1)
                pool.wait_ge(f1_done, i + 1)
                need(pool, fT_mm, i)
                nc.gpsimd.tensor_tensor(f2[:], f1[:], over(rscale[:], BS), ALU.mult).then_inc(f2_done, 1)

            def low3(i):
                pool.wait_ge(hs_hi_done, i + 1)
                at = slice(i * N + P, (i + 1) * N + P) if isinstance(i, int) else bass.ds(i * N + P, N)
                nc.gpsimd.tensor_tensor(hs_lo[:, block_of(i)], hT[:, at], hs_hi[:, block_of(i)].bitcast(F32),
                                        ALU.subtract).then_inc(hs_lo_done, 1)

            layer2(0)
            with pool.Fori(1, NB) as i:
                layer2(i)
                low3(i - 1)
            low3(NB - 1)
            for e in range(E):
                pool.wait_ge(w1_hi_done, e + 1)
                nc.gpsimd.tensor_tensor(w1_lo[:, e, :], w1_raw[:, e, :], w1_hi[:, e, :].bitcast(F32),
                                        ALU.subtract).then_inc(w1_lo_done, 1)
            pool.wait_ge(w2_hi_done, 1)
            nc.gpsimd.tensor_tensor(w2_lo[:], w2_raw[:], w2_hi[:].bitcast(F32), ALU.subtract).then_inc(w2_lo_done, 1)

            def layer3(i, main=True, tail=True):
                for k in range(NK3):
                    e, n = k // 2, i * NK3 + k
                    if main if k else tail:
                        pool.wait_ge(h3_hi_done, n)
                        nc.gpsimd.tensor_tensor(h3_lo[:, (k - 1) % 4, :], hf3[:, (k - 1) % 2, :],
                                                h3_hi[:, (k - 1) % 4, :].bitcast(F32),
                                                ALU.subtract).then_inc(h3_lo_done, 1)
                    if k % 2 == 1 and e != 1 and (main if e else tail):
                        m, f = i * E + e - 1, (e - 1) % E
                        pool.wait_ge(scaled3_done, m + 1)
                        pool.wait_ge(added3, m)
                        nc.gpsimd.tensor_tensor(xacc[:], xacc[:], scaled3, ALU.add).then_inc(added3, 1)

            layer3(0, tail=False)
            with pool.Fori(1, NB) as i:
                layer3(i)
            layer3(NB, main=False)


def kernel(**inputs):
    import numpy as np
    import concourse.bacc as bacc
    from concourse.bass_utils import run_bass_kernel_spmd

    a = {k: np.asarray(v) for k, v in inputs.items()}
    cond = a["cond_1024"]
    L3W = a["L3_cond_W"]
    parts = {
        "condT": cond.T, "W1T": a["L0_cond_W1"].T, "W2T": a["L0_cond_W2"].T,
        "b2": np.broadcast_to(a["L0_cond_b2"], (P, P)), "l2w": a["L2_cond_weight"], "rhsT": a["L2_ffn_rhs"].T,
        "WhT": L3W[:, :P].T, "WzT": L3W[:, P:].T, "Wh": a["L1_cond_Wh"],
        "wrT": a["L0_ffn_w_router"].T, "WgT": a["L3_ffn_Wg"].T,
        "b1": a["L0_cond_b1"][:, None], "nscale": a["L0_ffn_norm_scale"][:, None],
        "b3": a["L3_cond_b"][:, None], "alpha": a["L3_cond_alpha"][:, None]}
    ties = np.where(np.arange(E)[None, :] < np.arange(E)[:, None], -1.2e-38, 0.0)
    fixed = {
        "ident": np.eye(P), "before": np.triu(np.ones((P, P)), 1),
        "ties": np.broadcast_to(ties.reshape(1, -1), (P, E * E)),
        "rows": np.broadcast_to((np.arange(S * E) % S > 0)[None, :], (P, S * E)), "ones": np.ones((P, P)),
        "pick": (np.arange(P)[:, None] % E == np.arange(E)[None, :])}
    arrays = {
        "x": a["x"],
        "params": np.concatenate([parts[n] for n, _ in PARAMS], axis=1),
        "consts": np.concatenate([fixed[n] for n, _ in CONSTS], axis=1).astype(np.float32),
        "wx": a["L1_cond_Wx"], "bl": a["L1_cond_b"][None, :],
        "w_up": a["L0_ffn_w_up"].transpose(2, 0, 1),
        "w_down": a["L0_ffn_w_down"].transpose(0, 2, 1),
        "l1w": np.concatenate([a["L1_ffn_w_up"].reshape(3, P, P).transpose(1, 0, 2).reshape(P, H1),
                               a["L1_ffn_w_gate"].reshape(3, P, P).transpose(1, 0, 2).reshape(P, H1),
                               a["L1_ffn_w_down"]], axis=1),
        "w1": a["L3_ffn_W1"].transpose(1, 0, 2),
        "w2": a["L3_ffn_W2"].reshape(E, 2, P, P).transpose(2, 0, 1, 3)}
    nc = bacc.Bacc("TRN2", target_bir_lowering=False, num_devices=1)
    args = []
    for name in arrays:
        arrays[name] = np.ascontiguousarray(arrays[name])
        args.append(nc.dram_tensor(f"in_{name}", arrays[name].shape, F32, kind="ExternalInput").ap())
    args.append(nc.dram_tensor("out", (P, S, P), F32, kind="ExternalOutput").ap())
    mixer_kernel(nc, *args)
    r = run_bass_kernel_spmd(nc, [{f"in_{n}": v for n, v in arrays.items()}], core_ids=[0])
    return r.results[0]["out"]
```

```python
from contextlib import ExitStack

import concourse.bass as bass
from concourse import mybir

F32 = mybir.dt.float32
F32R = mybir.dt.float32r
BF16 = mybir.dt.bfloat16
ALU = mybir.AluOpType
ACT = mybir.ActivationFunctionType
X = mybir.AxisListType.X

P = 128
S = 32
E = 8
BS = 4
NB = S // BS
N = BS * P
T = S * P
H0 = 352
H1 = 384
H3 = 256
CH0 = [(0, 128), (128, 128), (256, 96)]
CAP = int(T * 2 * 1.25 / E)
MAGIC = 1.5 * 2.0 ** 23
MAGIC16 = 192.0
Q16 = 32767.0
TINY = 1e-12

PARAMS = [("condT", 128), ("W1T", 128), ("W2T", 128), ("b2", 128), ("l2w", 128), ("rhsT", 128),
          ("WhT", 128), ("WzT", 128), ("Wh", 512), ("wrT", 8), ("WgT", 8), ("b1", 1), ("nscale", 1), ("b3", 1), ("alpha", 1)]
CONSTS = [("ident", 128), ("before", 128), ("ties", 64), ("rows", 256), ("ones", 128),
          ("pick", 8)]


def columns(parts):
    at, out = 0, {}
    for name, n in parts:
        out[name] = slice(at, at + n)
        at += n
    return out, at


PC, NPC = columns(PARAMS)
CC, NCC = columns(CONSTS)


def block_of(i, n=N):
    return slice(i * n, (i + 1) * n) if isinstance(i, int) else bass.ds(i * n, n)


def need(engine, semaphore, value):
    if not isinstance(value, int) or value > 0:
        engine.wait_ge(semaphore, value)


def mixer_kernel(nc, x, params, consts, wx, bl, w_up, w_down, l1w, w1, w2, out):
    ctx = ExitStack()
    with ctx:
        def keep(name, shape, dt=F32):
            return ctx.enter_context(nc.sbuf_tensor(name, shape, dt))

        def sem(name):
            return ctx.enter_context(nc.semaphore(name))

        xh = keep("xh", [P, T + T + P])
        par = keep("par", [P, NPC])
        con = keep("con", [P, NCC])
        gate1 = keep("gate1", [P, P])
        hid = keep("hid", [P, P])
        tiny = keep("tiny", [P, 64])
        wsel = keep("wsel", [P, S, E])
        scores = keep("scores", [P, S, E])
        expo = keep("expo", [P, S, E])
        rowst = keep("rowst", [P, 4, S])
        xacc = keep("xacc", [P, N])
        xs_hi, xs_lo = keep("xs_hi", [P, N], F32R), keep("xs_lo", [P, N], F32R)
        wx_hi, wx_lo = keep("wx_hi", [P, N], F32R), keep("wx_lo", [P, N], F32R)
        bl_hi, bl_lo = keep("bl_hi", [1, N], F32R), keep("bl_lo", [1, N], F32R)
        ones_r = keep("ones_r", [1, P], F32R)
        pick_r = keep("pick_r", [2 * E, E, P], F32R)
        wparts = keep("wparts", [P, S, 2 * E])
        wround = keep("wround", [P, S, E], F32R)
        wcur = keep("wcur", [P, BS, 2 * E])
        wT = keep("wT", [2 * E, N], F32R)
        state2 = keep("state2", [P, P])
        stateT = keep("stateT", [P, P])
        cell = keep("cell", [P, P])
        gact = keep("gact", [P, 4, P])
        uv = keep("uv", [P, 2, P])
        tcell = keep("tcell", [P, P])
        wscale = keep("wscale", [P, 2, 36])
        maxima = keep("maxima", [P, 2 * NB])
        xT = xh[:, 0:T]
        hT = xh[:, T:]

        def col(n):
            return tiny[:, n:n + 1]

        def prm(name):
            return par[:, PC[name]]

        def cst(name):
            return con[:, CC[name]]

        ident = cst("ident")
        EPS_RMS, MAG, EPS_L2, NMAG = range(4)
        B1H, B3H, LEAK2 = 8, 9, 10
        INVX, KU, KG, SG, KGS, SGS, KO, SO, SX, SU, TMP, TMP2, RSC = range(16, 29)

        banks = [ctx.enter_context(nc.psum_tensor(f"bank{i}", [P, 512], F32)) for i in range(8)]
        GV, Y, BC, Z, TP = banks[0:4], banks[4], banks[5], banks[6], banks[7]
        Y3 = (Y, Z)

        def layer(parts):
            made = ExitStack()
            got = [made.enter_context(nc.sbuf_tensor(n, s, d)) for n, s, d in parts]
            made.close()
            return got

        (xn_hi, xn_lo, wu_hi, wu_lo, wd_hi, wd_lo, work0, wr_hi, wr_lo, h0_hi, h0_lo) = layer([
            ("xn_hi", [P, T], F32R), ("xn_lo", [P, T], F32R),
            ("wu_hi", [P, E, 2 * H0], F32R), ("wu_lo", [P, E, 2 * H0], F32R),
            ("wd_hi", [P, E, 3, P], F32R), ("wd_lo", [P, E, 3, P], F32R),
            ("work0", [P, 6 * N], F32), ("wr_hi", [P, E], F32R), ("wr_lo", [P, E], F32R),
            ("h0_hi", [P, 4, N], F32R), ("h0_lo", [P, 4, N], F32R)])
        silu0, hf0 = (work0[:, k * 2 * N:(k + 1) * 2 * N].rearrange("p (b n) -> p b n", b=2)
                      for k in range(2))
        scaled0, bcast0 = work0[:, 4 * N:5 * N], work0[:, 5 * N:6 * N]
        *_, tok = layer([
            ("u1", [P, T], F32R), ("u2", [P, T], F32R), ("u3", [P, E, 2 * H0], F32R),
            ("u4", [P, E, 2 * H0], F32R), ("u5", [P, E, 3, P], F32R), ("u6", [P, E, 3, P], F32R),
            ("u7", [P, 6 * N], F32), ("u8", [P, E], F32R), ("u9", [P, E], F32R), ("tok", [P, S, P], F32)])
        wup_raw = xh[:, 0:E * 2 * H0].rearrange("p (e r) -> p e r", e=E)
        wdown_raw = work0[:].rearrange("p (e c d) -> p e c d", e=E, c=3)
        lines = xh[:, E * 2 * H0:E * 2 * H0 + 5 * N].rearrange("p (k n) -> p k n", k=5)
        hrow, xnrow, square = lines[:, 0:2], lines[:, 2:4], lines[:, 4]
        pairs = xh[:, E * 2 * H0:E * 2 * H0 + S * E * E].rearrange("p (s e f) -> p s e f", s=S, e=E)

        layer1 = ExitStack()
        (gate_s, sig_s, l1_hi, l1_lo, xq_hi, xq_lo) = [
            layer1.enter_context(nc.sbuf_tensor(n, s, d)) for n, s, d in [
                ("gate_s", [P, NB * 3 * N], F32), ("sig_s", [P, 2, 3 * N], F32),
                ("l1_hi", [P, 9, P], F32R), ("l1_lo", [P, 9, P], F32R),
                ("xq_hi", [P, 2, N], F32R), ("xq_lo", [P, 2, N], F32R)]]
        dmod, ysT, rhs_q, lsc = [
            layer1.enter_context(nc.sbuf_tensor(n, s, d)) for n, s, d in [
                ("dmod", [P, P], F32), ("ysT", [P, P], F32),
                ("rhs_q", [P, P], BF16), ("lsc", [P, 2 * BS], F32)]]
        up_s, = layer([("up_s", [P, NB * 3 * N], F32)])
        (oq_hi, oq_lo, modx, norm2, q2, qT, f1, hs_hi, hs_lo) = layer([
            ("oq_hi", [P, 3, N], F32R), ("oq_lo", [P, 3, N], F32R), ("modx", [P, BS, P], F32),
            ("norm2", [P, BS, P], F32), ("q2", [P, BS, P], F32), ("qT", [P, N], BF16),
            ("f1", [P, BS, P], F32),
            ("hs_hi", [P, T], F32R), ("hs_lo", [P, T], F32R)])
        layer1.close()
        o_int = sig_s[:, 0, :]
        l1_raw = sig_s[:].rearrange("p b n -> p (b n)")[:, 0:9 * P]
        l1_q = sig_s[:].rearrange("p b n -> p (b n)")[:, 9 * P:18 * P]
        _, w1_raw, _, w2_raw = layer([
            ("w1_over", [P, E, 2 * H3], F32R), ("w1_raw", [P, E, 2 * H3], F32),
            ("w2_over", [P, E, 2, P], F32R), ("w2_raw", [P, E, 2, P], F32)])
        (w1_hi, w1_lo, w2_hi, w2_lo, work3, h3_hi, h3_lo, pairs3) = layer([
            ("w1_hi", [P, E, 2 * H3], F32R), ("w1_lo", [P, E, 2 * H3], F32R),
            ("w2_hi", [P, E, 2, P], F32R), ("w2_lo", [P, E, 2, P], F32R),
            ("work3", [P, 6 * N], F32), ("h3_hi", [P, 4, N], F32R), ("h3_lo", [P, 4, N], F32R),
            ("pairs3", [P, S, E, E], F32)])
        gelu3, hf3 = (work3[:, k * 2 * N:(k + 1) * 2 * N].rearrange("p (b n) -> p b n", b=2)
                      for k in range(2))
        scaled3, bcast3 = work3[:, 4 * N:5 * N], work3[:, 5 * N:6 * N]
        pairs_flat = pairs3[:].rearrange("p s e f -> p (s e f)")
        orow = pairs_flat[:, 0:N].rearrange("p (s d) -> p s d", s=BS)
        sel, place = (pairs_flat[:, k * S * E:(k + 1) * S * E].rearrange("p (e s) -> p e s", e=E) for k in (2, 3))
        counts = pairs_flat[:, 4 * S * E:4 * S * E + E]

        (params_in, consts_in, x_in, wdown_in, l1w_in, w1_in, w2_in) = map(
            sem, ["params_in", "consts_in", "x_in", "wdown_in", "l1w_in", "w1_in", "w2_in"])
        wx_in = sem("wx_in")
        (wx_scaled, wx_hi_done, wx_lo_done, picks_done, wcur_done, wturned, wT_done, bc_mm, bc_copied,
         x_turned, xT_done, xs_hi_done, xs_lo_done, h_turned, slot_done, state2_done) = map(sem, [
             "wx_scaled", "wx_hi_done", "wx_lo_done", "picks_done", "wcur_done", "wturned", "wT_done",
             "bc_mm", "bc_copied", "x_turned", "xT_done", "xs_hi_done", "xs_lo_done", "h_turned",
             "slot_done", "state2_done"])
        wcur3_done, wturned3, wT3_done, bc3_mm, bc3_copied, out_turned, orow_done = map(sem, [
            "wcur3_done", "wturned3", "wT3_done", "bc3_mm", "bc3_copied", "out_turned", "orow_done"])
        wup_in = [sem("wup_in_first"), sem("wup_in_last")]
        dve_step, eps_set = map(sem, ["dve_step", "eps_set"])
        (hidden_mm, hidden_done, gate_mm, gate_pre, gate_tanh, gate_done) = map(
            sem, ["hidden_mm", "hidden_done", "gate_mm", "gate_pre", "gate_tanh", "gate_done"])
        (h_done, square_done, sum_done, sqrt_done, xn_done, xnT_mm, xn_hi_done, xn_lo_done,
         r_done) = map(sem, ["h_done", "square_done", "sum_done", "sqrt_done", "xn_done", "xnT_mm",
                             "xn_hi_done", "xn_lo_done", "r_done"])
        wu_hi_done, wu_lo_done, wd_hi_done, wd_lo_done, wr_hi_done, wr_lo_done = map(
            sem, ["wu_hi_done", "wu_lo_done", "wd_hi_done", "wd_lo_done", "wr_hi_done", "wr_lo_done"])
        score_mm, scores_read, centred, exp_done = map(
            sem, ["score_mm", "scores_read", "centred", "exp_done"])
        (g_mm, v_mm, silu_done, h0_done, h0_hi_done, h0_lo_done, down_mm, scaled_done, added,
         x1T_done) = map(sem, ["g_mm", "v_mm", "silu_done", "h0_done", "h0_hi_done",
                                       "h0_lo_done", "down_mm", "scaled_done", "added",
                                       "x1T_done"])
        z_mm, gates_done, uv_done, cell_done, tcell_done, state_done, hmax_done = map(
            sem, ["z_mm", "gates_done", "uv_done", "cell_done", "tcell_done", "state_done", "hmax_done"])
        l1q_done, l1T_mm, l1_hi_done, l1_lo_done = map(sem, ["l1q_done", "l1T_mm", "l1_hi_done", "l1_lo_done"])
        prep_in, prep_mm, prep_act, bias_done, kept_done, wh_halved = map(
            sem, ["prep_in", "prep_mm", "prep_act", "bias_done", "kept_done", "wh_halved"])
        max_col, max_turned, max_row, max_mm, factor_done = map(
            sem, ["max_col", "max_turned", "max_row", "max_mm", "factor_done"])
        (xt_done, xq_hi_done, xq_lo_done, ug_mm, ug_copied, ug_max) = map(
            sem, ["xt_done", "xq_hi_done", "xq_lo_done", "ug_mm", "ug_copied", "ug_max"])
        (gt_done, g_done, sig_done, sig_rounded, gs_done, gs_max, ut_done) = map(
            sem, ["gt_done", "g_done", "sig_done", "sig_rounded", "gs_done", "gs_max", "ut_done"])
        gst_done, g2_done, o_done, o_max = map(sem, ["gst_done", "g2_done", "o_done", "o_max"])
        (ot_done, oq_hi_done, oq_lo_done, o_mm, x2T_done, modx_done, l2_mm, norm_done, nmax_done,
         lscale_done, linv_done, q2_done, q2T_mm, qT_done, acc_mm, f1_done,
         fT_mm, x3T_done) = map(sem, [
             "ot_done", "oq_hi_done", "oq_lo_done", "o_mm", "x2T_done", "modx_done", "l2_mm",
             "norm_done", "nmax_done", "lscale_done", "linv_done", "q2_done", "q2T_mm",
             "qT_done", "acc_mm", "f1_done", "fT_mm", "x3T_done"])
        (rz_mm, rgate_done, ru_done, rv_done, rstate_done, hs_hi_done, hs_lo_done) = map(sem, [
            "rz_mm", "rgate_done", "ru_done", "rv_done", "rstate_done", "hs_hi_done", "hs_lo_done"])
        (logit_mm, counts_done, before_mm) = map(sem, [
            "logit_mm", "counts_done", "before_mm"])
        w1_hi_done, w1_lo_done, w2_hi_done, w2_lo_done = map(
            sem, ["w1_hi_done", "w1_lo_done", "w2_hi_done", "w2_lo_done"])
        (i3_mm, g3_mm, gelu_done, h3_done, h3_hi_done, h3_lo_done, down3_mm, scaled3_done,
         added3, out_done) = map(sem, ["i3_mm", "g3_mm", "gelu_done", "h3_done", "h3_hi_done",
                                       "h3_lo_done", "down3_mm", "scaled3_done", "added3", "out_done"])

        steps = [0]

        def link(dve, ins):
            steps[0] += 1
            ins.then_inc(dve_step, 1)
            dve.wait_ge(dve_step, steps[0])

        LSTM_AT = [7, 11, 15, 19]
        NK0 = 3 * E
        NK3 = 2 * E

        def wide(ap, n):
            return ap.unsqueeze(2).broadcast_to([P, ap.shape[1], n])

        def over(ap, n):
            return ap.unsqueeze(1).broadcast_to([P, n, ap.shape[1]])

        def steps_of(i):
            return block_of(i, BS)

        block = ctx.enter_context(nc.Block())

        @block.sync
        def _(sp):
            sp.dma_start(par[:], params).then_inc(params_in, 16)
            sp.dma_start(tok[:], x).then_inc(x_in, 16)
            sp.dma_start(con[:], consts).then_inc(consts_in, 16)
            sp.dma_start(xacc[:], wx).then_inc(wx_in, 16)
            sp.dma_start(gact[0:1].rearrange("p g d -> p (g d)"), bl).then_inc(wx_in, 16)
            for e in range(E):
                sp.dma_start(wup_raw[:, e, :], w_up[:, e, :]).then_inc(wup_in[e // 4], 16)
            for c, (row, rows) in enumerate(CH0):
                sp.dma_start(wdown_raw[0:rows, :, c, :],
                             w_down[:, row:row + rows, :].rearrange("e p d -> p e d")).then_inc(wdown_in, 16)
            sp.wait_ge(v_mm, NB * NK0)
            sp.dma_start(l1_raw, l1w).then_inc(l1w_in, 16)
            sp.wait_ge(oq_lo_done, 3 * -(-2 * E * 2 * H3 // (3 * N)))
            sp.dma_start(w1_raw[:], w1).then_inc(w1_in, 16)
            sp.wait_ge(oq_lo_done, 3 * NB)
            sp.dma_start(w2_raw[:], w2).then_inc(w2_in, 16)
            for i in range(NB):
                sp.wait_ge(orow_done, i + 2)
                sp.dma_start(out[:, i * BS:(i + 1) * BS, :], orow).then_inc(out_done, 16)
            sp.wait_ge(out_done, 16 * NB + 1)

        @block.tensor
        def _(pe):
            pe.wait_ge(params_in, 16)
            pe.matmul(GV[0][:, 0:P], prm("W1T"), prm("condT"), start=True, stop=True).then_inc(hidden_mm, 1)
            pe.wait_ge(hidden_done, 1)
            pe.matmul(GV[1][:, 0:P], hid[:], prm("W2T"), start=True, stop=True).then_inc(gate_mm, 1)
            pe.wait_ge(consts_in, 16)
            pe.wait_ge(wr_lo_done, 1)
            for k in range(NB + 1):
                if k < NB:
                    pe.wait_ge(xn_done, k + 1)
                    need(pe, xn_lo_done, k - 1)
                    for j in range(BS):
                        m = pe.transpose(GV[2 + k % 2][:, j * P:(j + 1) * P],
                                         xnrow[:, k % 2, j * P:(j + 1) * P], ident)
                    m.then_inc(xnT_mm, 1)
                if k >= 1:
                    pe.wait_ge(xn_lo_done, k)
                    for t in range((k - 1) * BS, k * BS):
                        at, to = slice(t * P, (t + 1) * P), Z[:, t * E:(t + 1) * E]
                        pe.matmul(to, xn_hi[:, at], wr_hi[:], start=True, stop=False)
                        pe.matmul(to, xn_hi[:, at], wr_lo[:], start=False, stop=False)
                        m = pe.matmul(to, xn_lo[:, at], wr_hi[:], start=False, stop=True)
            m.then_inc(score_mm, 1)

            def product(to, a_hi, a_lo, b_hi, b_lo, start=True, stop=True):
                pe.matmul(to, a_hi, b_hi, start=start, stop=False)
                pe.matmul(to, a_hi, b_lo, start=False, stop=False)
                return pe.matmul(to, a_lo, b_hi, start=False, stop=stop)

            def up0(i, e, c):
                k = 3 * e + c
                row, rows = CH0[c]
                need(pe, h0_done, i * NK0 + k - 1)
                for bank, first, signal in ((GV[2 * (k % 2)], H0, g_mm), (GV[2 * (k % 2) + 1], 0, v_mm)):
                    at = slice(first + row, first + row + rows)
                    product(bank[0:rows, :], wu_hi[:, e, at], wu_lo[:, e, at], xn_hi[:, block_of(i)],
                            xn_lo[:, block_of(i)]).then_inc(signal, 1)

            def weigh0(m, e):
                need(pe, bc_copied, m)
                pe.matmul(BC[:, :], pick_r[:, e, :], wT[:], start=True, stop=True).then_inc(bc_mm, 1)

            def down0(m, e, c):
                rows, r = CH0[c][1], (3 * e + c) % 4
                pe.wait_ge(h0_lo_done, 3 * m + c + 1)
                if c == 0:
                    need(pe, scaled_done, m)
                product(Y[:, :], wd_hi[0:rows, e, c, :], wd_lo[0:rows, e, c, :], h0_hi[0:rows, r, :],
                        h0_lo[0:rows, r, :], start=(c == 0), stop=(c == 2)).then_inc(down_mm, 1)

            def turn_weights(done, signal, i):
                pe.wait_ge(done, i + 1)
                for j in range(BS):
                    last = pe.transpose(TP[0:2 * E, j * P:(j + 1) * P], wcur[:, j, :], ident)
                last.then_inc(signal, 1)

            def lstm_inputs(i, j):
                at = slice(j * P, (j + 1) * P)
                if j == 0:
                    pe.wait_ge(xs_lo_done, i)
                pe.wait_ge(gates_done, (i - 1) * BS + j + 1)
                pe.matmul(Z[:, :], ones_r[:], bl_hi[:], start=True, stop=False)
                pe.matmul(Z[:, :], ones_r[:], bl_lo[:], start=False, stop=False)
                product(Z[:, :], xs_hi[:, at], xs_lo[:, at], wx_hi[:], wx_lo[:], start=False, stop=False)

            def lstm_state(i, j):
                pe.wait_ge(state_done, (i - 1) * BS + j + 1)
                pe.matmul(Z[:, :], stateT[:], prm("Wh"), start=False, stop=True).then_inc(z_mm, 1)

            def turn_state(i, j):
                pe.wait_ge(state2_done, (i - 1) * BS + j + 1)
                pe.transpose(TP[:, 0:P], state2[:], ident).then_inc(h_turned, 1)

            def layer0(i, main=True, tail=True):
                for k in range(NK0):
                    e, c = k // 3, k % 3
                    if main:
                        up0(i, e, c)
                    if main if e else tail:
                        down0(i * E + e - 1, (e - 1) % E, c)
                        if c == 1:
                            if e == 1:
                                pe.wait_ge(wT_done, i + 1)
                            weigh0(i * E + e - 1, (e - 1) % E)
                    if main and k == 2:
                        need(pe, slot_done, BS * (i - 1) + 1)
                        turn_weights(wcur_done, wturned, i)
                    if main and tail and k in LSTM_AT:
                        lstm_inputs(i, LSTM_AT.index(k))
                        lstm_state(i, LSTM_AT.index(k))
                    if main and tail and k - 2 in LSTM_AT:
                        turn_state(i, LSTM_AT.index(k - 2))

            for i in range(NB):
                pe.wait_ge(wu_lo_done, E)
                pe.wait_ge(r_done, NB)
                need(pe, xT_done, i - 1)
                for j in range(BS):
                    last = pe.transpose(GV[i % 2][:, j * P:(j + 1) * P], tok[:, i * BS + j, :], ident)
                last.then_inc(x_turned, 1)
            pe.wait_ge(xT_done, NB)
            pe.wait_ge(picks_done, 1)
            pe.wait_ge(wx_lo_done, 2)
            pe.wait_ge(wh_halved, 1)
            pe.wait_ge(wu_lo_done, E)
            pe.wait_ge(wd_lo_done, 2)
            pe.wait_ge(scores_read, 1)
            layer0(0, tail=False)
            with pe.Fori(1, NB) as i:
                layer0(i)
            layer0(NB, main=False)
            lstm_inputs(NB, 0)
            for j in range(BS):
                lstm_state(NB, j)
                if j == BS - 1:
                    pe.wait_ge(l1q_done, 1)
                    for n in range(9):
                        last = pe.transpose(GV[n // 4][:, n % 4 * P:(n % 4 + 1) * P],
                                            l1_q[:, n * P:(n + 1) * P], ident)
                    last.then_inc(l1T_mm, 1)
                else:
                    lstm_inputs(NB, j + 1)
                turn_state(NB, j)

            spread = [0]

            def spread_max():
                spread[0] += 1
                n = spread[0]
                pe.wait_ge(max_col, n)
                pe.transpose(TP[0:1, 0:P], col(TMP), ident).then_inc(max_turned, 1)
                pe.wait_ge(max_row, n)
                pe.matmul(TP[:, P:P + 1], cst("ones")[0:1, :], tiny[0:1, TMP2:TMP2 + 1],
                          start=True, stop=True).then_inc(max_mm, 1)

            spread_max()

            def up_gate(i, b):
                pe.wait_ge(xq_lo_done, i + 1)
                for c in range(6):
                    need(pe, ug_copied, i * 6 + c - 5)
                    product(banks[c][:, :], l1_hi[:, c, :], l1_lo[:, c, :],
                            xq_hi[:, b, :], xq_lo[:, b, :]).then_inc(ug_mm, 1)

            pe.wait_ge(l1_lo_done, 3)
            up_gate(0, 0)
            pe.wait_ge(prep_in, 1)
            pe.matmul(Z[:, 0:P], f1[:, 0, :], f1[:, 1, :], start=True, stop=True)
            pe.transpose(Z[:, P:2 * P], f1[:, 2, :], ident).then_inc(prep_mm, 1)
            up_gate(1, 1)
            with pe.Fori(1, NB // 2) as i:
                up_gate(2 * i, 0)
                up_gate(2 * i + 1, 1)
            for _ in range(4):
                spread_max()

            def tile(bank, j):
                return bank[:, j * P:(j + 1) * P]

            def recur(i, j):
                t = i * BS + j
                if j == 0:
                    pe.wait_ge(x3T_done, i + 1)
                    pe.wait_ge(rgate_done, i * BS + 1)
                    pe.matmul(Z[:, :], prm("WzT"), xT[:, block_of(i)], start=True, stop=False,
                              skip_group_check=True)
                pe.wait_ge(rstate_done, t + 1)
                pe.matmul(tile(Z, j), prm("WhT"), hT[:, block_of(t, P)], start=False, stop=(j == 3),
                          skip_group_check=True).then_inc(rz_mm, 1)

            def logits(first, last):
                pe.wait_ge(rstate_done, last + 1)
                for t in range(first, last):
                    m = pe.matmul(TP[:, t * E:(t + 1) * E], hT[:, (t + 1) * P:(t + 2) * P], prm("WgT"),
                                  start=True, stop=True)
                m.then_inc(logit_mm, 1)

            def layer2(i, main=True, middle=True, tail=True, router=None):
                if tail:
                    recur(i - 2, 0)
                if router:
                    logits(*router[0])
                if main:
                    need(pe, x2T_done, i)
                for c in range(3):
                    if tail and c == 2:
                        recur(i - 2, 1)
                    if main:
                        pe.wait_ge(oq_lo_done, 3 * i + c + 1)
                        product(GV[0][:, :], l1_hi[:, 6 + c, :], l1_lo[:, 6 + c, :], oq_hi[:, c, :],
                                oq_lo[:, c, :], start=(c == 0), stop=(c == 2)).then_inc(o_mm, 1)
                if router and len(router) > 1:
                    logits(*router[1])
                if middle:
                    pe.wait_ge(q2_done, BS * i)
                    need(pe, qT_done, i - 1)
                    for j in range(BS):
                        last = pe.transpose(tile(GV[2], j), q2[:, j, :], ident)
                    last.then_inc(q2T_mm, 1)
                if tail:
                    recur(i - 2, 2)
                if router and len(router) > 1:
                    logits(*router[2])
                if middle:
                    pe.wait_ge(qT_done, i)
                    need(pe, f1_done, i - 1)
                    for j in range(BS):
                        last = pe.matmul(tile(GV[3], j), qT[:, j * P:(j + 1) * P], rhs_q[:], start=True, stop=True)
                    last.then_inc(acc_mm, 1)
                if main:
                    pe.wait_ge(modx_done, i + 1)
                    need(pe, norm_done, i)
                    for j in range(BS):
                        last = pe.matmul(tile(GV[1], j), modx[:, j, :], prm("l2w"), start=True, stop=True)
                    last.then_inc(l2_mm, 1)
                if tail:
                    recur(i - 2, 3)
                if middle:
                    pe.wait_ge(f1_done, i)
                    need(pe, x3T_done, i - 1)
                    for j in range(BS):
                        last = pe.transpose(tile(Y, j), f1[:, j, :], ident)
                    last.then_inc(fT_mm, 1)

            layer2(0, middle=False, tail=False)
            layer2(1, tail=False)
            with pe.Fori(2, NB) as i:
                layer2(i)
            layer2(NB, main=False, router=[(0, 8), (8, 16), (16, S - 2 * BS)])
            layer2(NB + 1, main=False, middle=False, router=[(S - 2 * BS, S - BS)])
            logits(S - BS, S)
            pe.wait_ge(counts_done, 1)
            pe.matmul(BC[:, 0:E], cst("before"), counts, start=True, stop=True).then_inc(before_mm, 1)
            def up3(i, e, c):
                k = 2 * e + c
                need(pe, h3_done, i * NK3 + k - 1)
                for bank, first, signal in ((GV[2 * (k % 2)], 0, i3_mm), (GV[2 * (k % 2) + 1], H3, g3_mm)):
                    at = slice(first + c * P, first + (c + 1) * P)
                    product(bank[:, :], w1_hi[:, e, at], w1_lo[:, e, at], hs_hi[:, block_of(i)],
                            hs_lo[:, block_of(i)]).then_inc(signal, 1)

            def weigh3(m, e):
                need(pe, bc3_copied, m)
                pe.matmul(BC[:, :], pick_r[:, e, :], wT[:], start=True, stop=True).then_inc(bc3_mm, 1)

            def down3(m, e, c):
                r = (2 * e + c) % 4
                pe.wait_ge(h3_lo_done, 2 * m + c + 1)
                if c == 0:
                    need(pe, scaled3_done, m - 1)
                product(Y3[e % 2][:, :], w2_hi[:, e, c, :], w2_lo[:, e, c, :], h3_hi[:, r, :], h3_lo[:, r, :],
                        start=(c == 0), stop=(c == 1)).then_inc(down3_mm, 1)

            def layer3(i, main=True, tail=True):
                for k in range(NK3):
                    e, c = k // 2, k % 2
                    if main:
                        up3(i, e, c)
                    if tail and k == 3:
                        pe.wait_ge(added3, E * i)
                        need(pe, wT3_done, i + 1 if main else i)
                        for j in range(BS):
                            last = pe.transpose(tile(TP, j), xacc[:, j * P:(j + 1) * P], ident)
                        last.then_inc(out_turned, 1)
                    if main if e else tail:
                        down3(i * E + e - 1, (e - 1) % E, c)
                        if c == 0:
                            if e == 1:
                                pe.wait_ge(wT3_done, i + 1)
                            weigh3(i * E + e - 1, (e - 1) % E)
                    if main and k == 1:
                        if tail:
                            need(pe, orow_done, i)
                        turn_weights(wcur3_done, wturned3, i)

            pe.wait_ge(w2_lo_done, 1)
            pe.wait_ge(w1_lo_done, E)
            pe.wait_ge(hs_lo_done, NB)
            pe.wait_ge(kept_done, 1)
            layer3(0, tail=False)
            with pe.Fori(1, NB) as i:
                layer3(i)
            layer3(NB, main=False)

        @block.scalar
        def _(act):
            act.wait_ge(params_in, 16)
            nc.scalar.mul(col(B3H), prm("b3"), 0.5).then_inc(bias_done, 1)
            act.wait_ge(hidden_mm, 1)
            nc.scalar.activation(hid[:], GV[0][:, 0:P], ACT.Silu, bias=prm("b1")).then_inc(hidden_done, 1)
            act.wait_ge(gate_pre, 1)
            nc.scalar.activation(gate1[:], gate1[:], ACT.Tanh, scale=0.5).then_inc(gate_tanh, 1)
            nc.scalar.copy(wr_hi[:], prm("wrT")).then_inc(wr_hi_done, 1)
            act.wait_ge(consts_in, 16)
            nc.scalar.copy(pick_r[:], cst("pick")[0:2 * E].unsqueeze(2).broadcast_to([2 * E, E, P]))
            nc.scalar.copy(ones_r[:], cst("ones")[0:1, :]).then_inc(picks_done, 1)
            act.wait_ge(wx_scaled, 2)
            nc.scalar.copy(wx_hi[:], xacc[:]).then_inc(wx_hi_done, 1)
            nc.scalar.copy(bl_hi[:], gact[0:1].rearrange("p g d -> p (g d)")).then_inc(wx_hi_done, 1)
            act.wait_ge(eps_set, 1)
            for k in range(NB + 1):
                if k < NB:
                    act.wait_ge(h_done, k + 1)
                    need(act, sum_done, k)
                    nc.scalar.activation(square, hrow[:, k % 2], ACT.Square).then_inc(square_done, 1)
                    act.wait_ge(sum_done, k + 1)
                    nc.scalar.activation(rowst[:, 3, k * BS:(k + 1) * BS], rowst[:, 3, k * BS:(k + 1) * BS],
                                         ACT.Sqrt, scale=1.0 / P, bias=col(EPS_RMS)).then_inc(sqrt_done, 1)
                if k >= 1:
                    act.wait_ge(xnT_mm, k)
                    nc.scalar.activation(xn_hi[:, block_of(k - 1)], GV[2 + (k - 1) % 2][:, :], ACT.Copy,
                                         scale=prm("nscale")).then_inc(xn_hi_done, 1)
                    for e in range((k - 1) * E // NB, k * E // NB):
                        act.wait_ge(wup_in[e // 4], 64)
                        nc.scalar.copy(wu_hi[:, e, :], wup_raw[:, e, :]).then_inc(wu_hi_done, 1)
            act.wait_ge(wdown_in, 48)
            nc.scalar.copy(wd_hi[:, :, 0:2, :], wdown_raw[:, :, 0:2, :]).then_inc(wd_hi_done, 1)
            nc.scalar.copy(wd_hi[0:96, :, 2, :], wdown_raw[0:96, :, 2, :]).then_inc(wd_hi_done, 1)
            act.wait_ge(centred, 1)
            nc.scalar.activation(expo[:], expo[:], ACT.Exp).then_inc(exp_done, 1)
            nc.scalar.mul(stateT[:], prm("condT"), 2.0).then_inc(state_done, 1)
            act.nop().then_inc(gates_done, 1)
            act.wait_ge(wu_lo_done, E)
            for i in range(NB):
                act.wait_ge(x_turned, i + 1)
                nc.scalar.copy(xT[:, block_of(i)], GV[i % 2][:, :]).then_inc(xT_done, 1)
            act.wait_ge(wd_lo_done, 2)

            def high0(n, k):
                rows = CH0[k % 3][1]
                act.wait_ge(h0_done, n + 1)
                return nc.scalar.copy(h0_hi[0:rows, k % 4, :], hf0[0:rows, k % 2, :]).then_inc(h0_hi_done, 1)

            def gates(i, j):
                act.wait_ge(z_mm, (i - 1) * BS + j + 1)
                nc.scalar.activation(gact[:].rearrange("p g d -> p (g d)"), Z[:, :], ACT.Tanh,
                                     scale=0.5).then_inc(gates_done, 1)

            def cell_tanh(i, j):
                t = (i - 1) * BS + j
                act.wait_ge(cell_done, t + 2)
                nc.scalar.activation(tcell[:], cell[:], ACT.Tanh, scale=0.5).then_inc(tcell_done, 1)

            def layer0(i, main=True, tail=True):
                for k in range(NK0):
                    n = i * NK0 + k
                    rows = CH0[k % 3][1]
                    if main:
                        act.wait_ge(g_mm, n + 1)
                        need(act, h0_done, n - 1)
                        nc.scalar.activation(silu0[0:rows, k % 2, :], GV[2 * (k % 2)][0:rows, :],
                                             ACT.Silu).then_inc(silu_done, 1)
                    if main if k else tail:
                        need(act, down_mm, n - 4)
                        high0(n - 1, (k - 1) % NK0)
                    if k % 3 == 1 and (main if k > 1 else tail):
                        m = i * E + k // 3 - 1
                        act.wait_ge(bc_mm, m + 1)
                        need(act, scaled_done, m)
                        nc.scalar.copy(bcast0, BC[:, :]).then_inc(bc_copied, 1)
                    if main and k == 2:
                        act.wait_ge(wturned, i + 1)
                        nc.scalar.copy(wT[:], TP[0:2 * E, :]).then_inc(wT_done, 1)
                    if tail and k == 4:
                        act.wait_ge(added, i * E)
                        nc.scalar.copy(xs_hi[:], xacc[:]).then_inc(xs_hi_done, 1)
                        nc.scalar.copy(xT[:, block_of(i - 1)], xacc[:]).then_inc(x1T_done, 1)
                    if main and tail and k in LSTM_AT:
                        gates(i, LSTM_AT.index(k))
                    if main and tail and k - 1 in LSTM_AT:
                        cell_tanh(i, LSTM_AT.index(k - 1))

            layer0(0, tail=False)
            with act.Fori(1, NB) as i:
                layer0(i)
            layer0(NB, main=False)

            for j in range(BS):
                gates(NB, j)
                cell_tanh(NB, j)
            act.wait_ge(l1T_mm, 1)
            for b in range(3):
                nc.scalar.copy(l1_hi[:, 4 * b:min(4 * b + 4, 9), :].rearrange("p n d -> p (n d)"),
                               GV[b][:, 0:min(4, 9 - 4 * b) * P]).then_inc(l1_hi_done, 1)

            act.wait_ge(factor_done, 1)

            def states(i):
                at = hT[:, bass.ds(i * N + P, N)] if not isinstance(i, int) else hT[:, P + i * N:P + (i + 1) * N]
                nc.scalar.activation(at, at, ACT.Identity, scale=col(INVX), bias=col(MAG)).then_inc(xt_done, 1)

            def keep_ug(i):
                for c in range(6):
                    act.wait_ge(ug_mm, i * 6 + c + 1)
                    to, r = (up_s, c) if c < 3 else (gate_s, c - 3)
                    at = slice((i * 3 + r) * N, (i * 3 + r + 1) * N) if isinstance(i, int) else \
                        bass.ds((i * 3 + r) * N, N)
                    nc.scalar.copy(to[:, at], banks[c][:, :]).then_inc(ug_copied, 1)

            states(0)
            states(1)
            states(2)
            act.wait_ge(prep_mm, 1)
            nc.scalar.activation(dmod[:], Z[:, 0:P], ACT.Sqrt, bias=col(EPS_L2))
            nc.scalar.copy(rhs_q[:], Z[:, P:2 * P]).then_inc(prep_act, 1)
            with act.Fori(0, NB - 3) as i:
                states(i + 3)
                keep_ug(i)
            keep_ug(NB - 3)
            keep_ug(NB - 2)
            keep_ug(NB - 1)

            def rounded(i, scale, signal):
                at = gate_s[:, block_of(i, 3 * N)]
                nc.scalar.activation(at, at, ACT.Identity, scale=col(scale), bias=col(MAG)).then_inc(signal, 1)

            def sigmoid(i, b):
                act.wait_ge(g_done, i + 1)
                need(act, gs_done, i - 1)
                nc.scalar.activation(sig_s[:, b, :], gate_s[:, block_of(i, 3 * N)],
                                     ACT.Sigmoid, scale=col(SG)).then_inc(sig_done, 1)

            act.wait_ge(factor_done, 2)
            rounded(0, KG, gt_done)
            rounded(1, KG, gt_done)
            for i in range(NB):
                if i + 2 < NB:
                    rounded(i + 2, KG, gt_done)
                sigmoid(i, i % 2)
            act.wait_ge(factor_done, 3)
            rounded(0, KGS, gst_done)
            for i in range(NB):
                if i + 1 < NB:
                    rounded(i + 1, KGS, gst_done)
                act.wait_ge(gst_done, i + 1)
                at = gate_s[:, block_of(i, 3 * N)]
                nc.scalar.activation(at, at, ACT.Identity, bias=col(NMAG)).then_inc(g2_done, 1)
            act.wait_ge(factor_done, 4)
            nc.scalar.copy(hT[:, 0:P], prm("condT")).then_inc(rstate_done, 1)
            act.nop().then_inc(rgate_done, 1)

            def recur_gate(i, j):
                t = i * BS + j
                act.wait_ge(rz_mm, t + 1)
                nc.scalar.activation(gact[:, 0, :], Z[:, j * P:(j + 1) * P], ACT.Tanh, scale=0.5,
                                     bias=col(B3H)).then_inc(rgate_done, 1)

            def recur_state(i, j):
                t = i * BS + j
                act.wait_ge(rv_done, t + 1)
                nc.scalar.activation(hT[:, block_of(t + 1, P)], uv[:, 1, :], ACT.Tanh,
                                     scale=0.5).then_inc(rstate_done, 1)

            def round_o(i, c):
                need(act, oq_lo_done, 3 * i + c - 2)
                act.nop()
                at = (i * 3 + c) * N
                at = slice(at, at + N) if isinstance(i, int) else bass.ds(at, N)
                nc.scalar.activation(o_int[:, c * N:(c + 1) * N], gate_s[:, at], ACT.Identity, scale=col(KO),
                                     bias=col(MAG)).then_inc(ot_done, 1)

            def high_o(i, c):
                act.wait_ge(ot_done, 3 * i + c + 1)
                need(act, o_mm, 3 * i + c - 2)
                nc.scalar.activation(oq_hi[:, c, :], o_int[:, c * N:(c + 1) * N], ACT.Identity,
                                     bias=col(NMAG)).then_inc(oq_hi_done, 1)

            def round_rows(i, j):
                if j == 0:
                    act.wait_ge(linv_done, i + 1)
                    need(act, q2T_mm, i)
                nc.scalar.activation(q2[:, j, :], norm2[:, j, :], ACT.Identity,
                                     scale=lsc[:, BS + j:BS + j + 1], bias=col(MAG)).then_inc(q2_done, 1)

            def turn_rows(i):
                act.wait_ge(q2T_mm, i + 1)
                nc.scalar.activation(qT[:], GV[2][:, :], ACT.Identity, bias=col(NMAG)).then_inc(qT_done, 1)

            def layer2(i, middle=True, tail=True, ahead=True):
                if middle:
                    round_rows(i - 1, 0)
                    round_rows(i - 1, 1)
                if tail:
                    recur_gate(i - 2, 0)
                if middle:
                    round_rows(i - 1, 2)
                    round_rows(i - 1, 3)
                if tail:
                    recur_state(i - 2, 0)
                if ahead:
                    round_o(i + 1, 0)
                if tail:
                    recur_gate(i - 2, 1)
                if ahead:
                    round_o(i + 1, 1)
                if tail:
                    recur_state(i - 2, 1)
                if ahead:
                    high_o(i + 1, 0)
                if tail:
                    recur_gate(i - 2, 2)
                if middle:
                    turn_rows(i - 1)
                if tail:
                    recur_state(i - 2, 2)
                if ahead:
                    round_o(i + 1, 2)
                if tail:
                    recur_gate(i - 2, 3)
                if ahead:
                    high_o(i + 1, 1)
                if tail:
                    recur_state(i - 2, 3)
                if ahead:
                    high_o(i + 1, 2)
                if tail:
                    at = slice((i - 2) * N + P, (i - 1) * N + P) if isinstance(i, int) else bass.ds((i - 2) * N + P, N)
                    act.wait_ge(rstate_done, (i - 1) * BS + 1)
                    nc.scalar.copy(hs_hi[:, block_of(i - 2)], hT[:, at]).then_inc(hs_hi_done, 1)

            for c in range(3):
                round_o(0, c)
                high_o(0, c)
            layer2(0, middle=False, tail=False)
            layer2(1, tail=False)
            with act.Fori(2, NB - 1) as i:
                layer2(i)
            layer2(NB - 1, ahead=False)
            layer2(NB, ahead=False)
            act.wait_ge(w1_in, 16)
            for j in range(BS):
                recur_gate(NB - 1, j)
                nc.scalar.copy(w1_hi[:, 2 * j, :], w1_raw[:, 2 * j, :]).then_inc(w1_hi_done, 1)
                recur_state(NB - 1, j)
                nc.scalar.copy(w1_hi[:, 2 * j + 1, :], w1_raw[:, 2 * j + 1, :]).then_inc(w1_hi_done, 1)
            act.wait_ge(w2_in, 16)
            nc.scalar.copy(w2_hi[:], w2_raw[:]).then_inc(w2_hi_done, 1)
            act.wait_ge(rstate_done, S + 1)
            nc.scalar.copy(hs_hi[:, (NB - 1) * N:], hT[:, T - N + P:T + P]).then_inc(hs_hi_done, 1)

            act.wait_ge(centred, 2)
            nc.scalar.activation(expo[:], expo[:], ACT.Exp).then_inc(exp_done, 1)
            act.nop().then_inc(out_done, 1)
            act.nop().then_inc(orow_done, 1)

            def layer3(i, main=True, tail=True):
                for k in range(NK3):
                    n = i * NK3 + k
                    if main:
                        act.wait_ge(i3_mm, n + 1)
                        need(act, h3_done, n - 1)
                        nc.scalar.activation(gelu3[:, k % 2, :], GV[2 * (k % 2)][:, :],
                                             ACT.Gelu).then_inc(gelu_done, 1)
                    if main if k else tail:
                        need(act, down3_mm, n - 4)
                        act.wait_ge(h3_done, n)
                        nc.scalar.copy(h3_hi[:, (k - 1) % 4, :], hf3[:, (k - 1) % 2, :]).then_inc(h3_hi_done, 1)
                    if k % 2 == 0 and (main if k else tail):
                        m = i * E + k // 2 - 1
                        act.wait_ge(bc3_mm, m + 1)
                        need(act, scaled3_done, m)
                        nc.scalar.copy(bcast3, BC[:, :]).then_inc(bc3_copied, 1)
                    if main and k == 1:
                        act.wait_ge(wturned3, i + 1)
                        nc.scalar.copy(wT[:], TP[0:2 * E, :]).then_inc(wT3_done, 1)
                    if tail and k == 4:
                        act.wait_ge(out_turned, i)
                        act.wait_ge(out_done, 16 * (i - 1) + 1)
                        nc.scalar.copy(orow.rearrange("p s d -> p (s d)"), TP[:, :]).then_inc(orow_done, 1)

            layer3(0, tail=False)
            with act.Fori(1, NB) as i:
                layer3(i)
            layer3(NB, main=False)

        @block.vector
        def _(dve):
            dve.memset(col(EPS_RMS), 1e-6)
            dve.memset(col(MAG), MAGIC)
            dve.memset(col(NMAG), -MAGIC)
            dve.memset(col(EPS_L2), 1e-8)
            dve.memset(cell[:], 0.0).then_inc(cell_done, 1)
            dve.wait_ge(cell_done, 1)
            dve.nop().then_inc(eps_set, 1)
            dve.nop().then_inc(slot_done, 1)
            dve.wait_ge(params_in, 16)
            dve.wait_ge(gate_mm, 1)
            dve.tensor_tensor(gate1[:], GV[1][:, 0:P], prm("b2"), ALU.add).then_inc(gate_pre, 1)
            dve.wait_ge(gate_tanh, 1)
            dve.tensor_scalar(gate1[:], gate1[:], 0.5, 1.5, ALU.mult, ALU.add).then_inc(gate_done, 1)
            dve.wait_ge(gate_done, 1)
            dve.wait_ge(wr_hi_done, 1)
            dve.tensor_tensor(wr_lo[:], prm("wrT"), wr_hi[:].bitcast(F32), ALU.subtract).then_inc(wr_lo_done, 1)
            dve.tensor_scalar(prm("Wh")[:, 0:3 * P], prm("Wh")[:, 0:3 * P], 0.5, None, ALU.mult).then_inc(wh_halved, 1)
            dve.wait_ge(wx_in, 32)
            dve.tensor_scalar(xacc[:, 3 * P:], xacc[:, 3 * P:], 2.0, None, ALU.mult).then_inc(wx_scaled, 1)
            dve.tensor_scalar(gact[0:1, 3, :], gact[0:1, 3, :], 2.0, None, ALU.mult).then_inc(wx_scaled, 1)
            dve.wait_ge(wx_hi_done, 2)
            dve.tensor_tensor(wx_lo[:], xacc[:], wx_hi[:].bitcast(F32), ALU.subtract).then_inc(wx_lo_done, 1)
            dve.tensor_tensor(bl_lo[:], gact[0:1].rearrange("p g d -> p (g d)"), bl_hi[:].bitcast(F32),
                              ALU.subtract).then_inc(wx_lo_done, 1)
            dve.wait_ge(x_in, 16)

            def gated(k):
                need(dve, r_done, k - 1)
                need(dve, xn_done, k - 1)
                dve.tensor_tensor(hrow[:, k % 2].rearrange("p (s d) -> p s d", s=BS),
                                  tok[:, k * BS:(k + 1) * BS, :], over(gate1[:], BS),
                                  ALU.mult).then_inc(h_done, 1)

            gated(0)
            for k in range(NB + 1):
                if k + 1 < NB:
                    gated(k + 1)
                if k < NB:
                    at = rowst[:, 3, k * BS:(k + 1) * BS]
                    dve.wait_ge(square_done, k + 1)
                    dve.tensor_reduce(at, square.rearrange("p (s d) -> p s d", s=BS), X,
                                      ALU.add).then_inc(sum_done, 1)
                    dve.wait_ge(sqrt_done, k + 1)
                    link(dve, dve.reciprocal(at, at))
                    need(dve, xnT_mm, k - 1)
                    dve.tensor_tensor(xnrow[:, k % 2].rearrange("p (s d) -> p s d", s=BS),
                                      hrow[:, k % 2].rearrange("p (s d) -> p s d", s=BS), wide(at, P),
                                      ALU.mult).then_inc(xn_done, 1)
                if k >= 1:
                    dve.wait_ge(xn_hi_done, k)
                    dve.scalar_tensor_tensor(
                        out=xn_lo[:, block_of(k - 1)], in0=GV[2 + (k - 1) % 2][:, :], scalar=prm("nscale"),
                        in1=xn_hi[:, block_of(k - 1)].bitcast(F32), op0=ALU.mult,
                        op1=ALU.subtract).then_inc(xn_lo_done, 1)

            def centre(first, last):
                at = slice(first, last)
                link(dve, dve.tensor_reduce(rowst[:, 0, at], scores[:, at], X, ALU.max))
                return dve.tensor_tensor(expo[:, at], scores[:, at], wide(rowst[:, 0, at], E), ALU.subtract)

            def differences(pairs_at, first, last):
                n, part = last - first, scores[:, first:last]
                link(dve, dve.tensor_tensor(pairs_at[:, first:last], part.unsqueeze(2).broadcast_to([P, n, E, E]),
                                            part.unsqueeze(3).broadcast_to([P, n, E, E]), ALU.subtract))

            def outranked(pairs_at, first, last):
                flat = pairs_at[:, first:last].rearrange("p s e f -> p s (e f)")
                link(dve, dve.tensor_tensor(flat, flat, over(cst("ties"), last - first), ALU.is_gt))

            def ranks(pairs_at, first, last):
                link(dve, dve.tensor_reduce(wsel[:, first:last], pairs_at[:, first:last], X, ALU.add))

            def weight_parts():
                link(dve, dve.tensor_copy(wround[:], wsel[:]))
                link(dve, dve.tensor_copy(wparts[:, :, 0:E], wround[:].bitcast(F32)))
                link(dve, dve.tensor_tensor(wparts[:, :, E:], wsel[:], wround[:].bitcast(F32), ALU.subtract))

            dve.wait_ge(score_mm, 1)
            steps[0] += 1
            dve.tensor_copy(scores[:].rearrange("p s e -> p (s e)"), Z[:, 0:S * E]).then_inc(dve_step, 1)
            dve.wait_ge(dve_step, steps[0])
            dve.nop().then_inc(scores_read, 1)
            dve.wait_ge(r_done, NB)
            centre(0, S).then_inc(centred, 1)
            differences(pairs, 0, S)
            outranked(pairs, 0, S)
            ranks(pairs, 0, S)
            dve.wait_ge(exp_done, 1)
            link(dve, dve.tensor_reduce(rowst[:, 1, :], expo[:], X, ALU.add))
            link(dve, dve.reciprocal(rowst[:, 2, :], rowst[:, 1, :]))
            link(dve, dve.scalar_tensor_tensor(out=wsel[:], in0=wsel[:], scalar=1.5, in1=expo[:],
                                               op0=ALU.is_lt, op1=ALU.mult))
            link(dve, dve.tensor_tensor(wsel[:], wsel[:], wide(rowst[:, 2, :], E), ALU.mult))
            weight_parts()
            dve.wait_ge(wd_lo_done, 2)
            dve.wait_ge(r_done, NB)

            def state_parts(i, j):
                t = (i - 1) * BS + j
                dve.wait_ge(gates_done, t + 2)
                dve.wait_ge(cell_done, t + 1)
                dve.scalar_tensor_tensor(out=uv[:, 0, :], in0=gact[:, 0, :], scalar=1.0, in1=gact[:, 3, :],
                                         op0=ALU.add, op1=ALU.mult).then_inc(uv_done, 1)
                dve.scalar_tensor_tensor(out=uv[:, 1, :], in0=gact[:, 1, :], scalar=1.0, in1=cell[:],
                                         op0=ALU.add, op1=ALU.mult).then_inc(uv_done, 1)
                dve.wait_ge(uv_done, 2 * t + 2)
                dve.scalar_tensor_tensor(out=cell[:], in0=uv[:, 1, :], scalar=0.5, in1=uv[:, 0, :],
                                         op0=ALU.mult, op1=ALU.add).then_inc(cell_done, 1)

            def state(i, j):
                dve.wait_ge(tcell_done, (i - 1) * BS + j + 1)
                dve.scalar_tensor_tensor(out=state2[:], in0=gact[:, 2, :], scalar=1.0, in1=tcell[:],
                                         op0=ALU.add, op1=ALU.mult).then_inc(state2_done, 1)

            def keep_state(i, j):
                t = (i - 1) * BS + j
                dve.wait_ge(h_turned, t + 1)
                dve.tensor_copy(stateT[:], TP[:, 0:P]).then_inc(state_done, 1)
                dve.tensor_copy(hT[:, block_of(t + 1, P)], TP[:, 0:P]).then_inc(slot_done, 1)

            def largest_state(i):
                at = slice((i - 1) * N + P, i * N + P) if isinstance(i, int) else bass.ds((i - 1) * N + P, N)
                dve.wait_ge(slot_done, i * BS + 1)
                dve.tensor_reduce(maxima[:, block_of(i - 1, 1)], hT[:, at], X, ALU.max,
                                  apply_absolute_value=True).then_inc(hmax_done, 1)

            def layer0(i, main=True, tail=True):
                for k in range(NK0):
                    n = i * NK0 + k
                    e, rows = k // 3, CH0[k % 3][1]
                    if main:
                        dve.wait_ge(v_mm, n + 1)
                        dve.wait_ge(silu_done, n + 1)
                        need(dve, h0_lo_done, n - 1)
                        dve.tensor_tensor(hf0[0:rows, k % 2, :], GV[2 * (k % 2) + 1][0:rows, :],
                                          silu0[0:rows, k % 2, :], ALU.mult).then_inc(h0_done, 1)
                    if k % 3 == 2 and (main if e else tail):
                        m, f = i * E + e - 1, (e - 1) % E
                        at = block_of(i)
                        dve.wait_ge(down_mm, 3 * m + 3)
                        dve.wait_ge(bc_copied, m + 1)
                        need(dve, added, m)
                        dve.tensor_tensor(scaled0, Y[:, :], bcast0, ALU.mult).then_inc(scaled_done, 1)
                        if f == 0:
                            dve.wait_ge(scaled_done, m + 1)
                            need(dve, x1T_done, i)
                            need(dve, xs_lo_done, i)
                            dve.tensor_tensor(xacc[:], xT[:, at], scaled0, ALU.add).then_inc(added, 1)
                    if main and k == 1:
                        need(dve, wturned, i)
                        dve.tensor_copy(wcur[:], wparts[:, steps_of(i), :]).then_inc(wcur_done, 1)
                    if main and tail and k in LSTM_AT:
                        state_parts(i, LSTM_AT.index(k))
                    if main and tail and k - 1 in LSTM_AT:
                        state(i, LSTM_AT.index(k - 1))
                    if main and tail and k - 2 in LSTM_AT:
                        keep_state(i, LSTM_AT.index(k - 2))
                    if main and tail and k == 22:
                        largest_state(i)

            layer0(0, tail=False)
            with dve.Fori(1, NB) as i:
                layer0(i)
            layer0(NB, main=False)

            raw = l1_raw.rearrange("p (g k) -> p g k", k=32)
            qv = l1_q.rearrange("p (g k) -> p g k", k=32)
            dve.wait_ge(l1w_in, 16)
            link(dve, dve.tensor_reduce(wscale[:, 0, :], raw, X, ALU.max, apply_absolute_value=True))
            link(dve, dve.tensor_scalar(wscale[:, 0, :], wscale[:, 0, :], 1.0 / 7.0, TINY, ALU.mult, ALU.max))
            link(dve, dve.reciprocal(wscale[:, 1, :], wscale[:, 0, :]))
            for j in range(BS):
                state_parts(NB, j)
                state(NB, j)
                keep_state(NB, j)
                if j == 0:
                    link(dve, dve.tensor_tensor(qv, raw, wide(wscale[:, 1, :], 32), ALU.mult))
                    link(dve, dve.tensor_scalar(l1_q, l1_q, MAGIC, MAGIC, ALU.add, ALU.subtract))
                if j == 1:
                    dve.tensor_tensor(qv, qv, wide(wscale[:, 0, :], 32), ALU.mult).then_inc(l1q_done, 1)
                if j == 2:
                    link(dve, dve.tensor_scalar(ysT[:], prm("condT"), P ** -0.5, None, ALU.mult))
                    link(dve, dve.tensor_tensor(f1[:, 0, :], ysT[:], ysT[:], ALU.mult))
                    link(dve, dve.tensor_tensor(f1[:, 1, :], prm("l2w"), prm("l2w"), ALU.mult))
            largest_state(NB)
            for b in range(3):
                dve.wait_ge(l1_hi_done, b + 1)
                at = slice(4 * b, min(4 * b + 4, 9))
                dve.tensor_tensor(l1_lo[:, at, :].rearrange("p n d -> p (n d)"), GV[b][:, 0:min(4, 9 - 4 * b) * P],
                                  l1_hi[:, at, :].rearrange("p n d -> p (n d)").bitcast(F32),
                                  ALU.subtract).then_inc(l1_lo_done, 1)

            counted = [0]

            def whole_max(columns_at):
                counted[0] += 1
                n = counted[0]
                dve.tensor_reduce(col(TMP), columns_at, X, ALU.max).then_inc(max_col, 1)
                dve.wait_ge(max_turned, n)
                dve.tensor_reduce(tiny[0:1, TMP2:TMP2 + 1], TP[0:1, 0:P], X, ALU.max).then_inc(max_row, 1)
                dve.wait_ge(max_mm, n)
                return TP[:, P:P + 1]

            dve.wait_ge(hmax_done, NB)
            m = whole_max(maxima[:, 0:NB])
            link(dve, dve.tensor_scalar(col(SX), m, 0.5 / Q16, TINY, ALU.mult, ALU.max))
            link(dve, dve.reciprocal(col(TMP), col(SX)))
            dve.tensor_scalar(col(INVX), col(TMP), 0.5, None, ALU.mult).then_inc(factor_done, 1)
            dve.wait_ge(factor_done, 1)

            def parts_of_x(i, b):
                at = slice(i * N + P, (i + 1) * N + P) if isinstance(i, int) else bass.ds(i * N + P, N)
                dve.wait_ge(xt_done, i + 1)
                need(dve, ug_mm, i * 6 - 6)
                dve.tensor_scalar(xq_hi[:, b, :], hT[:, at], MAGIC, None, ALU.subtract).then_inc(xq_hi_done, 1)
                dve.wait_ge(xq_hi_done, i + 1)
                dve.scalar_tensor_tensor(out=xq_lo[:, b, :], in0=hT[:, at], scalar=MAGIC,
                                         in1=xq_hi[:, b, :].bitcast(F32), op0=ALU.subtract,
                                         op1=ALU.subtract).then_inc(xq_lo_done, 1)

            def maximum_of(i, r, rows):
                at = slice(r * NB + i, r * NB + i + 1) if isinstance(i, int) else bass.ds(i + r * NB, 1)
                dve.wait_ge(ug_copied, i * 6 + 3 * r + 3)
                dve.tensor_reduce(maxima[:, at], rows[:, block_of(i, 3 * N)], X, ALU.max,
                                  apply_absolute_value=True).then_inc(ug_max, 1)

            def block_b(i, b, ahead=True):
                maximum_of(i, 0, up_s)
                if ahead:
                    parts_of_x(i + 2, b)
                maximum_of(i, 1, gate_s)

            parts_of_x(0, 0)
            parts_of_x(1, 1)
            link(dve, dve.tensor_reduce(col(TMP), prm("rhsT"), X, ALU.max, apply_absolute_value=True))
            link(dve, dve.tensor_scalar(col(RSC), col(TMP), TINY, 1.0 / 127.0, ALU.max, ALU.mult))
            link(dve, dve.reciprocal(col(TMP), col(RSC)))
            link(dve, dve.tensor_scalar(f1[:, 2, :], prm("rhsT"), col(TMP), MAGIC, ALU.mult, ALU.add))
            dve.tensor_scalar(f1[:, 2, :], f1[:, 2, :], MAGIC, None, ALU.subtract).then_inc(prep_in, 1)
            link(dve, dve.tensor_scalar(col(LEAK2), prm("alpha"), -2.0, 2.0, ALU.mult, ALU.add))
            with dve.Fori(0, NB // 2 - 1) as i:
                block_b(2 * i, 0)
                block_b(2 * i + 1, 1)
            block_b(NB - 2, 0, ahead=False)
            block_b(NB - 1, 1, ahead=False)
            dve.wait_ge(prep_act, 1)
            link(dve, dve.reciprocal(dmod[:], dmod[:]))
            dve.wait_ge(ug_max, 2 * NB)
            for at, scale, factor in ((slice(0, NB), SU, KU), (slice(NB, 2 * NB), SG, KG)):
                m = whole_max(maxima[:, at])
                link(dve, dve.tensor_scalar(col(TMP), m, col(SX), 1.0 / Q16, ALU.mult, ALU.mult))
                link(dve, dve.tensor_scalar(col(scale), col(TMP), TINY, None, ALU.max))
                link(dve, dve.reciprocal(col(TMP), col(scale)))
                link(dve, dve.tensor_scalar(col(factor), col(TMP), col(SX), None, ALU.mult))
            dve.nop().then_inc(factor_done, 1)

            def round_sig(i, b):
                dve.wait_ge(sig_done, i + 1)
                dve.tensor_scalar(sig_s[:, b, :], sig_s[:, b, :], 65535.0 / 65536.0, MAGIC16, ALU.min,
                                  ALU.add).then_inc(sig_rounded, 1)

            def gated_sig(i, b, ahead=True):
                at = gate_s[:, block_of(i, 3 * N)]
                dve.wait_ge(sig_rounded, i + 1)
                dve.scalar_tensor_tensor(out=at, in0=sig_s[:, b, :], scalar=MAGIC16, in1=at,
                                         op0=ALU.subtract, op1=ALU.mult).then_inc(gs_done, 1)
                if ahead:
                    round_sig(i + 1, 1 - b)
                dve.wait_ge(gs_done, i + 1)
                dve.tensor_reduce(maxima[:, block_of(i, 1)], at, X, ALU.max,
                                  apply_absolute_value=True).then_inc(gs_max, 1)

            round_sig(0, 0)
            gated_sig(0, 0)
            with dve.Fori(1, NB // 2) as i:
                gated_sig(2 * i - 1, 1)
                gated_sig(2 * i, 0)
            gated_sig(NB - 1, 1, ahead=False)
            dve.wait_ge(gs_max, NB)
            m = whole_max(maxima[:, 0:NB])
            link(dve, dve.tensor_scalar(col(TMP), m, col(SG), 1.0 / Q16, ALU.mult, ALU.mult))
            link(dve, dve.tensor_scalar(col(SGS), col(TMP), TINY, None, ALU.max))
            link(dve, dve.reciprocal(col(TMP), col(SGS)))
            link(dve, dve.tensor_scalar(col(KGS), col(TMP), col(SG), None, ALU.mult))
            dve.nop().then_inc(factor_done, 1)

            def outer(i):
                at, ups = gate_s[:, block_of(i, 3 * N)], up_s[:, block_of(i, 3 * N)]
                dve.wait_ge(g2_done, i + 1)
                dve.wait_ge(ut_done, i + 1)
                dve.scalar_tensor_tensor(out=at, in0=ups, scalar=MAGIC, in1=at, op0=ALU.subtract,
                                         op1=ALU.mult).then_inc(o_done, 1)

            def largest_o(i):
                dve.wait_ge(o_done, i + 1)
                dve.tensor_reduce(maxima[:, block_of(i, 1)], gate_s[:, block_of(i, 3 * N)], X, ALU.max,
                                  apply_absolute_value=True).then_inc(o_max, 1)

            outer(0)
            with dve.Fori(0, NB - 1) as i:
                outer(i + 1)
                largest_o(i)
            largest_o(NB - 1)
            dve.wait_ge(o_max, NB)
            m = whole_max(maxima[:, 0:NB])
            link(dve, dve.tensor_scalar(col(SGS), col(SGS), col(SU), None, ALU.mult))
            link(dve, dve.tensor_scalar(col(TMP), m, col(SGS), 1.0 / Q16, ALU.mult, ALU.mult))
            link(dve, dve.tensor_scalar(col(SO), col(TMP), TINY, None, ALU.max))
            link(dve, dve.reciprocal(col(TMP), col(SO)))
            dve.tensor_scalar(col(KO), col(TMP), col(SGS), None, ALU.mult).then_inc(factor_done, 1)
            dve.wait_ge(factor_done, 4)

            def recur(i, j):
                t = i * BS + j
                dve.wait_ge(rgate_done, t + 2)
                dve.scalar_tensor_tensor(out=uv[:, 0, :], in0=gact[:, 0, :], scalar=1.0,
                                         in1=xT[:, block_of(t, P)], op0=ALU.add,
                                         op1=ALU.mult).then_inc(ru_done, 1)
                dve.wait_ge(ru_done, t + 1)
                dve.scalar_tensor_tensor(out=uv[:, 1, :], in0=hT[:, block_of(t, P)], scalar=col(LEAK2),
                                         in1=uv[:, 0, :], op0=ALU.mult, op1=ALU.add).then_inc(rv_done, 1)

            def grid(ap):
                return ap.rearrange("p (s d) -> p s d", s=BS)

            def low_o(i, c):
                dve.wait_ge(oq_hi_done, 3 * i + c + 1)
                dve.scalar_tensor_tensor(out=oq_lo[:, c, :], in0=o_int[:, c * N:(c + 1) * N], scalar=MAGIC,
                                         in1=oq_hi[:, c, :].bitcast(F32), op0=ALU.subtract,
                                         op1=ALU.subtract).then_inc(oq_lo_done, 1)

            def modulate(i):
                xb = xT[:, block_of(i)]
                dve.wait_ge(o_mm, 3 * i + 3)
                dve.scalar_tensor_tensor(out=xb, in0=GV[0][:, :], scalar=col(SO), in1=xb, op0=ALU.mult,
                                         op1=ALU.add).then_inc(x2T_done, 1)
                dve.wait_ge(x2T_done, i + 1)
                need(dve, l2_mm, i)
                dve.tensor_tensor(modx[:], grid(xb), over(ysT[:], BS), ALU.mult).then_inc(modx_done, 1)

            def scale_rows(i):
                dve.wait_ge(acc_mm, i + 1)
                need(dve, fT_mm, i)
                dve.tensor_tensor(f1[:], grid(GV[3][:, :]), wide(lsc[:, 0:BS], P), ALU.mult).then_inc(f1_done, 1)

            def finish_x3(i):
                xb = xT[:, block_of(i)]
                dve.wait_ge(fT_mm, i + 1)
                dve.scalar_tensor_tensor(out=xb, in0=Y[:, :], scalar=col(RSC), in1=xb, op0=ALU.mult,
                                         op1=ALU.add).then_inc(x3T_done, 1)

            def demodulate(i, middle):
                dve.wait_ge(l2_mm, i + 1)
                need(dve, q2_done, BS * i)
                if middle:
                    dve.wait_ge(f1_done, i)
                dve.tensor_tensor(norm2[:], grid(GV[1][:, :]), over(dmod[:], BS), ALU.mult).then_inc(norm_done, 1)
                dve.wait_ge(norm_done, i + 1)
                dve.tensor_reduce(lsc[:, 0:BS], norm2[:], X, ALU.max,
                                  apply_absolute_value=True).then_inc(nmax_done, 1)
                dve.wait_ge(nmax_done, i + 1)
                dve.tensor_scalar(lsc[:, 0:BS], lsc[:, 0:BS], TINY, 1.0 / 127.0, ALU.max,
                                  ALU.mult).then_inc(lscale_done, 1)
                dve.wait_ge(lscale_done, i + 1)
                dve.reciprocal(lsc[:, BS:2 * BS], lsc[:, 0:BS]).then_inc(linv_done, 1)

            def layer2(i, main=True, middle=True, tail=True, ahead=True):
                if tail:
                    recur(i - 2, 0)
                    recur(i - 2, 1)
                if main:
                    modulate(i)
                if tail:
                    recur(i - 2, 2)
                if middle:
                    scale_rows(i - 1)
                if ahead:
                    low_o(i + 1, 0)
                if tail:
                    recur(i - 2, 3)
                if middle:
                    finish_x3(i - 1)
                if main:
                    demodulate(i, middle)
                if ahead:
                    low_o(i + 1, 1)
                    low_o(i + 1, 2)

            for c in range(3):
                low_o(0, c)
            layer2(0, middle=False, tail=False)
            layer2(1, tail=False)
            with dve.Fori(2, NB - 1) as i:
                layer2(i)
            layer2(NB - 1, ahead=False)
            layer2(NB, main=False, ahead=False)
            recur(NB - 1, 0)
            dve.wait_ge(logit_mm, 4)
            first = S - BS
            link(dve, dve.tensor_copy(scores[:, 0:first].rearrange("p s e -> p (s e)"), TP[:, 0:first * E]))
            centre(0, first)
            differences(pairs3[:], 0, first)
            recur(NB - 1, 1)
            outranked(pairs3[:], 0, first)
            recur(NB - 1, 2)
            ranks(pairs3[:], 0, first)
            recur(NB - 1, 3)
            dve.wait_ge(logit_mm, 5)
            link(dve, dve.tensor_copy(scores[:, first:].rearrange("p s e -> p (s e)"), TP[:, first * E:S * E]))
            centre(first, S).then_inc(centred, 1)
            differences(pairs3[:], first, S)
            outranked(pairs3[:], first, S)
            ranks(pairs3[:], first, S)
            turned_sel = sel.rearrange("p e s -> p s e")
            link(dve, dve.tensor_scalar(turned_sel, wsel[:], 1.5, None, ALU.is_lt))
            link(dve, dve.tensor_tensor_scan(place.rearrange("p e s -> p (e s)"), cst("rows"),
                                             sel.rearrange("p e s -> p (e s)"), 0.0, ALU.mult, ALU.add))
            dve.tensor_copy(counts, place[:, :, S - 1]).then_inc(counts_done, 1)
            dve.wait_ge(exp_done, 2)
            link(dve, dve.tensor_tensor(wsel[:], turned_sel, expo[:], ALU.mult))
            link(dve, dve.tensor_reduce(rowst[:, 1, :], wsel[:], X, ALU.add))
            link(dve, dve.reciprocal(rowst[:, 2, :], rowst[:, 1, :]))
            link(dve, dve.tensor_tensor(wsel[:], wsel[:], wide(rowst[:, 2, :], E), ALU.mult))
            dve.wait_ge(before_mm, 1)
            link(dve, dve.tensor_tensor(place, place, wide(BC[:, 0:E], S), ALU.add))
            link(dve, dve.scalar_tensor_tensor(out=wsel[:], in0=place.rearrange("p e s -> p s e"),
                                               scalar=float(CAP), in1=wsel[:], op0=ALU.is_le, op1=ALU.mult))
            weight_parts()
            dve.nop().then_inc(kept_done, 1)
            dve.wait_ge(w2_lo_done, 1)

            def layer3(i, main=True, tail=True):
                for k in range(NK3):
                    n, e = i * NK3 + k, k // 2
                    if main:
                        dve.wait_ge(g3_mm, n + 1)
                        dve.wait_ge(gelu_done, n + 1)
                        need(dve, h3_lo_done, n - 1)
                        dve.tensor_tensor(hf3[:, k % 2, :], GV[2 * (k % 2) + 1][:, :], gelu3[:, k % 2, :],
                                          ALU.mult).then_inc(h3_done, 1)
                    if main if k else tail:
                        dve.wait_ge(h3_hi_done, n)
                        need(dve, down3_mm, n - 4)
                        dve.tensor_tensor(h3_lo[:, (k - 1) % 4, :], hf3[:, (k - 1) % 2, :],
                                          h3_hi[:, (k - 1) % 4, :].bitcast(F32),
                                          ALU.subtract).then_inc(h3_lo_done, 1)
                    if k % 2 == 1 and (main if e else tail):
                        m, f = i * E + e - 1, (e - 1) % E
                        at = block_of(i)
                        dve.wait_ge(down3_mm, 2 * m + 2)
                        dve.wait_ge(bc3_copied, m + 1)
                        need(dve, added3, m)
                        dve.tensor_tensor(scaled3, Y3[f % 2][:, :], bcast3, ALU.mult).then_inc(scaled3_done, 1)
                        if f == 0:
                            dve.wait_ge(scaled3_done, m + 1)
                            need(dve, out_turned, i)
                            dve.tensor_tensor(xacc[:], xT[:, at], scaled3, ALU.add).then_inc(added3, 1)
                    if main and k == 0:
                        need(dve, wturned3, i)
                        dve.tensor_copy(wcur[:], wparts[:, steps_of(i), :]).then_inc(wcur3_done, 1)

            layer3(0, tail=False)
            with dve.Fori(1, NB) as i:
                layer3(i)
            layer3(NB, main=False)

        @block.gpsimd
        def _(pool):
            def low_up(e):
                pool.wait_ge(wu_hi_done, e + 1)
                nc.gpsimd.tensor_tensor(wu_lo[:, e, :], wup_raw[:, e, :], wu_hi[:, e, :].bitcast(F32),
                                        ALU.subtract).then_inc(wu_lo_done, 1)

            for k in range(NB):
                pool.wait_ge(h_done, k + 1)
                rows = tok[:, k * BS:(k + 1) * BS, :]
                nc.gpsimd.tensor_tensor(rows, rows, hrow[:, k % 2].rearrange("p (s d) -> p s d", s=BS),
                                        ALU.add).then_inc(r_done, 1)
                if k >= 2:
                    low_up(k - 2)
            for e in range(NB - 2, E):
                low_up(e)
            pool.wait_ge(wd_hi_done, 2)
            nc.gpsimd.tensor_tensor(wd_lo[:, :, 0:2, :], wdown_raw[:, :, 0:2, :],
                                    wd_hi[:, :, 0:2, :].bitcast(F32), ALU.subtract).then_inc(wd_lo_done, 1)
            nc.gpsimd.tensor_tensor(wd_lo[0:96, :, 2, :], wdown_raw[0:96, :, 2, :],
                                    wd_hi[0:96, :, 2, :].bitcast(F32), ALU.subtract).then_inc(wd_lo_done, 1)

            def low0(n, k):
                rows = CH0[k % 3][1]
                pool.wait_ge(h0_hi_done, n + 1)
                nc.gpsimd.tensor_tensor(h0_lo[0:rows, k % 4, :], hf0[0:rows, k % 2, :],
                                        h0_hi[0:rows, k % 4, :].bitcast(F32), ALU.subtract).then_inc(h0_lo_done, 1)

            def add0(m, f):
                pool.wait_ge(scaled_done, m + 1)
                pool.wait_ge(added, m)
                nc.gpsimd.tensor_tensor(xacc[:], xacc[:], scaled0, ALU.add).then_inc(added, 1)

            def layer0(i, main=True, tail=True):
                for k in range(NK0):
                    e = k // 3
                    if main if k else tail:
                        low0(i * NK0 + k - 1, (k - 1) % NK0)
                    if k % 3 == 2 and e != 1 and (main if e else tail):
                        add0(i * E + e - 1, (e - 1) % E)
                    if tail and k == 4:
                        pool.wait_ge(xs_hi_done, i)
                        nc.gpsimd.tensor_tensor(xs_lo[:], xacc[:], xs_hi[:].bitcast(F32),
                                                ALU.subtract).then_inc(xs_lo_done, 1)

            layer0(0, tail=False)
            with pool.Fori(1, NB) as i:
                layer0(i)
            layer0(NB, main=False)

            pool.wait_ge(factor_done, 2)
            for i in range(NB):
                at = gate_s[:, block_of(i, 3 * N)]
                pool.wait_ge(gt_done, i + 1)
                nc.gpsimd.tensor_scalar(at, at, 1.0, -MAGIC, ALU.mult, ALU.add).then_inc(g_done, 1)
            for i in range(NB):
                at = up_s[:, block_of(i, 3 * N)]
                nc.gpsimd.tensor_scalar(at, at, col(KU), MAGIC, ALU.mult, ALU.add).then_inc(ut_done, 1)

            def low3(i):
                pool.wait_ge(hs_hi_done, i + 1)
                at = slice(i * N + P, (i + 1) * N + P) if isinstance(i, int) else bass.ds(i * N + P, N)
                nc.gpsimd.tensor_tensor(hs_lo[:, block_of(i)], hT[:, at], hs_hi[:, block_of(i)].bitcast(F32),
                                        ALU.subtract).then_inc(hs_lo_done, 1)

            low3(0)
            with pool.Fori(1, NB - 1) as i:
                low3(i)
            for e in range(E):
                pool.wait_ge(w1_hi_done, e + 1)
                nc.gpsimd.tensor_tensor(w1_lo[:, e, :], w1_raw[:, e, :], w1_hi[:, e, :].bitcast(F32),
                                        ALU.subtract).then_inc(w1_lo_done, 1)
            pool.wait_ge(w2_hi_done, 1)
            nc.gpsimd.tensor_tensor(w2_lo[:], w2_raw[:], w2_hi[:].bitcast(F32), ALU.subtract).then_inc(w2_lo_done, 1)
            low3(NB - 1)

            def layer3(i, main=True, tail=True):
                for k in range(NK3):
                    e = k // 2
                    if k % 2 == 1 and e != 1 and (main if e else tail):
                        m, f = i * E + e - 1, (e - 1) % E
                        pool.wait_ge(scaled3_done, m + 1)
                        pool.wait_ge(added3, m)
                        nc.gpsimd.tensor_tensor(xacc[:], xacc[:], scaled3, ALU.add).then_inc(added3, 1)

            layer3(0, tail=False)
            with pool.Fori(1, NB) as i:
                layer3(i)
            layer3(NB, main=False)


def kernel(**inputs):
    import numpy as np
    import concourse.bacc as bacc
    from concourse.bass_utils import run_bass_kernel_spmd

    a = {k: np.asarray(v) for k, v in inputs.items()}
    cond = a["cond_1024"]
    L3W = a["L3_cond_W"]
    parts = {
        "condT": cond.T, "W1T": a["L0_cond_W1"].T, "W2T": a["L0_cond_W2"].T,
        "b2": np.broadcast_to(a["L0_cond_b2"], (P, P)), "l2w": a["L2_cond_weight"], "rhsT": a["L2_ffn_rhs"].T,
        "WhT": L3W[:, :P].T, "WzT": L3W[:, P:].T, "Wh": a["L1_cond_Wh"],
        "wrT": a["L0_ffn_w_router"].T, "WgT": a["L3_ffn_Wg"].T,
        "b1": a["L0_cond_b1"][:, None], "nscale": a["L0_ffn_norm_scale"][:, None],
        "b3": a["L3_cond_b"][:, None], "alpha": a["L3_cond_alpha"][:, None]}
    ties = np.where(np.arange(E)[None, :] < np.arange(E)[:, None], -1.2e-38, 0.0)
    fixed = {
        "ident": np.eye(P), "before": np.triu(np.ones((P, P)), 1),
        "ties": np.broadcast_to(ties.reshape(1, -1), (P, E * E)),
        "rows": np.broadcast_to((np.arange(S * E) % S > 0)[None, :], (P, S * E)), "ones": np.ones((P, P)),
        "pick": (np.arange(P)[:, None] % E == np.arange(E)[None, :])}
    arrays = {
        "x": a["x"],
        "params": np.concatenate([parts[n] for n, _ in PARAMS], axis=1),
        "consts": np.concatenate([fixed[n] for n, _ in CONSTS], axis=1).astype(np.float32),
        "wx": a["L1_cond_Wx"], "bl": a["L1_cond_b"][None, :],
        "w_up": a["L0_ffn_w_up"].transpose(2, 0, 1),
        "w_down": a["L0_ffn_w_down"].transpose(0, 2, 1),
        "l1w": np.concatenate([a["L1_ffn_w_up"].reshape(3, P, P).transpose(1, 0, 2).reshape(P, H1),
                               a["L1_ffn_w_gate"].reshape(3, P, P).transpose(1, 0, 2).reshape(P, H1),
                               a["L1_ffn_w_down"]], axis=1),
        "w1": a["L3_ffn_W1"].transpose(1, 0, 2),
        "w2": a["L3_ffn_W2"].reshape(E, 2, P, P).transpose(2, 0, 1, 3)}
    nc = bacc.Bacc("TRN2", target_bir_lowering=False, num_devices=1)
    args = []
    for name in arrays:
        arrays[name] = np.ascontiguousarray(arrays[name])
        args.append(nc.dram_tensor(f"in_{name}", arrays[name].shape, F32, kind="ExternalInput").ap())
    args.append(nc.dram_tensor("out", (P, S, P), F32, kind="ExternalOutput").ap())
    mixer_kernel(nc, *args)
    r = run_bass_kernel_spmd(nc, [{f"in_{n}": v for n, v in arrays.items()}], core_ids=[0])
    return r.results[0]["out"]
```
